# Optimizing a Trainium2 kernel written in Bass

```python
import numpy as np
import jax
import jax.numpy as jnp

def _softmax(x, axis=-1):
    return jax.nn.softmax(x, axis=axis)

def _gelu(x):
    return jax.nn.gelu(x, approximate=True)

def _silu(x):
    return jax.nn.silu(x)

def _sigmoid(x):
    return jax.nn.sigmoid(x)

def _layernorm(x, axis=-1, eps=1e-05):
    m = jnp.mean(x, axis=axis, keepdims=True)
    v = jnp.var(x, axis=axis, keepdims=True)
    return (x - m) / jnp.sqrt(v + eps)

def _scatter_add(tgt, idx, src, axis=0):
    return tgt.at[idx].add(src)

def _segment_sum(src, seg, n):
    return jax.ops.segment_sum(src, seg, n)
kernel_name = 'mk_gnn_resnorm_d1_gnn_r32_3bf533'

def setup_inputs(seed: int=0):
    np.random.seed(seed)
    _w = jnp.asarray

    def _rec_inputs():
        import jax
        import jax.numpy as jnp
        _gk = jax.random.key(seed)
        x = -0.000202 + 1 * jax.random.normal(jax.random.fold_in(_gk, 1), (3125, 128), jnp.float32)
        src = jax.random.randint(jax.random.fold_in(_gk, 2), (100000,), 0, 3125, jnp.int32)
        dst = jnp.minimum((3125 * jax.random.uniform(jax.random.fold_in(_gk, 3), (100000,)) ** 2.0).astype(jnp.int32), 99999)
        _o = jnp.argsort(dst, stable=True)
        src = src[_o]
        dst = dst[_o]
        edge_type_8 = jax.random.randint(jax.random.fold_in(_gk, 12), (100000,), 0, 8, jnp.int32)
        node_type_8 = jax.random.randint(jax.random.fold_in(_gk, 13), (3125,), 0, 8, jnp.int32)
        return (x, src, dst, edge_type_8, node_type_8)
    x, src, dst, edge_type_8, node_type_8 = _rec_inputs()

    def _L0_gnn_setup():
        import jax, jax.numpy as jnp
        import numpy as np
        N = 50000
        E = 12500
        HID = 128
        H = 8
        HS = HID // H
        TN = 8
        R = 8
        L = 2
        OUT = 128
        EPS = 1e-05
        SQRT_D = float(np.sqrt(HS))

        def typed_linear(x, types, W):
            out = jnp.zeros((x.shape[0], W.shape[-1]), x.dtype)
            for t in range(W.shape[0]):
                out = out + jnp.where((types == t)[:, None], x @ W[t], 0.0)
            return out

        def rel_apply(h, etype, W):
            out = jnp.zeros_like(h)
            for r in range(W.shape[1]):
                out = out + jnp.where((etype == r)[:, None, None], jnp.einsum('ehi,hio->eho', h, W[:, r]), 0.0)
            return out

        def gt_layer(x, src, dst, ntype, etype, Wk, Wq, Wv, Wa, pri, Watt, Wmsg, skip, g, b):
            n = x.shape[0]
            k = typed_linear(x, ntype, Wk).reshape(n, H, HS)
            q = typed_linear(x, ntype, Wq).reshape(n, H, HS)
            v = typed_linear(x, ntype, Wv).reshape(n, H, HS)
            k_j, q_i, v_j = (k[src], q[dst], v[src])
            kw = rel_apply(k_j, etype, Watt)
            a = (kw * q_i).sum(-1) * pri[:, etype].T / SQRT_D
            amax = jax.ops.segment_max(a, dst, num_segments=n)
            ex = jnp.exp(a - amax[dst])
            den = jax.ops.segment_sum(ex, dst, num_segments=n)
            alpha = ex / (den[dst] + 1e-16)
            m = rel_apply(v_j, etype, Wmsg)
            agg = jax.ops.segment_sum(alpha[..., None] * m, dst, num_segments=n)
            out = jax.nn.silu(typed_linear(agg.reshape(n, HID), ntype, Wa))
            al = jax.nn.sigmoid(skip[ntype])[:, None]
            out = out * al + x * (1.0 - al)
            mu = out.mean(-1, keepdims=True)
            var = ((out - mu) ** 2).mean(-1, keepdims=True)
            return (out - mu) / jnp.sqrt(var + EPS) * g + b
        key = jax.random.key(seed)
        ks = jax.random.split(key, 12)
        s = 1.0 / np.sqrt(HID)
        sh = 1.0 / np.sqrt(HS)
        return {'x': jax.random.normal(ks[0], (N, HID), jnp.float32), 'edge_index': jax.random.randint(ks[1], (2, E), 0, N, dtype=jnp.int32), 'ntype': jax.random.randint(ks[2], (N,), 0, TN, dtype=jnp.int32), 'etype': jax.random.randint(ks[3], (E,), 0, R, dtype=jnp.int32), 'Wk': jax.random.normal(ks[4], (L, TN, HID, HID), jnp.float32) * s, 'Wq': jax.random.normal(ks[5], (L, TN, HID, HID), jnp.float32) * s, 'Wv': jax.random.normal(ks[6], (L, TN, HID, HID), jnp.float32) * s, 'Wa': jax.random.normal(ks[7], (L, TN, HID, HID), jnp.float32) * s, 'pri': jnp.ones((L, H, R), jnp.float32), 'Watt': jax.random.normal(ks[8], (L, H, R, HS, HS), jnp.float32) * sh, 'Wmsg': jax.random.normal(ks[9], (L, H, R, HS, HS), jnp.float32) * sh, 'skip': jnp.ones((L, TN), jnp.float32), 'ln_g': jnp.ones((L, HID), jnp.float32), 'ln_b': jnp.zeros((L, HID), jnp.float32), 'Wff': jax.random.normal(ks[10], (HID, OUT), jnp.float32) * s, 'bff': jnp.zeros((OUT,), jnp.float32)}
    _L0_gnn_all = _L0_gnn_setup()
    _L0_gnn_in = {k: v for k, v in _L0_gnn_all.items() if k in ('Wk', 'Wq', 'Wv', 'Wa', 'pri', 'Watt', 'Wmsg', 'skip', 'ln_g', 'ln_b', 'Wff', 'bff')}
    del _L0_gnn_all
    return {'x': x, 'src': src, 'dst': dst, 'edge_type_8': edge_type_8, 'node_type_8': node_type_8, 'L0_gnn_Wk': _L0_gnn_in['Wk'], 'L0_gnn_Wq': _L0_gnn_in['Wq'], 'L0_gnn_Wv': _L0_gnn_in['Wv'], 'L0_gnn_Wa': _L0_gnn_in['Wa'], 'L0_gnn_pri': _L0_gnn_in['pri'], 'L0_gnn_Watt': _L0_gnn_in['Watt'], 'L0_gnn_Wmsg': _L0_gnn_in['Wmsg'], 'L0_gnn_skip': _L0_gnn_in['skip'], 'L0_gnn_ln_g': _L0_gnn_in['ln_g'], 'L0_gnn_ln_b': _L0_gnn_in['ln_b'], 'L0_gnn_Wff': _L0_gnn_in['Wff'], 'L0_gnn_bff': _L0_gnn_in['bff']}

def reference(x, src, dst, edge_type_8, node_type_8, L0_gnn_Wk, L0_gnn_Wq, L0_gnn_Wv, L0_gnn_Wa, L0_gnn_pri, L0_gnn_Watt, L0_gnn_Wmsg, L0_gnn_skip, L0_gnn_ln_g, L0_gnn_ln_b, L0_gnn_Wff, L0_gnn_bff):
    import jax
    import jax.numpy as jnp

    def _L0_gnn_ref(x, edge_index, ntype, etype, Wk, Wq, Wv, Wa, pri, Watt, Wmsg, skip, ln_g, ln_b, Wff, bff):
        import jax, jax.numpy as jnp
        import numpy as np
        N = 50000
        E = 12500
        HID = 128
        H = 8
        HS = HID // H
        TN = 8
        R = 8
        L = 2
        OUT = 128
        EPS = 1e-05
        SQRT_D = float(np.sqrt(HS))

        def typed_linear(x, types, W):
            out = jnp.zeros((x.shape[0], W.shape[-1]), x.dtype)
            for t in range(W.shape[0]):
                out = out + jnp.where((types == t)[:, None], x @ W[t], 0.0)
            return out

        def rel_apply(h, etype, W):
            out = jnp.zeros_like(h)
            for r in range(W.shape[1]):
                out = out + jnp.where((etype == r)[:, None, None], jnp.einsum('ehi,hio->eho', h, W[:, r]), 0.0)
            return out

        def gt_layer(x, src, dst, ntype, etype, Wk, Wq, Wv, Wa, pri, Watt, Wmsg, skip, g, b):
            n = x.shape[0]
            k = typed_linear(x, ntype, Wk).reshape(n, H, HS)
            q = typed_linear(x, ntype, Wq).reshape(n, H, HS)
            v = typed_linear(x, ntype, Wv).reshape(n, H, HS)
            k_j, q_i, v_j = (k[src], q[dst], v[src])
            kw = rel_apply(k_j, etype, Watt)
            a = (kw * q_i).sum(-1) * pri[:, etype].T / SQRT_D
            amax = jax.ops.segment_max(a, dst, num_segments=n)
            ex = jnp.exp(a - amax[dst])
            den = jax.ops.segment_sum(ex, dst, num_segments=n)
            alpha = ex / (den[dst] + 1e-16)
            m = rel_apply(v_j, etype, Wmsg)
            agg = jax.ops.segment_sum(alpha[..., None] * m, dst, num_segments=n)
            out = jax.nn.silu(typed_linear(agg.reshape(n, HID), ntype, Wa))
            al = jax.nn.sigmoid(skip[ntype])[:, None]
            out = out * al + x * (1.0 - al)
            mu = out.mean(-1, keepdims=True)
            var = ((out - mu) ** 2).mean(-1, keepdims=True)
            return (out - mu) / jnp.sqrt(var + EPS) * g + b
        src, dst = (edge_index[0], edge_index[1])
        emb = x
        for l in range(L):
            emb = gt_layer(emb, src, dst, ntype, etype, Wk[l], Wq[l], Wv[l], Wa[l], pri[l], Watt[l], Wmsg[l], skip[l], ln_g[l], ln_b[l])
        return emb @ Wff + bff
    edge_index = jnp.stack([src, dst])
    x = _layernorm(x + _L0_gnn_ref(x, edge_index, node_type_8, edge_type_8, L0_gnn_Wk, L0_gnn_Wq, L0_gnn_Wv, L0_gnn_Wa, L0_gnn_pri, L0_gnn_Watt, L0_gnn_Wmsg, L0_gnn_skip, L0_gnn_ln_g, L0_gnn_ln_b, L0_gnn_Wff, L0_gnn_bff), axis=-1)
    return x

_drawn_inputs = setup_inputs


def setup_inputs(seed=0):
    import zlib

    import numpy as np

    out = dict(_drawn_inputs(seed))
    spreads = {'L0_gnn_pri': (1.0, 0.2),
     'L0_gnn_skip': (1.0, 0.2),
     'L0_gnn_ln_g': (1.0, 0.2),
     'L0_gnn_ln_b': (0.0, 0.1),
     'L0_gnn_bff': (0.0, 0.1)}
    factors = {}
    for name, (base, spread) in spreads.items():
        noise = np.random.default_rng([zlib.crc32(name.encode()), seed]).standard_normal(out[name].shape)
        drawn = base * np.exp(spread * noise) if base else spread * noise
        out[name] = jnp.asarray(drawn.astype(out[name].dtype))
    for name, factor in factors.items():
        out[name] = (out[name] * factor).astype(out[name].dtype)
    return out
```

```python
from contextlib import ExitStack, contextmanager

import numpy as np

import concourse.bass as bass
from concourse import mybir

F32 = mybir.dt.float32
BF16 = mybir.dt.bfloat16
I32 = mybir.dt.int32
ALU = mybir.AluOpType
ACT = mybir.ActivationFunctionType
AX = mybir.AxisListType
ds = bass.ds

P = 128
NODES, HID = 3125, 128
EDGES = 100000
HEADS, HS = 8, 16
TYPES, RELS, LAYERS = 8, 8, 2
EPS = 1e-5

NP = 125
NT = NODES // NP
BT = 5
NBATCH = NT // BT
BN = BT * NP
KEY_CUT = 3 * NP

EP = 125
EC = EDGES // EP
EB = 4
BLOCKS = EDGES // EB

ROW_TILES = 4
GR = ROW_TILES * P
GROUPS = -(-(BLOCKS + NODES) // GR)
ROWS = GROUPS * GR
TILES = ROWS // P
SLOTS = ROW_TILES * EB
RC = ROWS // P
HALF = TILES // 2
PAIRS = (GROUPS - 1) // 2
assert GROUPS % 2 == 1 and TILES % (2 * NBATCH) == 0

PART = TILES // (2 * NBATCH)

LO = 64
HI = -(-NODES // LO)
CHUNK = 50
CHUNK_PAIRS = EC // CHUNK // 2

LINE = 2 * HID
OUT_LINE = HID + HEADS

OFF = 1e30
FLOOR = -1e29
RESET = -1e31


class Steps:

    def __init__(self, engine, sem):
        self.engine, self.sem, self.count, self.steps = engine, sem, 0, 0

    def step(self, instruction):
        instruction.then_inc(self.sem, 1)
        self.count = self.count + 1
        self.steps += 1

    def wait(self):
        self.engine.wait_ge(self.sem, self.count)

    def chained(self, instruction):
        self.step(instruction)
        self.wait()

    @contextmanager
    def loop(self, trips, steps_each):
        start, steps = self.count, self.steps
        with self.engine.Fori(0, trips) as i:
            self.count = start + i * steps_each
            yield i
        assert self.steps - steps == steps_each, self.steps - steps
        self.count = start + trips * steps_each


START, DMA_START = 1, 16


class Arena:

    def __init__(self, whole):
        self.whole, self.used = whole, 0

    def take(self, shape, dt=F32, rows=P):
        count = int(np.prod(shape))
        words = -(-count * (2 if dt == BF16 else 4) // 64) * 16
        ap = self.whole[0:rows, self.used:self.used + words]
        self.used += words
        if dt != F32:
            ap = ap.bitcast(dt)
        ap = ap[:, 0:count]
        if len(shape) > 1:
            names = "abcd"[:len(shape)]
            ap = ap.rearrange(f"p ({' '.join(names)}) -> p {' '.join(names)}", **dict(zip(names, shape)))
        return ap


def build(nc, x, src, dst, etype, ntype, Wk, Wq, Wv, Wa, pri, Watt, Wmsg, skip, ln_g, ln_b, Wff, bff, out):
    ctx = ExitStack()
    with ctx:
        def sb(name, shape, dt=F32):
            return ctx.enter_context(nc.sbuf_tensor(name, shape, dt))

        def sem(name):
            return ctx.enter_context(nc.semaphore(name))

        def dram(name, shape, dt=F32):
            return nc.dram_tensor(name, shape, dt, kind="Internal").ap()

        block_lines = dram("block_lines", [BLOCKS, 2 * EB], I32)
        node_info = dram("node_info", [HI * LO, 4], I32)
        markers = dram("markers", [ROWS, 2], I32)
        row_node = dram("row_node", [2, ROWS])
        row_block = dram("row_block", [ROWS])
        row_node_int = dram("row_node_int", [ROWS], I32)
        query_table = dram("query_table", [NODES + P, HID])
        line_table = dram("line_table", [NODES * RELS, LINE])
        row_table = dram("row_table", [ROWS, OUT_LINE])

        ident = sb("ident", [P, P])
        zeros = sb("zeros", [P, P])
        primer = sb("primer", [1, BT + 4, 16])
        before = sb("before", [HI, HI])
        head_pick = sb("head_pick", [P, HEADS])
        part_index = sb("part_index", [P, 1])
        ones_row = sb("ones_row", [1, P])
        iota_hi = sb("iota_hi", [P, HI], BF16)
        iota_lo = sb("iota_lo", [P, LO], BF16)
        node_iota = sb("node_iota", [HI, LO])
        row_iota = sb("row_iota", [P, RC])

        emb = sb("emb", [NP, NT, HID])
        type_row = sb("type_row", [P, NODES])
        alpha_part = sb("alpha_part", [NP, NT])
        alpha = sb("alpha", [NP, NT])
        type_col = sb("type_col", [NP, NT], I32)
        type_col_f = sb("type_col_f", [NP, NT])
        skip_sig = sb("skip_sig", [P, TYPES])
        weights = sb("weights", [P, TYPES, 4, HID])
        rel_mats = sb("rel_mats", [P, 2, RELS, HID])
        pri_scale = sb("pri_scale", [P, RELS])
        gain = sb("gain", [P, HID])
        shift = sb("shift", [P, HID])
        wff = sb("wff", [P, HID])
        bff_row = sb("bff_row", [P, HID])
        info = sb("info", [NP, NT, 4], I32)
        block_of = sb("block_of", [P, TILES], I32)
        node_of = sb("node_of", [P, TILES])
        tile_base = sb("tile_base", [P, TILES])
        codes = sb("codes", [P, TILES * EB], I32)
        limit = sb("limit", [P, TILES * EB])
        first_nodes = sb("first_nodes", [1, TILES], I32)

        masked = sb("masked", [P, TYPES, BN])
        current = sb("current", [NP, BT, HID])
        emb_t = sb("emb_t", [P, BN])
        kv_t = sb("kv_t", [P, 2, BN])

        lines = sb("lines", [P, 2, SLOTS, LINE])
        scratch = sb("scratch", [P, 1600])
        area = sb("area", [P, 12288])
        lines_arena = Arena(lines[:, :, :, :].rearrange("p a b c -> p (a b c)"))
        scratch_arena = Arena(scratch[:, :])
        area_arena = Arena(area[:, :])
        dst_i = lines_arena.take([EC], I32, EP)
        src_i = lines_arena.take([EC], I32, EP)
        ety_i = lines_arena.take([EC], I32, EP)
        dst_hi_i = scratch_arena.take([EC], I32, EP)
        blk = lines_arena.take([EC // EB, 2 * EB], I32, EP)
        onehot_lo = [lines_arena.take([CHUNK, LO], BF16, EP) for _ in range(2)]
        dst_hi = scratch_arena.take([EC], BF16, EP)
        dst_lo = scratch_arena.take([EC], BF16, EP)
        onehot_hi = [area_arena.take([CHUNK, HI], BF16, EP) for _ in range(2)]
        area_arena.used = 0
        counts = sb("counts", [HI, 10, LO])
        counts_int = sb("counts_int", [HI, 3, LO], I32)
        info_pack = sb("info_pack", [HI, LO, 4], I32)
        tot = sb("tot", [HI, 2])
        lines_arena.used = 0
        mark_i = lines_arena.take([RC, 2], I32)
        mark = lines_arena.take([2, RC])
        held = lines_arena.take([2, RC])
        row_out = lines_arena.take([3, RC])
        node_int = lines_arena.take([RC], I32)
        last_col = lines_arena.take([2])
        last_row = lines_arena.take([P + 1], F32, 2)
        prior_row = lines_arena.take([P], F32, 2)
        prior_col = lines_arena.take([2])
        tile_rows = lines_arena.take([2, 2, P], F32, HALF)
        base_row = lines_arena.take([TILES], F32, 1)
        block_idx = [lines_arena.take([PART], I32) for _ in range(2)]
        block_in = [lines_arena.take([PART, 2 * EB], I32) for _ in range(2)]
        slot_ok = [lines_arena.take([PART, EB]) for _ in range(2)]
        last_idx = sb("last_idx", [NP, BT], I32)
        table_rows = [area_arena.take([RELS, LINE], F32, NP) for _ in range(BT)]
        query_out = area_arena.take([BT, HID], F32, NP)
        area_arena.used = 0
        last_rows = area_arena.take([BT, OUT_LINE], F32, NP)
        den_inv = area_arena.take([BT, HEADS], F32, NP)
        agg = area_arena.take([BT, HID], F32, NP)
        gate = area_arena.take([BT, HID], F32, NP)
        mixed = area_arena.take([BT, HID], F32, NP)
        squares = area_arena.take([BT, HID], F32, NP)
        stats = area_arena.take([4, BT], F32, NP)
        x_again = area_arena.take([BT, HID], F32, NP)
        result = area_arena.take([BT, HID], F32, NP)
        area_arena.used = 0
        slot_idx = [sb(f"slot_idx{u}", [P, SLOTS], I32) for u in range(2)]
        window = [area_arena.take([ROW_TILES, HID]) for _ in range(2)]
        row_info = [area_arena.take([2, GR]) for _ in range(2)]
        spread = area_arena.take([ROW_TILES, P])
        score = [area_arena.take([ROW_TILES, EB, HEADS]) for _ in range(2)]
        row_max = [area_arena.take([ROW_TILES, HEADS]) for _ in range(2)]
        row_den = [area_arena.take([ROW_TILES, HEADS]) for _ in range(2)]
        prob = [area_arena.take([ROW_TILES, EB, HEADS]) for _ in range(2)]
        max_wide = area_arena.take([ROW_TILES, HEADS, HS])
        den_wide = area_arena.take([ROW_TILES, HEADS, HS])
        run_max = [area_arena.take([GR + 1]) for _ in range(2)]
        factor = area_arena.take([2, GR])
        scaled = area_arena.take([2, GR])
        run_sum = [area_arena.take([2, GR]) for _ in range(2)]
        out_rows = [sb(f"out_rows{u}", [P, ROW_TILES, OUT_LINE]) for u in range(2)]

        ps = ctx.enter_context(nc.psum_tensor("ps", [P, 8, 512], F32))

        s_const = sem("const_ready")
        s_turns = sem("gather_turns")
        s_edges_in = sem("edges_in")
        s_weights_in = sem("weights_in")
        s_small_in = sem("small_in")
        s_late_in = sem("output_weights_in")
        s_emb_in = sem("emb_in")
        s_dve = sem("vector_steps")
        s_act = sem("scalar_steps")
        s_pool = sem("pool_steps")
        s_pe_idx = sem("index_products")
        s_dst_split = sem("destinations_split")
        s_hot = [sem(f"onehots_ready{u}") for u in range(2)]
        s_hist = [sem(f"histogram_chunk{u}") for u in range(2)]
        s_blocks_ready = sem("block_lines_ready")
        s_blocks_out = sem("block_lines_out")
        s_info_ready = sem("node_info_ready")
        s_info_dram = sem("node_info_out")
        s_info_in = sem("node_info_in")
        s_zeros = sem("zeros_ready")
        s_zero_out = sem("markers_zeroed")
        s_marks_out = sem("markers_out")
        s_marks_in = sem("markers_in")
        s_idx_vec = sem("index_vector")
        s_rows_ready = sem("rows_ready")
        s_rows_out = sem("rows_out")
        s_rows_in = sem("rows_in")
        s_block_of = sem("block_of_ready")
        s_blk_idx = [sem(f"block_indices{u}") for u in range(2)]
        s_blk_in = [sem(f"blocks_in{u}") for u in range(2)]
        s_blk_used = [sem(f"blocks_used{u}") for u in range(2)]
        s_rel = sem("relation_matrices_ready")
        s_et = sem("embedding_transposed")
        s_etc = sem("embedding_copied")
        s_mask = sem("masked_ready")
        s_mask_used = sem("masked_used")
        s_kt = sem("keys_values_ready")
        s_ktc = sem("keys_values_copied")
        s_q = sem("queries_ready")
        s_qc = sem("queries_copied")
        s_q_out = sem("queries_out")
        s_tk = sem("key_lines_ready")
        s_tv = sem("value_lines_ready")
        s_tkc = sem("key_lines_copied")
        s_tvc = sem("value_lines_copied")
        s_t_out = [sem(f"lines_out{j}") for j in range(BT)]
        s_pad_out = sem("query_padding_out")
        s_idx_in = [sem(f"slot_indices_in{u}") for u in range(2)]
        s_win_in = [sem(f"windows_in{u}") for u in range(2)]
        s_ri_in = [sem(f"row_info_in{u}") for u in range(2)]
        s_kv_in = [sem(f"gathered{u}") for u in range(2)]
        s_spread = sem("spread_ready")
        s_rq = sem("row_queries_ready")
        s_prod = sem("products_ready")
        s_sum = sem("score_sums_ready")
        s_lim = sem("scores_limited")
        s_mx = sem("slot_maximum_ready")
        s_max = sem("row_maximum_ready")
        s_diff = sem("score_differences_ready")
        s_prob = sem("probabilities_ready")
        s_maxw = sem("maximum_widened")
        s_den = sem("row_sums_ready")
        s_denw = sem("row_sums_widened")
        s_pv = sem("weighted_values_ready")
        s_half_used = [sem(f"values_summed{k}") for k in range(2)]
        s_mt = sem("maximum_transposed")
        s_ut = sem("row_totals_transposed")
        s_run = sem("running_maximum_ready")
        s_grow = sem("growth_started")
        s_fac_in = sem("factor_exponents_ready")
        s_fac = sem("factors_ready")
        s_scaled = sem("totals_scaled")
        s_sums = sem("running_sums_ready")
        s_back = sem("rows_transposed_back")
        s_row = sem("rows_copied")
        s_row_out = [sem(f"rows_out{u}") for u in range(2)]
        s_li = sem("last_indices_ready")
        s_lr_in = sem("last_rows_in")
        s_ag = sem("aggregates_ready")
        s_at = sem("aggregates_transposed")
        s_atc = sem("aggregates_copied")
        s_am = sem("masked_aggregates_ready")
        s_y = sem("outputs_ready")
        s_ye = sem("output_exponentials_ready")
        s_var = sem("variance_ready")
        s_sd = sem("deviation_ready")
        s_cur = sem("batch_copied")
        s_emb = sem("embedding_ready")
        s_skip = sem("skip_exponentials_ready")
        s_gain = sem("gain_applied")
        s_ht = sem("head_transposed")
        s_htc = sem("head_copied")
        s_hy = sem("head_ready")
        s_xa = sem("input_again")
        s_var2 = sem("final_variance_ready")
        s_sd2 = sem("final_deviation_ready")
        s_res = sem("result_ready")
        s_out = sem("result_out")

        N_CONST = 10
        BLK_LOADS = 4
        NODE_LOADS = 3 + 3 * HEADS

        block = ctx.enter_context(nc.Block())

        def part_uses(u):
            return PAIRS + 1 if u == 0 else PAIRS

        @block.sync
        def _(sp):
            for s in (*s_half_used, *s_hist, *s_blk_used, s_etc, s_tkc, s_tvc, s_qc, s_mask, s_tk, s_tv, s_et, s_q, s_rq, s_fac_in, s_ut, s_scaled, s_back, s_row, s_res, s_ag, s_emb, s_sums, s_prod, s_mt):
                sp.sem_inc(s, START)
            for k, s in enumerate((*s_t_out, s_q_out, *s_row_out, s_out)):
                sp.dma_start(primer[:, k, :], x[0:1, 0:16]).then_inc(s, DMA_START)
            for t, a in ((dst_i, dst), (src_i, src), (ety_i, etype)):
                sp.dma_start(t, a.rearrange("(p c) -> p c", p=EP)).then_inc(s_edges_in, 16)
            sp.dma_start(emb[:, :, :], x.rearrange("(t p) d -> p t d", p=NP)).then_inc(s_emb_in, 16)
            type_int = masked[:, :, :].rearrange("p a b -> p (a b)")[:, 0:NODES].bitcast(I32)
            for t, a in ((type_int, ntype.partition_broadcast(P)),
                         (type_col[:, :], ntype.rearrange("(t p) -> p t", p=NP)),
                         (wff[:, :], Wff), (bff_row[:, :], bff.partition_broadcast(P))):
                with nc.allow_non_contiguous_dma("types of the nodes"):
                    sp.dma_start(t, a).then_inc(s_small_in, 16)

            def node_weights(l):
                for k, w in enumerate((Wk, Wv, Wq)):
                    sp.dma_start(weights[:, :, k, :], w[l].rearrange("t i o -> i t o")).then_inc(s_weights_in, 16)
                sp.wait_ge(s_rel, 1)
                for h in range(HEADS):
                    part = slice(h * HS, (h + 1) * HS)
                    for k, w in enumerate((Watt, Wmsg)):
                        sp.dma_start(rel_mats[part, k, :, part], w[l, h].rearrange("r i o -> i r o")).then_inc(s_weights_in, 16)
                    sp.dma_start(pri_scale[part, :], pri[l, h].partition_broadcast(HS)).then_inc(s_weights_in, 16)

            def output_weights(l):
                if l > 0:
                    sp.wait_ge(s_emb, START + NBATCH * l)
                sp.dma_start(weights[:, :, 3, :], Wa[l].rearrange("t i o -> i t o")).then_inc(s_late_in, 16)
                sp.dma_start(gain[:, :], ln_g[l].partition_broadcast(P)).then_inc(s_late_in, 16)
                sp.dma_start(shift[:, :], ln_b[l].partition_broadcast(P)).then_inc(s_late_in, 16)
                sp.dma_start(skip_sig[:, :], skip[l].partition_broadcast(P)).then_inc(s_late_in, 16)

            node_weights(0)
            output_weights(0)
            sp.wait_ge(s_zeros, 1)
            sp.dma_start(query_table[NODES:NODES + P, :], zeros[:, :]).then_inc(s_pad_out, 16)
            sp.wait_ge(s_blocks_ready, 2)
            sp.dma_start(block_lines.rearrange("(p b) c -> p b c", p=EP), blk).then_inc(s_blocks_out, 16)
            sp.dma_start(markers.rearrange("(p k r) c -> p k (r c)", p=P, k=4),
                         zeros[:, 0:RC // 2].bitcast(I32).unsqueeze(1).broadcast_to([P, 4, RC // 2])).then_inc(s_zero_out, 16)
            sp.wait_ge(s_info_ready, 4)
            sp.dma_start(node_info.rearrange("(p c) k -> p c k", p=HI), info_pack[:, :, :]).then_inc(s_info_dram, 16)
            sp.wait_ge(s_info_dram, 16)
            sp.dma_start(info[:, :, :], node_info[0:NODES, :].rearrange("(t p) k -> p t k", p=NP)).then_inc(s_info_in, 16)
            sp.wait_ge(s_marks_out, 16 * NT)
            sp.wait_ge(s_blocks_out, 16)
            sp.dma_start(mark_i, markers.rearrange("(p r) c -> p r c", p=P)).then_inc(s_marks_in, 16)
            sp.wait_ge(s_rows_ready, 4)
            sp.dma_start(row_node.rearrange("k (p r) -> p k r", p=P), row_out[:, 0:2, :]).then_inc(s_rows_out, 16)
            sp.dma_start(row_block.rearrange("(p r) -> p r", p=P), row_out[:, 2, :]).then_inc(s_rows_out, 16)
            sp.dma_start(row_node_int.rearrange("(p r) -> p r", p=P), node_int).then_inc(s_rows_out, 16)
            sp.wait_ge(s_rows_out, 48)
            sp.dma_start(tile_rows[:, 0, :, :], row_node[0].rearrange("(k q p) -> q k p", k=2, p=P)).then_inc(s_rows_in, 16)
            sp.dma_start(tile_rows[:, 1, :, :], row_block.rearrange("(k q p) -> q k p", k=2, p=P)).then_inc(s_rows_in, 16)
            with nc.allow_non_contiguous_dma("first rows of the tiles"):
                sp.dma_start(base_row, row_node[0:1, :].rearrange("o (t p) -> o t p", p=P)[:, :, 0]).then_inc(s_rows_in, 16)
                sp.dma_start(first_nodes[:, :], row_node_int.rearrange("(o t p) -> o t p", o=1, p=P)[:, :, 0]).then_inc(s_rows_in, 16)

            def node_stores(l):
                with sp.Fori(0, NBATCH) as b:
                    for j in range(BT):
                        sp.wait_ge(s_tkc, START + (l * NBATCH + b) * BT + (j + 1))
                        sp.wait_ge(s_tvc, START + (l * NBATCH + b) * BT + (j + 1))
                        sp.dma_start(line_table.rearrange("(t p r) c -> t p (r c)", p=NP, r=RELS)[ds(b * BT + j, 1)].rearrange("o p c -> p (o c)"),
                                     table_rows[j].rearrange("p r c -> p (r c)")).then_inc(s_t_out[j], 16)
                    sp.wait_ge(s_qc, START + l * NBATCH + b + 1)
                    sp.dma_start(query_table[0:NODES, :].rearrange("(t p) d -> p t d", p=NP)[:, ds(b * BT, BT), :],
                                 query_out).then_inc(s_q_out, 16)

            def edge_loads(l, g, half, u, first):
                if not first:
                    sp.wait_ge(s_prod, START + l * GROUPS + g - 1)
                sp.dma_start(slot_idx[u][:, :], codes[:, ds(g * SLOTS, SLOTS)]).then_inc(s_idx_in[u], 16)
                if not first:
                    sp.wait_ge(s_rq, START + l * GROUPS + g - 1)
                    sp.wait_ge(s_fac_in, START + l * GROUPS + g - 1)
                for t in range(ROW_TILES):
                    node = sp.value_load(first_nodes[0:1, ds(g * ROW_TILES + t, 1)], min_val=0, max_val=NODES - 1)
                    sp.dma_start(window[u][:, t, :], query_table[ds(node, P), :]).then_inc(s_win_in[u], 16)
                sp.dma_start(row_info[u], row_node.rearrange("k (g r) -> g k r", r=GR)[ds(g, 1)].rearrange("o k r -> (o k) r").partition_broadcast(P)).then_inc(s_ri_in[u], 16)

            for l in range(LAYERS):
                node_stores(l)
                sp.wait_ge(s_q_out, DMA_START + 16 * NBATCH * (l + 1))
                sp.wait_ge(s_pad_out, 16)
                for j in range(BT):
                    sp.wait_ge(s_t_out[j], DMA_START + 16 * NBATCH * (l + 1))
                if l == 0:
                    sp.wait_ge(s_rows_in, 16 * BLK_LOADS)
                    for u in range(2):
                        sp.wait_ge(s_blk_used[u], START + NBATCH)
                if l > 0:
                    output_weights(l)
                if l + 1 < LAYERS:
                    node_weights(l + 1)
                edge_loads(l, 0, 0, 0, True)
                with sp.Fori(0, PAIRS) as i:
                    edge_loads(l, 1 + 2 * i, i, 1, False)
                    edge_loads(l, 2 + 2 * i, i + 1, 0, False)
            with sp.Fori(0, NBATCH) as b:
                sp.wait_ge(s_res, START + b)
                sp.wait_ge(s_lr_in, 16 * BT * (NBATCH * (LAYERS - 1) + b + 1))
                sp.dma_start(x_again, x.rearrange("(t p) d -> p t d", p=NP)[:, ds(b * BT, BT), :]).then_inc(s_xa, 16)
                sp.wait_ge(s_res, START + b + 1)
                sp.dma_start(out.rearrange("(t p) d -> p t d", p=NP)[:, ds(b * BT, BT), :], result).then_inc(s_out, 16)
            sp.wait_ge(s_out, DMA_START + 16 * NBATCH)

        @block.gpsimd
        def _(pool):
            own = Steps(pool, s_pool)

            def turn_counted():
                pool.sem_inc(s_turns, 1)

            def const(instruction):
                instruction.then_inc(s_const, 1)

            pool.iota(ident[:, :], [[1, P]], base=0, channel_multiplier=-1, allow_small_or_imprecise_dtypes=True).then_inc(s_pool, 1)
            pool.iota(before[:, :], [[1, HI]], base=0, channel_multiplier=-1, allow_small_or_imprecise_dtypes=True).then_inc(s_pool, 1)
            pool.memset(head_pick[:, :], 0.0).then_inc(s_pool, 1)
            own.count = 3
            own.wait()
            const(pool.iota(iota_hi[:, :], [[1, HI]], base=0, channel_multiplier=0, allow_small_or_imprecise_dtypes=True))
            const(pool.iota(iota_lo[:, :], [[1, LO]], base=0, channel_multiplier=0, allow_small_or_imprecise_dtypes=True))
            const(pool.tensor_scalar(ident[:, :], ident[:, :], 0.0, None, ALU.is_equal))
            const(pool.tensor_scalar(before[:, :], before[:, :], 0.0, None, ALU.is_gt))
            const(pool.affine_select(out=head_pick[:, :], in_=head_pick[:, :], compare_op=ALU.not_equal, fill=1.0,
                                     base=0, pattern=[[-HS, HEADS]], channel_multiplier=1))
            const(pool.iota(part_index[:, :], [[0, 1]], base=0, channel_multiplier=1, allow_small_or_imprecise_dtypes=True))
            const(pool.memset(ones_row[:, :], 1.0))
            const(pool.iota(node_iota[:, :], [[1, LO]], base=1, channel_multiplier=LO, allow_small_or_imprecise_dtypes=True))
            const(pool.iota(row_iota[:, :], [[1, RC]], base=0, channel_multiplier=RC, allow_small_or_imprecise_dtypes=True))
            const(pool.memset(tot[:, :], 0.0))
            pool.wait_ge(s_info_in, 16)
            pool.wait_ge(s_zero_out, 16)
            for t in range(NT):
                pool.indirect_dma_start(out=markers, out_offset=bass.IndirectOffsetOnAxis(ap=info[:, t, 0:1], axis=0),
                                        in_=info[:, t, 1:3], in_offset=None).then_inc(s_marks_out, 16)
            pool.wait_ge(s_blocks_out, 16)
            pool.wait_ge(s_block_of, 2)
            with pool.Fori(0, NBATCH) as b:
                for u in range(2):
                    pool.wait_ge(s_blk_used[u], START + b)
                    pool.tensor_copy(block_idx[u], block_of[:, ds((2 * b + u) * PART, PART)]).then_inc(s_blk_idx[u], 1)
                    pool.wait_ge(s_blk_idx[u], b + 1)
                    turn_counted()
                    for t in range(PART):
                        pool.indirect_dma_start(out=block_in[u][:, t, :], out_offset=None, in_=block_lines,
                                                in_offset=bass.IndirectOffsetOnAxis(ap=block_idx[u][:, t:t + 1], axis=0)
                                                ).then_inc(s_blk_in[u], 16)

            def gathers(l, g, half, u, first):
                pool.wait_ge(s_idx_in[u], 16 * (l * part_uses(u) + half + 1))
                for k in range(SLOTS):
                    if k in (0, SLOTS // 2):
                        if not first:
                            pool.wait_ge(s_half_used[k * 2 // SLOTS], START + l * GROUPS + g - 1)
                        turn_counted()
                    pool.indirect_dma_start(out=lines[:, u, k, :], out_offset=None, in_=line_table,
                                            in_offset=bass.IndirectOffsetOnAxis(ap=slot_idx[u][:, k:k + 1], axis=0)
                                            ).then_inc(s_kv_in[u], 16)

            for l in range(LAYERS):
                for j in range(BT):
                    pool.wait_ge(s_t_out[j], DMA_START + 16 * NBATCH * (l + 1))
                gathers(l, 0, 0, 0, True)
                with pool.Fori(0, PAIRS) as i:
                    gathers(l, 1 + 2 * i, i, 1, False)
                    gathers(l, 2 + 2 * i, i + 1, 0, False)
                for u in range(2):
                    pool.wait_ge(s_row_out[u], DMA_START + 16 * (l + 1) * part_uses(u))
                with pool.Fori(0, NBATCH) as b:
                    pool.wait_ge(s_ag, START + l * NBATCH + b)
                    pool.tensor_copy(last_idx[:, :], info[:, ds(b * BT, BT), 3]).then_inc(s_li, 1)
                    pool.wait_ge(s_li, l * NBATCH + b + 1)
                    turn_counted()
                    for j in range(BT):
                        pool.indirect_dma_start(out=last_rows[:, j, :], out_offset=None, in_=row_table,
                                                in_offset=bass.IndirectOffsetOnAxis(ap=last_idx[:, j:j + 1], axis=0)
                                                ).then_inc(s_lr_in, 16)

        @block.tensor
        def _(pe):
            def bank(k, rows, a, b):
                return ps[0:rows, k, a:b]

            def wide(k, rows, a, b):
                return bank(k + a // 512, rows, a % 512, (b - 1) % 512 + 1)

            pe.wait_ge(s_const, N_CONST)
            pe.wait_ge(s_zeros, 1)
            onehot_zero = zeros[0:EP, :].bitcast(BF16)
            pe.matmul(bank(0, HI, 0, LO), onehot_zero[:, 0:HI], onehot_zero[:, 0:LO], start=True, stop=False, skip_group_check=True)
            with pe.Fori(0, CHUNK_PAIRS) as i:
                for u in range(2):
                    pe.wait_ge(s_hot[u], i + 1)
                    for c in range(CHUNK):
                        mm = pe.matmul(bank(0, HI, 0, LO), onehot_hi[u][:, c, :], onehot_lo[u][:, c, :],
                                       start=False, stop=False, skip_group_check=True)
                    mm.then_inc(s_hist[u], 1)
            pe.matmul(bank(0, HI, 0, LO), onehot_zero[:, 0:HI], onehot_zero[:, 0:LO], start=False, stop=True, skip_group_check=True).then_inc(s_pe_idx, 1)
            for k in range(2):
                pe.wait_ge(s_idx_vec, k + 1)
                pe.matmul(bank(1, HI, k, k + 1), before[:, :], tot[:, k:k + 1], start=True, stop=True).then_inc(s_pe_idx, 1)
            pe.wait_ge(s_idx_vec, 3)
            pe.transpose(bank(2, 2, 0, P), last_col, ident[:, :]).then_inc(s_pe_idx, 1)
            pe.wait_ge(s_idx_vec, 4)
            pe.transpose(bank(3, P, 0, 2), prior_row, ident[0:2, 0:2]).then_inc(s_pe_idx, 1)
            pe.wait_ge(s_rows_in, 16 * BLK_LOADS)
            for k in range(2):
                for h in range(2):
                    mm = pe.transpose(bank(4 + k, P, h * HALF, (h + 1) * HALF), tile_rows[:, k, h, :], ident[0:HALF, 0:HALF])
            pe.matmul(bank(6, P, 0, TILES), ones_row[:, :], base_row, start=True, stop=True).then_inc(s_pe_idx, 1)

            def transposed(source, ready):
                for j in range(BT):
                    mm = pe.transpose(wide(0, P, j * P, j * P + NP), source[:, j, :], ident[0:NP, 0:NP])
                mm.then_inc(ready, 1)

            def node_stage(l):
                pe.wait_ge(s_rel, l + 2)
                pe.wait_ge(s_weights_in, 16 * NODE_LOADS * (l + 1))
                if l == 0:
                    pe.wait_ge(s_block_of, 3)
                with pe.Fori(0, NBATCH) as b:
                    n = l * NBATCH + b
                    pe.wait_ge(s_etc, START + n)
                    pe.wait_ge(s_cur, n + 1)
                    transposed(current, s_et)
                    pe.wait_ge(s_mask, START + n + 1)
                    pe.wait_ge(s_tkc, START + n * BT)
                    pe.wait_ge(s_tvc, START + n * BT)
                    for k in range(2):
                        for part, (lo, hi) in enumerate(((0, KEY_CUT), (KEY_CUT, BN))):
                            for t in range(TYPES):
                                mm = pe.matmul(bank(2 + 2 * k + part, P, 0, hi - lo), weights[:, t, k, :], masked[:, t, lo:hi],
                                               start=(t == 0), stop=(t == TYPES - 1))
                        mm.then_inc(s_kt, 1)
                    pe.wait_ge(s_qc, START + n)
                    for j in range(BT):
                        for t in range(TYPES):
                            mm = pe.matmul(wide(6, NP, j * HID, (j + 1) * HID), masked[:, t, j * NP:(j + 1) * NP], weights[:, t, 2, :],
                                           start=(t == 0), stop=(t == TYPES - 1))
                    mm.then_inc(s_q, 1)
                    pe.wait_ge(s_ktc, 2 * n + 2)
                    for j in range(BT):
                        for k, (ready, copied) in enumerate(((s_tk, s_tkc), (s_tv, s_tvc))):
                            pe.wait_ge(copied, START + n * BT + j)
                            for half in range(2):
                                mm = pe.matmul(bank(2 + 2 * k + half, NP, 0, 512), kv_t[:, k, j * NP:(j + 1) * NP],
                                               rel_mats[:, k, half * 4:half * 4 + 4, :].rearrange("p r d -> p (r d)"), start=True, stop=True)
                            mm.then_inc(ready, 1)

            def row_queries(l, g, half, u):
                pe.wait_ge(s_win_in[u], 16 * ROW_TILES * (l * part_uses(u) + half + 1))
                pe.wait_ge(s_spread, l * GROUPS + g + 1)
                pe.wait_ge(s_prod, START + l * GROUPS + g)
                for t in range(ROW_TILES):
                    mm = pe.matmul(bank(0, P, t * P, (t + 1) * P), spread[:, t, :], window[u][:, t, :], start=True, stop=True)
                mm.then_inc(s_rq, 1)

            def transposes(l, g, u, first):
                G = l * GROUPS + g
                pe.wait_ge(s_maxw, G + 1)
                if not first:
                    pe.wait_ge(s_fac_in, START + G)
                for t in range(ROW_TILES):
                    mm = pe.transpose(bank(5, P, t * P, (t + 1) * P), max_wide[:, t, :, :].rearrange("p h c -> p (h c)"), ident[:, :])
                mm.then_inc(s_mt, 1)
                if not first:
                    pe.wait_ge(s_scaled, START + G - 1)
                for half in range(2):
                    pe.wait_ge(s_pv, 2 * G + half + 1)
                    for t in range(half * ROW_TILES // 2, (half + 1) * ROW_TILES // 2):
                        for k in range(EB):
                            mm = pe.matmul(bank(1 + 2 * u, P, t * P, (t + 1) * P), lines[:, u, t * EB + k, HID:LINE], ident[:, :],
                                           start=(k == 0), stop=(k == EB - 1))
                    mm.then_inc(s_half_used[half], 1)
                pe.wait_ge(s_denw, G + 1)
                for t in range(ROW_TILES):
                    mm = pe.transpose(bank(2 + 2 * u, P, t * P, (t + 1) * P), den_wide[:, t, :, :].rearrange("p h c -> p (h c)"), ident[:, :])
                mm.then_inc(s_ut, 1)

            def back(l, g, u, first):
                G = l * GROUPS + g
                pe.wait_ge(s_sums, START + 2 * G + 2)
                if not first:
                    pe.wait_ge(s_row, START + G)
                for t in range(ROW_TILES):
                    pe.transpose(bank(6, P, t * P, (t + 1) * P), run_sum[u][:, 0, t * P:(t + 1) * P], ident[:, :])
                for t in range(ROW_TILES):
                    mm = pe.matmul(bank(7, P, t * HEADS, (t + 1) * HEADS), run_sum[u][:, 1, t * P:(t + 1) * P], head_pick[:, :], start=True, stop=True)
                mm.then_inc(s_back, 1)

            def edge_stage(l):
                pe.wait_ge(s_tkc, START + NT * (l + 1))
                pe.wait_ge(s_tvc, START + NT * (l + 1))
                pe.wait_ge(s_qc, START + NBATCH * (l + 1))
                row_queries(l, 0, 0, 0)
                row_queries(l, 1, 0, 1)
                transposes(l, 0, 0, True)
                with pe.Fori(0, PAIRS - 1) as i:
                    for g, half, u in ((2 + 2 * i, i + 1, 0), (3 + 2 * i, i + 1, 1)):
                        row_queries(l, g, half, u)
                        transposes(l, g - 1, 1 - u, False)
                        back(l, g - 2, u, False)
                row_queries(l, GROUPS - 1, PAIRS, 0)
                transposes(l, GROUPS - 2, 1, False)
                back(l, GROUPS - 3, 0, False)
                transposes(l, GROUPS - 1, 0, False)
                back(l, GROUPS - 2, 1, False)
                back(l, GROUPS - 1, 0, False)

            def output_stage(l):
                last = l == LAYERS - 1
                pe.wait_ge(s_row, START + GROUPS * (l + 1))
                pe.wait_ge(s_late_in, 16 * 4 * (l + 1))
                with pe.Fori(0, NBATCH) as b:
                    n = l * NBATCH + b
                    pe.wait_ge(s_ag, START + n + 1)
                    pe.wait_ge(s_emb, START + n)
                    if last:
                        pe.wait_ge(s_res, START + b)
                    transposed(agg, s_at)
                    pe.wait_ge(s_am, n + 1)
                    for j in range(BT):
                        for t in range(TYPES):
                            mm = pe.matmul(wide(2, NP, j * HID, (j + 1) * HID), masked[:, t, j * NP:(j + 1) * NP], weights[:, t, 3, :],
                                           start=(t == 0), stop=(t == TYPES - 1))
                    mm.then_inc(s_y, 1)
                    if last:
                        pe.wait_ge(s_emb, START + n + 1)
                        transposed(current, s_ht)
                        pe.wait_ge(s_htc, b + 1)
                        for j in range(BT):
                            mm = pe.matmul(wide(4, NP, j * HID, (j + 1) * HID), emb_t[:, j * NP:(j + 1) * NP], wff[:, :], start=True, stop=True)
                        mm.then_inc(s_hy, 1)

            for l in range(LAYERS):
                node_stage(l)
                edge_stage(l)
                output_stage(l)

        @block.scalar
        def _(act):
            copy = ACT.Copy

            def copied_wide(dst_ap, k, rows, width, done):
                src_ap = ps[0:rows, k:k + 2, :].rearrange("p a c -> p (a c)")[:, 0:BT * P].rearrange("p (t c) -> p t c", t=BT)
                act.activation(dst_ap, src_ap[:, :, 0:width], copy).then_inc(done, 1)

            def node_stage(l):
                if l == 0:
                    act.wait_ge(s_emb_in, 16)
                act.wait_ge(s_emb, START + NBATCH * l)
                with act.Fori(0, NBATCH) as b:
                    n = l * NBATCH + b
                    act.wait_ge(s_et, START + n)
                    act.activation(current[:, :, :], emb[:, ds(b * BT, BT), :], copy).then_inc(s_cur, 1)
                    act.wait_ge(s_et, START + n + 1)
                    act.wait_ge(s_mask, START + n)
                    copied_wide(emb_t[:, :].rearrange("p (t c) -> p t c", t=BT), 0, P, NP, s_etc)
                    act.wait_ge(s_tk, START + n * BT)
                    act.wait_ge(s_tv, START + n * BT)
                    for k in range(2):
                        act.wait_ge(s_kt, 2 * n + k + 1)
                        act.activation(kv_t[:, k, 0:KEY_CUT], ps[:, 2 + 2 * k, 0:KEY_CUT], copy)
                        act.activation(kv_t[:, k, KEY_CUT:BN], ps[:, 3 + 2 * k, 0:BN - KEY_CUT], copy).then_inc(s_ktc, 1)
                    act.wait_ge(s_q, START + n + 1)
                    act.wait_ge(s_q_out, DMA_START + 16 * n)
                    copied_wide(query_out, 6, NP, HID, s_qc)
                    for j in range(BT):
                        act.wait_ge(s_tk, START + n * BT + j + 1)
                        act.wait_ge(s_t_out[j], DMA_START + 16 * n)
                        act.activation(table_rows[j][:, :, 0:HID], ps[0:NP, 2:4, :].rearrange("p a (r d) -> p (a r) d", d=HID),
                                       copy).then_inc(s_tkc, 1)

            def exponentials(l, g, u, first):
                G = l * GROUPS + g
                act.wait_ge(s_diff, G + 1)
                act.activation(prob[u], score[u], ACT.Exp).then_inc(s_prob, 1)
                act.wait_ge(s_max, G + 1)
                if not first:
                    act.wait_ge(s_mt, START + G)
                act.activation(max_wide, row_max[u].unsqueeze(3).broadcast_to([P, ROW_TILES, HEADS, HS]), copy).then_inc(s_maxw, 1)

            def factors(l, g):
                G = l * GROUPS + g
                act.wait_ge(s_fac_in, START + G + 1)
                act.activation(factor, factor, ACT.Exp).then_inc(s_fac, 1)

            def sums_widened(l, g, u, first):
                G = l * GROUPS + g
                act.wait_ge(s_den, G + 1)
                if not first:
                    act.wait_ge(s_ut, START + G)
                act.activation(den_wide, row_den[u].unsqueeze(3).broadcast_to([P, ROW_TILES, HEADS, HS]), copy).then_inc(s_denw, 1)

            def rows_stored(l, g, half, u):
                G = l * GROUPS + g
                act.wait_ge(s_back, START + G + 1)
                act.wait_ge(s_row_out[u], DMA_START + 16 * (l * part_uses(u) + half))
                act.activation(out_rows[u][:, :, 0:HID], ps[:, 6, :].rearrange("p (t d) -> p t d", t=ROW_TILES), copy)
                act.activation(out_rows[u][:, :, HID:OUT_LINE],
                               ps[:, 7, 0:ROW_TILES * HEADS].rearrange("p (t d) -> p t d", t=ROW_TILES), copy).then_inc(s_row, 1)
                act.wait_ge(s_row, START + G + 1)
                act.dma_start(row_table.rearrange("(g t p) c -> g p t c", t=ROW_TILES, p=P)[ds(g, 1)].rearrange("o p t c -> (o p) t c"),
                              out_rows[u][:, :, :]).then_inc(s_row_out[u], 16)

            def edge_stage(l):
                exponentials(l, 0, 0, True)
                sums_widened(l, 0, 0, True)
                factors(l, 0)
                exponentials(l, 1, 1, False)
                sums_widened(l, 1, 1, False)
                rows_stored(l, 0, 0, 0)
                with act.Fori(0, PAIRS - 1) as i:
                    for g, before_half, u in ((2 + 2 * i, i, 0), (3 + 2 * i, i + 1, 1)):
                        factors(l, g - 1)
                        exponentials(l, g, u, False)
                        sums_widened(l, g, u, False)
                        rows_stored(l, g - 1, before_half, 1 - u)
                factors(l, GROUPS - 2)
                exponentials(l, GROUPS - 1, 0, False)
                sums_widened(l, GROUPS - 1, 0, False)
                rows_stored(l, GROUPS - 2, PAIRS - 1, 1)
                factors(l, GROUPS - 1)
                rows_stored(l, GROUPS - 1, PAIRS, 0)

            def output_stage(l):
                last = l == LAYERS - 1
                act.wait_ge(s_late_in, 16 * 4 * (l + 1))
                act.activation(skip_sig[:, :], skip_sig[:, :], ACT.Exp, scale=-1.0).then_inc(s_skip, 1)
                with act.Fori(0, NBATCH) as b:
                    n = l * NBATCH + b
                    act.wait_ge(s_at, n + 1)
                    copied_wide(emb_t[:, :].rearrange("p (t c) -> p t c", t=BT), 0, P, NP, s_atc)
                    act.wait_ge(s_y, n + 1)
                    act.activation(gate, ps[0:NP, 2:4, :].rearrange("p a c -> p (a c)")[:, 0:BT * HID].rearrange("p (t c) -> p t c", t=BT),
                                   ACT.Exp, scale=-1.0).then_inc(s_ye, 1)
                    act.wait_ge(s_var, n + 1)
                    act.activation(stats[:, 3, :], stats[:, 2, :], ACT.Sqrt).then_inc(s_sd, 1)
                    if last:
                        act.wait_ge(s_ht, b + 1)
                        copied_wide(emb_t[:, :].rearrange("p (t c) -> p t c", t=BT), 0, P, NP, s_htc)
                        act.wait_ge(s_var2, b + 1)
                        act.activation(stats[:, 3, :], stats[:, 2, :], ACT.Sqrt).then_inc(s_sd2, 1)

            for l in range(LAYERS):
                node_stage(l)
                edge_stage(l)
                output_stage(l)

        @block.vector
        def _(dve):
            own = Steps(dve, s_dve)
            chained = own.chained

            def blocks4(ap):
                return ap.rearrange("p (b k) -> p b k", k=EB)

            dve.memset(zeros[:, :], 0.0).then_inc(s_zeros, 1)
            dve.memset(rel_mats[:, :, :, :], 0.0).then_inc(s_rel, 1)
            dve.wait_ge(s_edges_in, 48)
            chained(dve.tensor_single_scalar(dst_hi_i, dst_i, 6, ALU.logical_shift_right))
            dve.tensor_copy(dst_hi, dst_hi_i).then_inc(s_dst_split, 1)
            dve.wait_ge(s_dst_split, 1)
            chained(dve.tensor_single_scalar(dst_hi_i, dst_i, LO - 1, ALU.bitwise_and))
            dve.tensor_copy(dst_lo, dst_hi_i).then_inc(s_dst_split, 1)
            dve.scalar_tensor_tensor(out=blk[:, :, 0:EB], in0=blocks4(src_i), scalar=float(RELS), in1=blocks4(ety_i),
                                     op0=ALU.mult, op1=ALU.add).then_inc(s_blocks_ready, 1)
            dve.tensor_copy(blk[:, :, EB:2 * EB], blocks4(dst_i)).then_inc(s_blocks_ready, 1)
            dve.wait_ge(s_small_in, 64)
            type_int = masked[:, :, :].rearrange("p a b -> p (a b)")[:, 0:NODES].bitcast(I32)
            chained(dve.tensor_copy(type_row[:, :], type_int))
            chained(dve.tensor_copy(type_col_f[:, :], type_col[:, :]))
            dve.wait_ge(s_const, N_CONST)
            dve.wait_ge(s_dst_split, 2)
            with dve.Fori(0, CHUNK_PAIRS) as i:
                for u in range(2):
                    dve.wait_ge(s_hist[u], START + i)
                    for digits, iota, hot, n in ((dst_hi, iota_hi, onehot_hi[u], HI), (dst_lo, iota_lo, onehot_lo[u], LO)):
                        ins = dve.tensor_tensor(hot, digits[:, ds((2 * i + u) * CHUNK, CHUNK)].unsqueeze(2).broadcast_to([EP, CHUNK, n]),
                                                iota[0:EP, :].unsqueeze(1).broadcast_to([EP, CHUNK, n]), ALU.is_equal)
                    ins.then_inc(s_hot[u], 1)

            count, incl, end, start, first_block, last_block, some, rows, rows_incl, row_end = (counts[:, k, :] for k in range(10))
            dve.wait_ge(s_pe_idx, 1)
            chained(dve.tensor_copy(count, ps[0:HI, 0, 0:LO]))
            chained(dve.tensor_tensor_scan(incl, count, count, 0.0, ALU.add, ALU.max))
            dve.tensor_copy(tot[:, 0:1], incl[:, LO - 1:LO]).then_inc(s_idx_vec, 1)
            dve.wait_ge(s_pe_idx, 2)
            chained(dve.tensor_scalar(end, incl, ps[0:HI, 1, 0:1], None, ALU.add))
            chained(dve.tensor_tensor(start, end, count, ALU.subtract))
            chained(dve.tensor_copy(counts_int[:, 0, :], start))
            chained(dve.tensor_scalar(counts_int[:, 1, :], end, -1.0, None, ALU.add))
            chained(dve.tensor_single_scalar(counts_int[:, 0:2, :], counts_int[:, 0:2, :], EB.bit_length() - 1, ALU.arith_shift_right))
            chained(dve.tensor_copy(counts[:, 4:6, :], counts_int[:, 0:2, :]))
            chained(dve.tensor_single_scalar(some, count, 0.0, ALU.is_gt))
            chained(dve.tensor_tensor(rows, last_block, first_block, ALU.subtract))
            chained(dve.tensor_tensor(rows, rows, some, ALU.mult))
            chained(dve.tensor_scalar(rows, rows, 1.0, None, ALU.add))
            chained(dve.tensor_tensor_scan(rows_incl, rows, rows, 0.0, ALU.add, ALU.max))
            dve.tensor_copy(tot[:, 1:2], rows_incl[:, LO - 1:LO]).then_inc(s_idx_vec, 1)
            dve.wait_ge(s_pe_idx, 3)
            chained(dve.tensor_scalar(row_end, rows_incl, ps[0:HI, 1, 1:2], -1.0, ALU.add, ALU.add))
            chained(dve.tensor_tensor(start, row_end, rows, ALU.subtract))
            chained(dve.tensor_scalar(start, start, 1.0, None, ALU.add))
            chained(dve.tensor_tensor(end, start, first_block, ALU.subtract))
            for k, values in enumerate((start, node_iota[:, :], end, row_end)):
                dve.tensor_copy(info_pack[:, :, k], values).then_inc(s_info_ready, 1)

            dve.wait_ge(s_marks_in, 16)
            chained(dve.tensor_copy(mark, mark_i.rearrange("p r c -> p c r")))
            for k in range(2):
                own.step(dve.tensor_tensor_scan(held[:, k, :], mark[:, k, :], mark[:, k, :], 0.0, ALU.max, ALU.max))
            own.wait()
            dve.tensor_copy(last_col, held[:, :, RC - 1]).then_inc(s_idx_vec, 1)
            chained(dve.memset(last_row, 0.0))
            dve.wait_ge(s_pe_idx, 4)
            chained(dve.tensor_copy(last_row[:, 1:P + 1], ps[0:2, 2, 0:P]))
            dve.tensor_tensor_scan(prior_row, last_row[:, 0:P], last_row[:, 0:P], 0.0, ALU.max, ALU.max).then_inc(s_idx_vec, 1)
            dve.wait_ge(s_pe_idx, 5)
            chained(dve.tensor_copy(prior_col, ps[:, 3, 0:2]))
            for k in range(2):
                own.step(dve.tensor_scalar(held[:, k, :], held[:, k, :], prior_col[:, k:k + 1], None, ALU.max))
            own.wait()
            dve.tensor_scalar(row_out[:, 0, :], held[:, 0, :], -1.0, None, ALU.add).then_inc(s_rows_ready, 1)
            dve.tensor_scalar(row_out[:, 1, :], mark[:, 0, :], 0.0, RESET, ALU.is_gt, ALU.mult).then_inc(s_rows_ready, 1)
            chained(dve.tensor_tensor(row_out[:, 2, :], row_iota[:, :], held[:, 1, :], ALU.subtract))
            dve.tensor_scalar(row_out[:, 2, :], row_out[:, 2, :], float(BLOCKS - 1), None, ALU.min).then_inc(s_rows_ready, 1)
            dve.tensor_copy(node_int, row_out[:, 0, :]).then_inc(s_rows_ready, 1)
            dve.wait_ge(s_pe_idx, 6)
            dve.tensor_copy(block_of[:, :], ps[:, 5, 0:TILES]).then_inc(s_block_of, 1)
            dve.tensor_copy(node_of[:, :], ps[:, 4, 0:TILES]).then_inc(s_block_of, 1)
            dve.tensor_scalar(tile_base[:, :], ps[:, 6, 0:TILES], part_index[:, 0:1], None, ALU.add).then_inc(s_block_of, 1)
            dve.wait_ge(s_block_of, 3)

            def masks(b, done):
                for t in range(TYPES):
                    ins = dve.scalar_tensor_tensor(out=masked[:, t, :], in0=type_row[:, ds(b * BN, BN)], scalar=float(t),
                                                   in1=emb_t[:, :], op0=ALU.is_equal, op1=ALU.mult)
                ins.then_inc(done, 1)

            def slot_part(b, u):
                tiles = ds((2 * b + u) * PART, PART)
                slots = ds((2 * b + u) * PART * EB, PART * EB)
                dve.wait_ge(s_blk_in[u], 16 * PART * (b + 1))
                dve.wait_ge(s_blk_used[u], START + b)
                dve.tensor_copy(codes[:, slots].rearrange("p (t k) -> p t k", k=EB), block_in[u][:, :, 0:EB])
                chained(dve.tensor_tensor(slot_ok[u], block_in[u][:, :, EB:2 * EB], node_of[:, tiles].unsqueeze(2).broadcast_to([P, PART, EB]), ALU.is_equal))
                dve.tensor_scalar(limit[:, slots], slot_ok[u].rearrange("p t k -> p (t k)"), 2 * OFF, -OFF, ALU.mult, ALU.add).then_inc(s_blk_used[u], 1)

            def node_stage(l):
                dve.wait_ge(s_weights_in, 16 * NODE_LOADS * (l + 1))
                chained(dve.tensor_scalar(pri_scale[:, :], pri_scale[:, :], float(HS) ** -0.5, None, ALU.mult))
                dve.tensor_tensor(rel_mats[:, 0, :, :], rel_mats[:, 0, :, :],
                                  pri_scale[:, :].unsqueeze(2).broadcast_to([P, RELS, HID]), ALU.mult).then_inc(s_rel, 1)
                with own.loop(NBATCH, 2 if l == 0 else 0) as b:
                    n = l * NBATCH + b
                    dve.wait_ge(s_etc, START + n + 1)
                    dve.wait_ge(s_q, START + n)
                    masks(b, s_mask)
                    for j in range(BT):
                        dve.wait_ge(s_tv, START + n * BT + j + 1)
                        dve.wait_ge(s_t_out[j], DMA_START + 16 * n)
                        dve.tensor_copy(table_rows[j][:, :, HID:LINE], ps[0:NP, 4:6, :].rearrange("p a (r d) -> p (a r) d", d=HID)).then_inc(s_tvc, 1)
                    if l == 0:
                        for u in range(2):
                            slot_part(b, u)

            def spreads(l, g, half, u):
                G = l * GROUPS + g
                dve.wait_ge(s_ri_in[u], 16 * (l * part_uses(u) + half + 1))
                dve.wait_ge(s_rq, START + G)
                for t in range(ROW_TILES):
                    ins = dve.tensor_scalar(spread[:, t, :], row_info[u][:, 0, t * P:(t + 1) * P],
                                            tile_base[:, ds(g * ROW_TILES + t, 1)], None, ALU.is_equal)
                ins.then_inc(s_spread, 1)

            def scores(l, g, half, u):
                G = l * GROUPS + g
                keys = lines[:, u, :, 0:HID]
                dve.wait_ge(s_kv_in[u], 16 * SLOTS * (l * part_uses(u) + half + 1))
                dve.wait_ge(s_rq, START + G + 1)
                dve.tensor_tensor(keys.rearrange("p (t k) d -> p t k d", k=EB), keys.rearrange("p (t k) d -> p t k d", k=EB),
                                  ps[:, 0, :].rearrange("p (t d) -> p t d", d=HID).unsqueeze(2).broadcast_to([P, ROW_TILES, EB, HID]),
                                  ALU.mult).then_inc(s_prod, 1)
                dve.wait_ge(s_prod, START + G + 1)
                flat = score[u].rearrange("p t k h -> p (t k) h")
                dve.tensor_reduce(flat, keys.rearrange("p s (h c) -> p s h c", c=HS), AX.X, ALU.add).then_inc(s_sum, 1)
                dve.wait_ge(s_sum, G + 1)
                dve.tensor_tensor(flat, flat, limit[:, ds(g * SLOTS, SLOTS)].unsqueeze(2).broadcast_to([P, SLOTS, HEADS]),
                                  ALU.min).then_inc(s_lim, 1)
                dve.wait_ge(s_lim, G + 1)
                dve.tensor_reduce(row_max[u], score[u].rearrange("p t k h -> p t h k"), AX.X, ALU.max).then_inc(s_mx, 1)
                dve.wait_ge(s_mx, G + 1)
                dve.tensor_scalar(row_max[u], row_max[u], FLOOR, None, ALU.max).then_inc(s_max, 1)
                dve.wait_ge(s_max, G + 1)
                dve.tensor_tensor(score[u], score[u], row_max[u].unsqueeze(2).broadcast_to([P, ROW_TILES, EB, HEADS]),
                                  ALU.subtract).then_inc(s_diff, 1)

            def running_max(l, g, u, first):
                G = l * GROUPS + g
                peak = run_max[u]
                dve.wait_ge(s_mt, START + G + 1)
                if first:
                    dve.memset(peak[:, 0:1], 0.0).then_inc(s_run, 1)
                    dve.tensor_tensor_scan(peak[:, 1:GR + 1], row_info[u][:, 1, :], ps[:, 5, :], 0.0, ALU.add, ALU.max).then_inc(s_run, 1)
                else:
                    dve.wait_ge(s_run, 2 * G)
                    dve.tensor_copy(peak[:, 0:1], run_max[1 - u][:, GR:GR + 1]).then_inc(s_run, 1)
                    dve.tensor_tensor_scan(peak[:, 1:GR + 1], row_info[u][:, 1, :], ps[:, 5, :], run_max[1 - u][:, GR:GR + 1],
                                           ALU.add, ALU.max).then_inc(s_run, 1)
                dve.wait_ge(s_run, 2 * G + 2)
                dve.wait_ge(s_sums, START + 2 * G)
                dve.tensor_tensor(factor[:, 0, :], peak[:, 0:GR], row_info[u][:, 1, :], ALU.add).then_inc(s_grow, 1)
                dve.tensor_tensor(factor[:, 1, :], ps[:, 5, :], peak[:, 1:GR + 1], ALU.subtract)
                dve.wait_ge(s_grow, G + 1)
                dve.tensor_tensor(factor[:, 0, :], factor[:, 0, :], peak[:, 1:GR + 1], ALU.subtract).then_inc(s_fac_in, 1)

            def weighted(l, g, u):
                G = l * GROUPS + g
                dve.wait_ge(s_prob, G + 1)
                dve.tensor_reduce(row_den[u], prob[u].rearrange("p t k h -> p t h k"), AX.X, ALU.add).then_inc(s_den, 1)
                for half in range(2):
                    part = slice(half * SLOTS // 2, (half + 1) * SLOTS // 2)
                    values = lines[:, u, part, HID:LINE].rearrange("p s (h c) -> p s h c", c=HS)
                    dve.tensor_tensor(values, values, prob[u].rearrange("p t k h -> p (t k) h")[:, part, :].unsqueeze(3)
                                      .broadcast_to([P, SLOTS // 2, HEADS, HS]), ALU.mult).then_inc(s_pv, 1)

            def running_sums(l, g, u, first):
                G = l * GROUPS + g
                dve.wait_ge(s_fac, G + 1)
                dve.wait_ge(s_ut, START + G + 1)
                dve.tensor_tensor(scaled, ps[:, 1 + 2 * u:3 + 2 * u, :], factor[:, 1:2, :].broadcast_to([P, 2, GR]), ALU.mult).then_inc(s_scaled, 1)
                dve.wait_ge(s_scaled, START + G + 1)
                if not first:
                    dve.wait_ge(s_back, START + G - 1)
                    dve.wait_ge(s_sums, START + 2 * G)
                for k in range(2):
                    dve.tensor_tensor_scan(run_sum[u][:, k, :], factor[:, 0, :], scaled[:, k, :],
                                           0.0 if first else run_sum[1 - u][:, k, GR - 1:GR], ALU.mult, ALU.add).then_inc(s_sums, 1)

            def edge_stage(l):
                def turn(g, half, u):
                    spreads(l, g, half, u)
                    weighted(l, g - 1, 1 - u)
                    running_sums(l, g - 2, u, False)
                    running_max(l, g - 1, 1 - u, False)
                    scores(l, g, half, u)

                spreads(l, 0, 0, 0)
                scores(l, 0, 0, 0)
                spreads(l, 1, 0, 1)
                weighted(l, 0, 0)
                running_max(l, 0, 0, True)
                scores(l, 1, 0, 1)
                spreads(l, 2, 1, 0)
                weighted(l, 1, 1)
                running_sums(l, 0, 0, True)
                running_max(l, 1, 1, False)
                scores(l, 2, 1, 0)
                with dve.Fori(0, PAIRS - 1) as i:
                    turn(3 + 2 * i, i + 1, 1)
                    turn(4 + 2 * i, i + 2, 0)
                weighted(l, GROUPS - 1, 0)
                running_sums(l, GROUPS - 2, 1, False)
                running_max(l, GROUPS - 1, 0, False)
                running_sums(l, GROUPS - 1, 0, False)

            def mean_free(t, inv):
                def per_tile(k):
                    return stats[:, k, :].unsqueeze(2).broadcast_to([NP, BT, HID])
                chained(dve.tensor_reduce(stats[:, 0, :], t, AX.X, ALU.add))
                chained(dve.tensor_scalar(stats[:, 0, :], stats[:, 0, :], 1.0 / HID, None, ALU.mult))
                chained(dve.tensor_tensor(t, t, per_tile(0), ALU.subtract))
                chained(dve.tensor_tensor(squares, t, t, ALU.mult))
                chained(dve.tensor_reduce(stats[:, 1, :], squares, AX.X, ALU.add))
                dve.tensor_scalar(stats[:, 2, :], stats[:, 1, :], 1.0 / HID, EPS, ALU.mult, ALU.add).then_inc(inv, 1)

            def output_stage(l):
                last = l == LAYERS - 1
                dve.wait_ge(s_skip, l + 1)
                chained(dve.tensor_scalar(skip_sig[:, :], skip_sig[:, :], 1.0, None, ALU.add))
                chained(dve.reciprocal(skip_sig[:, :], skip_sig[:, :]))
                chained(dve.tensor_scalar(alpha[:, :], type_col_f[:, :], 0.0, skip_sig[0:NP, 0:1], ALU.is_equal, ALU.mult))
                for t in range(1, TYPES):
                    chained(dve.tensor_scalar(alpha_part[:, :], type_col_f[:, :], float(t), skip_sig[0:NP, t:t + 1], ALU.is_equal, ALU.mult))
                    chained(dve.tensor_tensor(alpha[:, :], alpha[:, :], alpha_part[:, :], ALU.add))
                with own.loop(NBATCH, 23 if last else 15) as b:
                    n = l * NBATCH + b
                    rows_now = emb[:, ds(b * BT, BT), :]
                    dve.wait_ge(s_lr_in, 16 * BT * (n + 1))
                    chained(dve.tensor_scalar(den_inv, last_rows[:, :, HID:OUT_LINE], 1e-16, None, ALU.add))
                    chained(dve.reciprocal(den_inv, den_inv))
                    for j in range(BT):
                        ins = dve.tensor_tensor(agg[:, j, :].rearrange("p (h c) -> p h c", c=HS), last_rows[:, j, 0:HID].rearrange("p (h c) -> p h c", c=HS),
                                                den_inv[:, j, :].unsqueeze(2).broadcast_to([NP, HEADS, HS]), ALU.mult)
                    ins.then_inc(s_ag, 1)
                    dve.wait_ge(s_atc, n + 1)
                    masks(b, s_am)
                    dve.wait_ge(s_ye, n + 1)
                    chained(dve.tensor_scalar(gate, gate, 1.0, None, ALU.add))
                    chained(dve.reciprocal(gate, gate))
                    y_ps = ps[0:NP, 2:4, :].rearrange("p a c -> p (a c)")[:, 0:BT * HID].rearrange("p (t c) -> p t c", t=BT)
                    chained(dve.tensor_tensor(mixed, y_ps, gate, ALU.mult))
                    chained(dve.tensor_tensor(mixed, mixed, rows_now, ALU.subtract))
                    chained(dve.tensor_tensor(mixed, mixed, alpha[:, ds(b * BT, BT)].unsqueeze(2).broadcast_to([NP, BT, HID]), ALU.mult))
                    chained(dve.tensor_tensor(mixed, mixed, rows_now, ALU.add))
                    mean_free(mixed, s_var)
                    dve.wait_ge(s_sd, n + 1)
                    chained(dve.reciprocal(stats[:, 3, :], stats[:, 3, :]))
                    chained(dve.tensor_tensor(mixed, mixed, stats[:, 3, :].unsqueeze(2).broadcast_to([NP, BT, HID]), ALU.mult))
                    dve.tensor_tensor(mixed, mixed, gain[0:NP, :].unsqueeze(1).broadcast_to([NP, BT, HID]), ALU.mult).then_inc(s_gain, 1)
                    dve.wait_ge(s_gain, n + 1)
                    dve.tensor_tensor(current[:, :, :] if last else rows_now, mixed, shift[0:NP, :].unsqueeze(1).broadcast_to([NP, BT, HID]), ALU.add).then_inc(s_emb, 1)
                    if last:
                        dve.wait_ge(s_hy, b + 1)
                        dve.wait_ge(s_out, DMA_START + 16 * b)
                        h_ps = ps[0:NP, 4:6, :].rearrange("p a c -> p (a c)")[:, 0:BT * HID].rearrange("p (t c) -> p t c", t=BT)
                        chained(dve.tensor_tensor(result, h_ps, bff_row[0:NP, :].unsqueeze(1).broadcast_to([NP, BT, HID]), ALU.add))
                        dve.wait_ge(s_xa, 16 * (b + 1))
                        chained(dve.tensor_tensor(result, result, x_again, ALU.add))
                        mean_free(result, s_var2)
                        dve.wait_ge(s_sd2, b + 1)
                        chained(dve.reciprocal(stats[:, 3, :], stats[:, 3, :]))
                        dve.tensor_tensor(result, result, stats[:, 3, :].unsqueeze(2).broadcast_to([NP, BT, HID]), ALU.mult).then_inc(s_res, 1)

            for l in range(LAYERS):
                node_stage(l)
                edge_stage(l)
                output_stage(l)


_INS = ["x", "src", "dst", "edge_type_8", "node_type_8", "L0_gnn_Wk", "L0_gnn_Wq", "L0_gnn_Wv", "L0_gnn_Wa", "L0_gnn_pri",
        "L0_gnn_Watt", "L0_gnn_Wmsg", "L0_gnn_skip", "L0_gnn_ln_g", "L0_gnn_ln_b", "L0_gnn_Wff", "L0_gnn_bff"]


def kernel(**inputs):
    import concourse.bacc as _bacc
    from concourse.bass_utils import run_bass_kernel_spmd as _run

    nc = _bacc.Bacc("TRN2", target_bir_lowering=False, num_devices=1)
    arrays, args = {}, []
    for name in _INS:
        a = np.ascontiguousarray(inputs[name])
        arrays[f"in_{name}"] = a
        args.append(nc.dram_tensor(f"in_{name}", a.shape, mybir.dt.from_np(a.dtype), kind="ExternalInput").ap())
    args.append(nc.dram_tensor("out_nodes", (NODES, HID), F32, kind="ExternalOutput").ap())
    build(nc, *args)
    return _run(nc, [arrays], core_ids=[0]).results[0]["out_nodes"]
```

```python
from contextlib import ExitStack, contextmanager

import numpy as np

import concourse.bass as bass
from concourse import mybir

F32 = mybir.dt.float32
BF16 = mybir.dt.bfloat16
I32 = mybir.dt.int32
ALU = mybir.AluOpType
ACT = mybir.ActivationFunctionType
AX = mybir.AxisListType
ds = bass.ds

P = 128
NODES, HID = 3125, 128
EDGES = 100000
HEADS, HS = 8, 16
TYPES, RELS, LAYERS = 8, 8, 2
EPS = 1e-5

NP = 125
NT = NODES // NP
BT = 5
NBATCH = NT // BT
BN = BT * NP
KEY_CUT = 3 * NP

EP = 125
EC = EDGES // EP
EB = 4
BLOCKS = EDGES // EB

ROW_TILES = 4
GR = ROW_TILES * P
GROUPS = -(-(BLOCKS + NODES) // GR)
ROWS = GROUPS * GR
TILES = ROWS // P
SLOTS = ROW_TILES * EB
RC = ROWS // P
HALF = TILES // 2

QUAD = 4
QUADS = RC // QUAD
FIELDS = 2 * EB
PAIRS = (GROUPS - 1) // 2
assert GROUPS % 2 == 1 and RC % QUAD == 0 and 2 * TILES <= 512

CHUNK = 32
CHUNKS = EDGES // CHUNK
SAMPLES = EC // CHUNK
ST = -(-NODES // P)
assert EC % CHUNK == 0 and SAMPLES <= P

LINE = 2 * HID
OUT_LINE = HID + HEADS

OFF = 1e30
FLOOR = -1e29
RESET = -1e31


class Steps:

    def __init__(self, engine, sem):
        self.engine, self.sem, self.count, self.steps = engine, sem, 0, 0

    def step(self, instruction):
        instruction.then_inc(self.sem, 1)
        self.count = self.count + 1
        self.steps += 1

    def wait(self):
        self.engine.wait_ge(self.sem, self.count)

    def chained(self, instruction):
        self.step(instruction)
        self.wait()

    @contextmanager
    def loop(self, trips, steps_each):
        start, steps = self.count, self.steps
        with self.engine.Fori(0, trips) as i:
            self.count = start + i * steps_each
            yield i
        assert self.steps - steps == steps_each, self.steps - steps
        self.count = start + trips * steps_each


START, DMA_START = 1, 16


class Arena:

    def __init__(self, whole):
        self.whole, self.used = whole, 0

    def take(self, shape, dt=F32, rows=P):
        count = int(np.prod(shape))
        words = -(-count * (2 if dt == BF16 else 4) // 64) * 16
        ap = self.whole[0:rows, self.used:self.used + words]
        self.used += words
        if dt != F32:
            ap = ap.bitcast(dt)
        ap = ap[:, 0:count]
        if len(shape) > 1:
            names = "abcd"[:len(shape)]
            ap = ap.rearrange(f"p ({' '.join(names)}) -> p {' '.join(names)}", **dict(zip(names, shape)))
        return ap


def build(nc, x, src, dst, etype, ntype, Wk, Wq, Wv, Wa, pri, Watt, Wmsg, skip, ln_g, ln_b, Wff, bff, out):
    ctx = ExitStack()
    with ctx:
        def sb(name, shape, dt=F32):
            return ctx.enter_context(nc.sbuf_tensor(name, shape, dt))

        def sem(name):
            return ctx.enter_context(nc.semaphore(name))

        def dram(name, shape, dt=F32):
            return nc.dram_tensor(name, shape, dt, kind="Internal").ap()

        block_lines = dram("block_lines", [BLOCKS + QUAD, FIELDS], I32)
        node_info = dram("node_info", [ST * P, 4], I32)
        markers = dram("markers", [ROWS, 2], I32)
        row_node = dram("row_node", [2, ROWS])
        row_lines = dram("row_lines", [ROWS, FIELDS])
        row_node_int = dram("row_node_int", [ROWS], I32)
        query_table = dram("query_table", [NODES + P, HID])
        line_table = dram("line_table", [NODES * RELS, LINE])
        row_table = dram("row_table", [ROWS, OUT_LINE])

        ident = sb("ident", [P, P])
        zeros = sb("zeros", [P, P])
        primer = sb("primer", [1, BT + 4, 16])
        before = sb("before", [P, P])
        next_one = sb("next_one", [P, P])
        wrap_one = sb("wrap_one", [P, P])
        ones = sb("ones", [P, P])
        head_pick = sb("head_pick", [P, HEADS])
        part_index = sb("part_index", [P, 1])
        ones_bf = sb("ones_bf", [P, P], BF16)
        iota_hi = sb("iota_hi", [P, ST], BF16)
        iota_lo = sb("iota_lo", [P, P], BF16)
        node_iota = sb("node_iota", [P, ST])
        row_iota = sb("row_iota", [P, RC])

        emb = sb("emb", [NP, NT, HID])
        type_row = sb("type_row", [P, NODES])
        alpha_part = sb("alpha_part", [NP, NT])
        alpha = sb("alpha", [NP, NT])
        type_col = sb("type_col", [NP, NT], I32)
        type_col_f = sb("type_col_f", [NP, NT])
        skip_sig = sb("skip_sig", [P, TYPES])
        weights = sb("weights", [P, TYPES, 4, HID])
        rel_mats = sb("rel_mats", [P, 2, RELS, HID])
        pri_scale = sb("pri_scale", [P, RELS])
        gain = sb("gain", [P, HID])
        shift = sb("shift", [P, HID])
        wff = sb("wff", [P, HID])
        bff_row = sb("bff_row", [P, HID])
        info = sb("info", [NP, NT, 4], I32)
        node_of = sb("node_of", [P, TILES])
        tile_base = sb("tile_base", [P, TILES])
        codes = sb("codes", [P, TILES * EB], I32)
        limit = sb("limit", [P, TILES * EB])
        first_nodes = sb("first_nodes", [1, TILES], I32)

        masked = sb("masked", [P, TYPES, BN])
        current = sb("current", [NP, BT, HID])
        emb_t = sb("emb_t", [P, BN])
        kv_t = sb("kv_t", [P, 2, BN])

        lines = sb("lines", [P, 2, SLOTS, LINE])
        scratch = sb("scratch", [P, 1600])
        area = sb("area", [P, 12288])
        lines_arena = Arena(lines[:, :, :, :].rearrange("p a b c -> p (a b c)"))
        scratch_arena = Arena(scratch[:, :])
        area_arena = Arena(area[:, :])
        dst_i = lines_arena.take([EC], I32, EP)
        src_i = lines_arena.take([EC], I32, EP)
        ety_i = lines_arena.take([EC], I32, EP)
        blk = lines_arena.take([EC // EB, 2 * EB], I32, EP)
        digits_i = scratch_arena.take([2, SAMPLES], I32, EP)
        digits = scratch_arena.take([2, SAMPLES], BF16, EP)
        hi_here = scratch_arena.take([SAMPLES, ST], BF16, EP)
        hi_above = scratch_arena.take([SAMPLES, ST], BF16, EP)
        lo_above = area_arena.take([SAMPLES, P], BF16, EP)
        chunk_dst = lines_arena.take([ST, CHUNK], I32)
        starts_later = lines_arena.take([ST, CHUNK])
        area_arena.used = 0
        counts = sb("counts", [P, 10, ST])
        counts_int = sb("counts_int", [P, 2, ST], I32)
        start_of = sb("start_of", [P, ST + 1])
        chunk_i = sb("chunk_i", [P, ST], I32)
        info_pack = sb("info_pack", [P, ST, 4], I32)
        lines_arena.used = 0
        mark_i = lines_arena.take([RC, 2], I32)
        mark = lines_arena.take([2, RC])
        held = lines_arena.take([2, RC])
        row_out = lines_arena.take([3, RC])
        node_int = lines_arena.take([RC], I32)
        last_col = lines_arena.take([2])
        last_row = lines_arena.take([P + 1], F32, 2)
        prior_row = lines_arena.take([P], F32, 2)
        prior_col = lines_arena.take([2])
        tile_rows = lines_arena.take([2, P], F32, HALF)
        base_row = lines_arena.take([TILES], F32, 1)
        quad_idx = sb("quad_idx", [P, QUADS], I32)
        quad_in = lines_arena.take([QUADS, QUAD, FIELDS], I32)
        chosen = lines_arena.take([QUADS, QUAD, FIELDS])
        quad_part = lines_arena.take([QUADS, QUAD - 1, FIELDS])
        assert lines_arena.used <= 2 * SLOTS * LINE
        scratch_arena.used = 0
        quad_steps = scratch_arena.take([QUADS, QUAD - 1, FIELDS])
        quad_off = sb("quad_off", [P, 2, QUADS, QUAD - 1])
        lines_arena.used = 0
        tile_lines = lines_arena.take([2, P, FIELDS], F32, HALF)
        last_idx = sb("last_idx", [NP, BT], I32)
        table_rows = [area_arena.take([RELS, LINE], F32, NP) for _ in range(BT)]
        query_out = area_arena.take([BT, HID], F32, NP)
        area_arena.used = 0
        last_rows = area_arena.take([BT, OUT_LINE], F32, NP)
        den_inv = area_arena.take([BT, HEADS], F32, NP)
        agg = area_arena.take([BT, HID], F32, NP)
        gate = area_arena.take([BT, HID], F32, NP)
        mixed = area_arena.take([BT, HID], F32, NP)
        squares = area_arena.take([BT, HID], F32, NP)
        stats = area_arena.take([4, BT], F32, NP)
        x_again = area_arena.take([BT, HID], F32, NP)
        result = area_arena.take([BT, HID], F32, NP)
        head_t = area_arena.take([BN])
        area_arena.used = 0
        slot_idx = [sb(f"slot_idx{u}", [P, SLOTS], I32) for u in range(2)]
        window = [area_arena.take([ROW_TILES, HID]) for _ in range(2)]
        row_info = [area_arena.take([2, GR]) for _ in range(2)]
        spread = area_arena.take([ROW_TILES, P])
        score = [area_arena.take([ROW_TILES, EB, HEADS]) for _ in range(2)]
        row_max = [area_arena.take([ROW_TILES, HEADS]) for _ in range(2)]
        row_den = [area_arena.take([ROW_TILES, HEADS]) for _ in range(2)]
        prob = [area_arena.take([ROW_TILES, EB, HEADS]) for _ in range(2)]
        max_wide = area_arena.take([ROW_TILES, HEADS, HS])
        den_wide = area_arena.take([ROW_TILES, HEADS, HS])
        run_max = [area_arena.take([GR + 1]) for _ in range(2)]
        factor = area_arena.take([2, GR])
        scaled = area_arena.take([2, GR])
        run_sum = [area_arena.take([2, GR]) for _ in range(2)]
        out_rows = [sb(f"out_rows{u}", [P, ROW_TILES, OUT_LINE]) for u in range(2)]

        ps = ctx.enter_context(nc.psum_tensor("ps", [P, 8, 512], F32))

        s_const = sem("const_ready")
        s_turns = sem("gather_turns")
        s_dst_in = sem("destinations_in")
        s_edges_in = sem("sources_and_relations_in")
        s_weights_in = sem("weights_in")
        s_small_in = sem("small_in")
        s_late_in = sem("output_weights_in")
        s_emb_in = sem("emb_in")
        s_dve = sem("vector_steps")
        s_act = sem("scalar_steps")
        s_pool = sem("pool_steps")
        s_pe_idx = sem("index_products")
        s_hot = sem("sample_onehots_ready")
        s_chunk = sem("chunk_indices_ready")
        s_chunk_in = sem("chunks_in")
        s_blocks_ready = sem("block_lines_ready")
        s_blocks_out = sem("block_lines_out")
        s_info_ready = sem("node_info_ready")
        s_info_dram = sem("node_info_out")
        s_info_in = sem("node_info_in")
        s_zeros = sem("zeros_ready")
        s_zero_out = sem("markers_zeroed")
        s_marks_out = sem("markers_out")
        s_marks_in = sem("markers_in")
        s_idx_vec = sem("index_vector")
        s_rows_ready = sem("rows_ready")
        s_rows_out = sem("rows_out")
        s_rows_in = sem("rows_in")
        s_bases = sem("rows_bases_ready")
        s_quad_idx = sem("quad_indices_ready")
        s_quad_in = sem("quads_in")
        s_chosen = sem("row_lines_ready")
        s_lines_out = sem("row_lines_out")
        s_lines_in = sem("row_lines_in")
        s_codes = sem("codes_ready")
        s_rel = sem("relation_matrices_ready")
        s_et = sem("embedding_transposed")
        s_etc = sem("embedding_copied")
        s_mask = sem("masked_ready")
        s_mask_used = sem("masked_used")
        s_kt = sem("keys_values_ready")
        s_ktc = sem("keys_values_copied")
        s_q = sem("queries_ready")
        s_qc = sem("queries_copied")
        s_q_out = sem("queries_out")
        s_tk = sem("key_lines_ready")
        s_tv = sem("value_lines_ready")
        s_tkc = sem("key_lines_copied")
        s_tvc = sem("value_lines_copied")
        s_t_out = [sem(f"lines_out{j}") for j in range(BT)]
        s_pad_out = sem("query_padding_out")
        s_idx_in = [sem(f"slot_indices_in{u}") for u in range(2)]
        s_win_in = [sem(f"windows_in{u}") for u in range(2)]
        s_node_in = [sem(f"row_nodes_in{u}") for u in range(2)]
        s_reset_in = [sem(f"row_resets_in{u}") for u in range(2)]
        s_kv_in = [sem(f"gathered{u}") for u in range(2)]
        s_spread = sem("spread_ready")
        s_rq = sem("row_queries_ready")
        s_prod = sem("products_ready")
        s_sum = sem("score_sums_ready")
        s_lim = sem("scores_limited")
        s_mx = sem("slot_maximum_ready")
        s_max = sem("row_maximum_ready")
        s_diff = sem("score_differences_ready")
        s_prob = sem("probabilities_ready")
        s_maxw = sem("maximum_widened")
        s_den = sem("row_sums_ready")
        s_denw = sem("row_sums_widened")
        s_pv = sem("weighted_values_ready")
        s_half_used = [sem(f"values_summed{k}") for k in range(2)]
        s_mt = sem("maximum_transposed")
        s_ut = sem("row_totals_transposed")
        s_run = sem("running_maximum_ready")
        s_grow = sem("growth_started")
        s_fac_in = sem("factor_exponents_ready")
        s_fac = sem("factors_ready")
        s_scaled = sem("totals_scaled")
        s_sums = sem("running_sums_ready")
        s_back = sem("rows_transposed_back")
        s_row = sem("rows_copied")
        s_row_out = [sem(f"rows_out{u}") for u in range(2)]
        s_li = sem("last_indices_ready")
        s_lr_in = sem("last_rows_in")
        s_ag = sem("aggregates_ready")
        s_at = sem("aggregates_transposed")
        s_atc = sem("aggregates_copied")
        s_am = sem("masked_aggregates_ready")
        s_y = sem("outputs_ready")
        s_yu = sem("outputs_used")
        s_hu = sem("head_used")
        s_ye = sem("output_exponentials_ready")
        s_var = sem("variance_ready")
        s_sd = sem("deviation_ready")
        s_cur = sem("batch_copied")
        s_emb = sem("embedding_ready")
        s_skip = sem("skip_exponentials_ready")
        s_gain = sem("gain_applied")
        s_ht = sem("head_transposed")
        s_htc = sem("head_copied")
        s_hy = sem("head_ready")
        s_xa = sem("input_again")
        s_var2 = sem("final_variance_ready")
        s_sd2 = sem("final_deviation_ready")
        s_res = sem("result_ready")
        s_out = sem("result_out")

        N_CONST = 12
        ROW_LOADS = 3
        NODE_LOADS = 3 + 3 * HEADS

        block = ctx.enter_context(nc.Block())

        def part_uses(u):
            return PAIRS + 1 if u == 0 else PAIRS

        @block.sync
        def _(sp):
            for s in (*s_half_used, s_etc, s_tkc, s_tvc, s_qc, s_mask, s_tk, s_tv, s_et, s_q, s_rq, s_fac_in, s_ut, s_scaled, s_back, s_row, s_res, s_ag, s_emb, s_sums, s_prod, s_mt, s_at, s_atc, s_am, s_yu, s_hu, s_htc, s_hy):
                sp.sem_inc(s, START)
            for t, a, done in ((dst_i, dst, s_dst_in), (src_i, src, s_edges_in), (ety_i, etype, s_edges_in)):
                sp.dma_start(t, a.rearrange("(p c) -> p c", p=EP)).then_inc(done, 16)
            for k, s in enumerate((*s_t_out, s_q_out, *s_row_out, s_out)):
                sp.dma_start(primer[:, k, :], x[0:1, 0:16]).then_inc(s, DMA_START)
            sp.dma_start(emb[:, :, :], x.rearrange("(t p) d -> p t d", p=NP)).then_inc(s_emb_in, 16)
            type_int = masked[:, :, :].rearrange("p a b -> p (a b)")[:, 0:NODES].bitcast(I32)
            for t, a in ((type_int, ntype.partition_broadcast(P)),
                         (type_col[:, :], ntype.rearrange("(t p) -> p t", p=NP)),
                         (wff[:, :], Wff), (bff_row[:, :], bff.partition_broadcast(P))):
                with nc.allow_non_contiguous_dma("types of the nodes"):
                    sp.dma_start(t, a).then_inc(s_small_in, 16)

            def node_weights(l):
                for k, w in enumerate((Wk, Wv, Wq)):
                    sp.dma_start(weights[:, :, k, :], w[l].rearrange("t i o -> i t o")).then_inc(s_weights_in, 16)
                sp.wait_ge(s_rel, 1)
                for h in range(HEADS):
                    part = slice(h * HS, (h + 1) * HS)
                    for k, w in enumerate((Watt, Wmsg)):
                        sp.dma_start(rel_mats[part, k, :, part], w[l, h].rearrange("r i o -> i r o")).then_inc(s_weights_in, 16)
                    sp.dma_start(pri_scale[part, :], pri[l, h].partition_broadcast(HS)).then_inc(s_weights_in, 16)

            def output_weights(l):
                if l > 0:
                    sp.wait_ge(s_emb, START + NBATCH * l)
                sp.dma_start(weights[:, :, 3, :], Wa[l].rearrange("t i o -> i t o")).then_inc(s_late_in, 16)
                sp.dma_start(gain[:, :], ln_g[l].partition_broadcast(P)).then_inc(s_late_in, 16)
                sp.dma_start(shift[:, :], ln_b[l].partition_broadcast(P)).then_inc(s_late_in, 16)
                sp.dma_start(skip_sig[:, :], skip[l].partition_broadcast(P)).then_inc(s_late_in, 16)

            node_weights(0)
            output_weights(0)
            sp.wait_ge(s_zeros, 1)
            sp.dma_start(query_table[NODES:NODES + P, :], zeros[:, :]).then_inc(s_pad_out, 16)
            sp.wait_ge(s_blocks_ready, 2)
            sp.dma_start(block_lines[0:BLOCKS, :].rearrange("(p b) c -> p b c", p=EP), blk).then_inc(s_blocks_out, 16)
            sp.dma_start(block_lines[BLOCKS:BLOCKS + QUAD, :], zeros[0:QUAD, 0:FIELDS].bitcast(I32)).then_inc(s_blocks_out, 16)
            sp.dma_start(markers.rearrange("(p k r) c -> p k (r c)", p=P, k=4),
                         zeros[:, 0:RC // 2].bitcast(I32).unsqueeze(1).broadcast_to([P, 4, RC // 2])).then_inc(s_zero_out, 16)
            def node_stores(l, b):
                for j in range(BT):
                    sp.wait_ge(s_tkc, START + (l * NBATCH + b) * BT + (j + 1))
                    sp.wait_ge(s_tvc, START + (l * NBATCH + b) * BT + (j + 1))
                    sp.dma_start(line_table.rearrange("(t p r) c -> t p (r c)", p=NP, r=RELS)[ds(b * BT + j, 1)].rearrange("o p c -> p (o c)"),
                                 table_rows[j].rearrange("p r c -> p (r c)")).then_inc(s_t_out[j], 16)
                sp.wait_ge(s_qc, START + l * NBATCH + b + 1)
                sp.dma_start(query_table[0:NODES, :].rearrange("(t p) d -> p t d", p=NP)[:, ds(b * BT, BT), :],
                             query_out).then_inc(s_q_out, 16)

            def first_stores():
                node_stores(0, 0)
                sp.wait_ge(s_info_ready, 4)
                sp.dma_start(node_info.rearrange("(t p) k -> p t k", p=P), info_pack[:, :, :]).then_inc(s_info_dram, 16)
                sp.wait_ge(s_info_dram, 16)
                sp.dma_start(info[:, :, :], node_info[0:NODES, :].rearrange("(t p) k -> p t k", p=NP)).then_inc(s_info_in, 16)
                sp.wait_ge(s_marks_out, 16 * ST)
                sp.wait_ge(s_blocks_out, 32)
                sp.dma_start(mark_i, markers.rearrange("(p r) c -> p r c", p=P)).then_inc(s_marks_in, 16)
                node_stores(0, 1)
                sp.wait_ge(s_rows_ready, 3)
                sp.dma_start(row_node.rearrange("k (p r) -> p k r", p=P), row_out[:, 0:2, :]).then_inc(s_rows_out, 16)
                sp.dma_start(row_node_int.rearrange("(p r) -> p r", p=P), node_int).then_inc(s_rows_out, 16)
                sp.wait_ge(s_rows_out, 32)
                sp.dma_start(tile_rows, row_node[0].rearrange("(k q p) -> q k p", k=2, p=P)).then_inc(s_rows_in, 16)
                with nc.allow_non_contiguous_dma("first rows of the tiles"):
                    sp.dma_start(base_row, row_node[0:1, :].rearrange("o (t p) -> o t p", p=P)[:, :, 0]).then_inc(s_rows_in, 16)
                    sp.dma_start(first_nodes[:, :], row_node_int.rearrange("(o t p) -> o t p", o=1, p=P)[:, :, 0]).then_inc(s_rows_in, 16)
                node_stores(0, 2)
                node_stores(0, 3)
                sp.wait_ge(s_chosen, 1)
                sp.dma_start(row_lines.rearrange("(p r) c -> p (r c)", p=P), chosen.rearrange("p q k c -> p (q k c)")).then_inc(s_lines_out, 16)
                sp.wait_ge(s_lines_out, 16)
                sp.dma_start(tile_lines, row_lines.rearrange("(k q r) c -> q k r c", k=2, r=P)).then_inc(s_lines_in, 16)
                node_stores(0, 4)

            def edge_loads(l, g, half, u, first):
                if not first:
                    sp.wait_ge(s_prod, START + l * GROUPS + g - 1)
                sp.dma_start(slot_idx[u][:, :], codes[:, ds(g * SLOTS, SLOTS)]).then_inc(s_idx_in[u], 16)
                if not first:
                    sp.wait_ge(s_rq, START + l * GROUPS + g - 1)
                nodes, resets = (row_node[k].rearrange("(g r) -> g r", r=GR)[ds(g, 1)].rearrange("o r -> (o r)").partition_broadcast(P)
                                 for k in range(2))
                sp.dma_start(row_info[u][:, 0, :], nodes).then_inc(s_node_in[u], 16)
                for t in range(ROW_TILES):
                    node = sp.value_load(first_nodes[0:1, ds(g * ROW_TILES + t, 1)], min_val=0, max_val=NODES - 1)
                    sp.dma_start(window[u][:, t, :], query_table[ds(node, P), :]).then_inc(s_win_in[u], 16)
                if not first:
                    sp.wait_ge(s_fac_in, START + l * GROUPS + g - 1)
                sp.dma_start(row_info[u][:, 1, :], resets).then_inc(s_reset_in[u], 16)

            for l in range(LAYERS):
                if l == 0:
                    first_stores()
                else:
                    with sp.Fori(0, NBATCH) as b:
                        node_stores(l, b)
                sp.wait_ge(s_q_out, DMA_START + 16 * NBATCH * (l + 1))
                sp.wait_ge(s_pad_out, 16)
                for j in range(BT):
                    sp.wait_ge(s_t_out[j], DMA_START + 16 * NBATCH * (l + 1))
                if l == 0:
                    sp.wait_ge(s_rows_in, 16 * ROW_LOADS)
                    sp.wait_ge(s_codes, 1)
                edge_loads(l, 0, 0, 0, True)
                if l > 0:
                    output_weights(l)
                if l + 1 < LAYERS:
                    node_weights(l + 1)
                with sp.Fori(0, PAIRS) as i:
                    edge_loads(l, 1 + 2 * i, i, 1, False)
                    edge_loads(l, 2 + 2 * i, i + 1, 0, False)
            with sp.Fori(0, NBATCH) as b:
                sp.wait_ge(s_res, START + b)
                sp.wait_ge(s_lr_in, 16 * BT * (NBATCH * (LAYERS - 1) + b + 1))
                sp.dma_start(x_again, x.rearrange("(t p) d -> p t d", p=NP)[:, ds(b * BT, BT), :]).then_inc(s_xa, 16)
                sp.wait_ge(s_res, START + b + 1)
                sp.dma_start(out.rearrange("(t p) d -> p t d", p=NP)[:, ds(b * BT, BT), :], result).then_inc(s_out, 16)
            sp.wait_ge(s_out, DMA_START + 16 * NBATCH)

        @block.gpsimd
        def _(pool):
            own = Steps(pool, s_pool)

            def turn_counted():
                pool.sem_inc(s_turns, 1)

            def const(instruction):
                instruction.then_inc(s_const, 1)

            pool.iota(ident[:, :], [[1, P]], base=0, channel_multiplier=-1, allow_small_or_imprecise_dtypes=True).then_inc(s_pool, 1)
            pool.iota(before[:, :], [[1, P]], base=0, channel_multiplier=-1, allow_small_or_imprecise_dtypes=True).then_inc(s_pool, 1)
            pool.memset(head_pick[:, :], 0.0).then_inc(s_pool, 1)
            own.count = 3
            own.wait()
            const(pool.tensor_scalar(next_one[:, :], before[:, :], -1.0, None, ALU.is_equal))
            const(pool.tensor_scalar(wrap_one[:, :], before[:, :], float(P - 1), None, ALU.is_equal))
            pool.wait_ge(s_const, 2)
            const(pool.iota(iota_hi[:, :], [[1, ST]], base=0, channel_multiplier=0, allow_small_or_imprecise_dtypes=True))
            const(pool.iota(iota_lo[:, :], [[1, P]], base=0, channel_multiplier=0, allow_small_or_imprecise_dtypes=True))
            const(pool.tensor_scalar(ident[:, :], ident[:, :], 0.0, None, ALU.is_equal))
            const(pool.tensor_scalar(before[:, :], before[:, :], 0.0, None, ALU.is_gt))
            const(pool.affine_select(out=head_pick[:, :], in_=head_pick[:, :], compare_op=ALU.not_equal, fill=1.0,
                                     base=0, pattern=[[-HS, HEADS]], channel_multiplier=1))
            const(pool.iota(part_index[:, :], [[0, 1]], base=0, channel_multiplier=1, allow_small_or_imprecise_dtypes=True))
            const(pool.memset(ones[:, :], 1.0))
            const(pool.memset(ones_bf[:, :], 1.0))
            const(pool.iota(node_iota[:, :], [[P, ST]], base=0, channel_multiplier=1, allow_small_or_imprecise_dtypes=True))
            const(pool.iota(row_iota[:, :], [[1, RC]], base=0, channel_multiplier=RC, allow_small_or_imprecise_dtypes=True))
            pool.wait_ge(s_chunk, 1)
            for t in range(ST):
                pool.indirect_dma_start(out=chunk_dst[:, t, :], out_offset=None, in_=dst.rearrange("(c e) -> c e", e=CHUNK),
                                        in_offset=bass.IndirectOffsetOnAxis(ap=chunk_i[:, t:t + 1], axis=0)).then_inc(s_chunk_in, 16)
            pool.wait_ge(s_info_ready, 4)
            pool.wait_ge(s_zero_out, 16)
            for t in range(ST):
                n = min(P, NODES - t * P)
                pool.indirect_dma_start(out=markers, out_offset=bass.IndirectOffsetOnAxis(ap=info_pack[0:n, t, 0:1], axis=0),
                                        in_=info_pack[0:n, t, 1:3], in_offset=None).then_inc(s_marks_out, 16)
            pool.wait_ge(s_blocks_out, 32)
            pool.wait_ge(s_quad_idx, 1)
            for t in range(QUADS):
                pool.indirect_dma_start(out=quad_in[:, t, :, :].rearrange("p k c -> p (k c)"), out_offset=None, in_=block_lines,
                                        in_offset=bass.IndirectOffsetOnAxis(ap=quad_idx[:, t:t + 1], axis=0)).then_inc(s_quad_in, 16)

            def gathers(l, g, half, u, first):
                pool.wait_ge(s_idx_in[u], 16 * (l * part_uses(u) + half + 1))
                for k in range(SLOTS):
                    if k in (0, SLOTS // 2):
                        if not first:
                            pool.wait_ge(s_half_used[k * 2 // SLOTS], START + l * GROUPS + g - 1)
                        turn_counted()
                    pool.indirect_dma_start(out=lines[:, u, k, :], out_offset=None, in_=line_table,
                                            in_offset=bass.IndirectOffsetOnAxis(ap=slot_idx[u][:, k:k + 1], axis=0)
                                            ).then_inc(s_kv_in[u], 16)

            for l in range(LAYERS):
                for j in range(BT):
                    pool.wait_ge(s_t_out[j], DMA_START + 16 * NBATCH * (l + 1))
                gathers(l, 0, 0, 0, True)
                with pool.Fori(0, PAIRS) as i:
                    gathers(l, 1 + 2 * i, i, 1, False)
                    gathers(l, 2 + 2 * i, i + 1, 0, False)
                pool.wait_ge(s_info_in, 16)
                for u in range(2):
                    pool.wait_ge(s_row_out[u], DMA_START + 16 * (l + 1) * part_uses(u))
                with pool.Fori(0, NBATCH) as b:
                    pool.wait_ge(s_ag, START + l * NBATCH + b)
                    pool.tensor_copy(last_idx[:, :], info[:, ds(b * BT, BT), 3]).then_inc(s_li, 1)
                    pool.wait_ge(s_li, l * NBATCH + b + 1)
                    turn_counted()
                    for j in range(BT):
                        pool.indirect_dma_start(out=last_rows[:, j, :], out_offset=None, in_=row_table,
                                                in_offset=bass.IndirectOffsetOnAxis(ap=last_idx[:, j:j + 1], axis=0)
                                                ).then_inc(s_lr_in, 16)

        @block.tensor
        def _(pe):
            def bank(k, rows, a, b):
                return ps[0:rows, k, a:b]

            def wide(k, rows, a, b):
                return bank(k + a // 512, rows, a % 512, (b - 1) % 512 + 1)

            pe.wait_ge(s_const, N_CONST)
            pe.wait_ge(s_hot, 1)
            for j in range(SAMPLES):
                pe.matmul(bank(0, P, 0, ST), ones_bf[0:EP, :], hi_above[:, j, :], start=(j == 0), stop=False)
                mm = pe.matmul(bank(0, P, 0, ST), lo_above[:, j, :], hi_here[:, j, :], start=False, stop=(j == SAMPLES - 1))
            mm.then_inc(s_pe_idx, 1)
            def nodes_indexed():
                pe.wait_ge(s_idx_vec, 1)
                pe.matmul(bank(0, P, 0, ST), next_one[:, :], start_of[:, 0:ST], start=True, stop=False)
                pe.matmul(bank(0, P, 0, ST), wrap_one[:, :], start_of[:, 1:ST + 1], start=False, stop=True).then_inc(s_pe_idx, 1)
                pe.wait_ge(s_idx_vec, 2)
                pe.matmul(bank(0, P, 0, ST), before[:, :], counts[:, 7, :], start=True, stop=True)
                pe.matmul(bank(0, P, ST, 2 * ST), ones[:, :], counts[:, 7, :], start=True, stop=True).then_inc(s_pe_idx, 1)

            def markers_carried():
                pe.wait_ge(s_idx_vec, 3)
                pe.transpose(bank(0, 2, 0, P), last_col, ident[:, :]).then_inc(s_pe_idx, 1)
                pe.wait_ge(s_idx_vec, 4)
                pe.transpose(bank(1, P, 0, 2), prior_row, ident[0:2, 0:2]).then_inc(s_pe_idx, 1)

            def rows_tiled():
                pe.wait_ge(s_rows_in, 16 * ROW_LOADS)
                for h in range(2):
                    pe.transpose(bank(0, P, h * HALF, (h + 1) * HALF), tile_rows[:, h, :], ident[0:HALF, 0:HALF])
                pe.matmul(bank(1, P, 0, TILES), ones[0:1, :], base_row, start=True, stop=True).then_inc(s_pe_idx, 1)

            def lines_tiled():
                pe.wait_ge(s_lines_in, 16)
                pe.wait_ge(s_tkc, START + NT)
                pe.wait_ge(s_tvc, START + NT)
                for f in range(FIELDS):
                    for h in range(2):
                        mm = pe.transpose(bank(2 + f // 2, P, f % 2 * TILES + h * HALF, f % 2 * TILES + (h + 1) * HALF),
                                          tile_lines[:, h, :, f], ident[0:HALF, 0:HALF])
                mm.then_inc(s_pe_idx, 1)

            def transposed(source, ready):
                for j in range(BT):
                    mm = pe.transpose(wide(0, P, j * P, j * P + NP), source[:, j, :], ident[0:NP, 0:NP])
                mm.then_inc(ready, 1)

            def node_stage(l):
                pe.wait_ge(s_rel, l + 2)
                pe.wait_ge(s_weights_in, 16 * NODE_LOADS * (l + 1))
                if l == 0:
                    pe.wait_ge(s_chunk, 1)

                def batch_transposed(b, free=None):
                    n = l * NBATCH + b
                    if free:
                        pe.wait_ge(*free)
                    pe.wait_ge(s_etc, START + n)
                    pe.wait_ge(s_cur, n + 1)
                    transposed(current, s_et)

                def turn(b, more, free=None):
                    n = l * NBATCH + b
                    pe.wait_ge(s_mask, START + n + 1)
                    pe.wait_ge(s_tkc, START + n * BT)
                    pe.wait_ge(s_tvc, START + n * BT)
                    for k in range(2):
                        for part, (lo, hi) in enumerate(((0, KEY_CUT), (KEY_CUT, BN))):
                            for t in range(TYPES):
                                mm = pe.matmul(bank(2 + 2 * k + part, P, 0, hi - lo), weights[:, t, k, :], masked[:, t, lo:hi],
                                               start=(t == 0), stop=(t == TYPES - 1))
                        mm.then_inc(s_kt, 1)
                    pe.wait_ge(s_qc, START + n)
                    for j in range(BT):
                        for t in range(TYPES):
                            mm = pe.matmul(wide(6, NP, j * HID, (j + 1) * HID), masked[:, t, j * NP:(j + 1) * NP], weights[:, t, 2, :],
                                           start=(t == 0), stop=(t == TYPES - 1))
                    mm.then_inc(s_q, 1)
                    if more:
                        batch_transposed(b + 1, free)
                    pe.wait_ge(s_ktc, 2 * n + 2)
                    for j in range(BT):
                        for k, (ready, copied) in enumerate(((s_tk, s_tkc), (s_tv, s_tvc))):
                            pe.wait_ge(copied, START + n * BT + j)
                            for half in range(2):
                                mm = pe.matmul(bank(2 + 2 * k + half, NP, 0, 512), kv_t[:, k, j * NP:(j + 1) * NP],
                                               rel_mats[:, k, half * 4:half * 4 + 4, :].rearrange("p r d -> p (r d)"), start=True, stop=True)
                            mm.then_inc(ready, 1)

                batch_transposed(0)
                if l == 0:
                    turn(0, True)
                    pe.wait_ge(s_etc, START + 2)
                    nodes_indexed()
                    turn(1, True, (s_info_ready, 4))
                    pe.wait_ge(s_etc, START + 3)
                    markers_carried()
                    turn(2, True, (s_rows_ready, 3))
                    pe.wait_ge(s_etc, START + 4)
                    rows_tiled()
                    turn(3, True, (s_bases, 2))
                    turn(4, False)
                    lines_tiled()
                else:
                    with pe.Fori(0, NBATCH - 1) as b:
                        turn(b, True)
                    turn(NBATCH - 1, False)

            def row_queries(l, g, half, u):
                pe.wait_ge(s_win_in[u], 16 * ROW_TILES * (l * part_uses(u) + half + 1))
                pe.wait_ge(s_spread, l * GROUPS + g + 1)
                pe.wait_ge(s_prod, START + l * GROUPS + g)
                for t in range(ROW_TILES):
                    mm = pe.matmul(bank(0, P, t * P, (t + 1) * P), spread[:, t, :], window[u][:, t, :], start=True, stop=True)
                mm.then_inc(s_rq, 1)

            def transposes(l, g, u, first):
                G = l * GROUPS + g
                pe.wait_ge(s_maxw, G + 1)
                if not first:
                    pe.wait_ge(s_fac_in, START + G)
                for t in range(ROW_TILES):
                    mm = pe.transpose(bank(5, P, t * P, (t + 1) * P), max_wide[:, t, :, :].rearrange("p h c -> p (h c)"), ident[:, :])
                mm.then_inc(s_mt, 1)
                if not first:
                    pe.wait_ge(s_scaled, START + G - 1)
                for half in range(2):
                    pe.wait_ge(s_pv, 2 * G + half + 1)
                    for t in range(half * ROW_TILES // 2, (half + 1) * ROW_TILES // 2):
                        for k in range(EB):
                            mm = pe.matmul(bank(1 + 2 * u, P, t * P, (t + 1) * P), lines[:, u, t * EB + k, HID:LINE], ident[:, :],
                                           start=(k == 0), stop=(k == EB - 1))
                    mm.then_inc(s_half_used[half], 1)
                pe.wait_ge(s_denw, G + 1)
                for t in range(ROW_TILES):
                    mm = pe.transpose(bank(2 + 2 * u, P, t * P, (t + 1) * P), den_wide[:, t, :, :].rearrange("p h c -> p (h c)"), ident[:, :])
                mm.then_inc(s_ut, 1)

            def back(l, g, u, first):
                G = l * GROUPS + g
                pe.wait_ge(s_sums, START + 2 * G + 2)
                if not first:
                    pe.wait_ge(s_row, START + G)
                for t in range(ROW_TILES):
                    pe.transpose(bank(6, P, t * P, (t + 1) * P), run_sum[u][:, 0, t * P:(t + 1) * P], ident[:, :])
                for t in range(ROW_TILES):
                    mm = pe.matmul(bank(7, P, t * HEADS, (t + 1) * HEADS), run_sum[u][:, 1, t * P:(t + 1) * P], head_pick[:, :], start=True, stop=True)
                mm.then_inc(s_back, 1)

            def edge_stage(l):
                pe.wait_ge(s_tkc, START + NT * (l + 1))
                pe.wait_ge(s_tvc, START + NT * (l + 1))
                pe.wait_ge(s_qc, START + NBATCH * (l + 1))
                pe.wait_ge(s_codes, 1)
                row_queries(l, 0, 0, 0)
                row_queries(l, 1, 0, 1)
                transposes(l, 0, 0, True)
                with pe.Fori(0, PAIRS - 1) as i:
                    for g, half, u in ((2 + 2 * i, i + 1, 0), (3 + 2 * i, i + 1, 1)):
                        row_queries(l, g, half, u)
                        transposes(l, g - 1, 1 - u, False)
                        back(l, g - 2, u, False)
                row_queries(l, GROUPS - 1, PAIRS, 0)
                transposes(l, GROUPS - 2, 1, False)
                back(l, GROUPS - 3, 0, False)
                transposes(l, GROUPS - 1, 0, False)
                back(l, GROUPS - 2, 1, False)
                back(l, GROUPS - 1, 0, False)

            def output_stage(l):
                last = l == LAYERS - 1
                pe.wait_ge(s_row, START + GROUPS * (l + 1))
                pe.wait_ge(s_late_in, 16 * 4 * (l + 1))
                def aggregates(b):
                    n = l * NBATCH + b
                    pe.wait_ge(s_ag, START + n + 1)
                    pe.wait_ge(s_atc, START + n)
                    transposed(agg, s_at)

                def outputs(b):
                    n = l * NBATCH + b
                    pe.wait_ge(s_am, START + n + 1)
                    pe.wait_ge(s_yu, START + n)
                    for j in range(BT):
                        for t in range(TYPES):
                            mm = pe.matmul(wide(2, NP, j * HID, (j + 1) * HID), masked[:, t, j * NP:(j + 1) * NP], weights[:, t, 3, :],
                                           start=(t == 0), stop=(t == TYPES - 1))
                    mm.then_inc(s_y, 1)

                def head_transposed(b):
                    pe.wait_ge(s_emb, START + l * NBATCH + b + 1)
                    pe.wait_ge(s_htc, START + b)
                    for j in range(BT):
                        mm = pe.transpose(wide(6, P, j * P, j * P + NP), current[:, j, :], ident[0:NP, 0:NP])
                    mm.then_inc(s_ht, 1)

                def head(b):
                    pe.wait_ge(s_htc, START + b + 1)
                    pe.wait_ge(s_hu, START + b)
                    for j in range(BT):
                        mm = pe.matmul(wide(4, NP, j * HID, (j + 1) * HID), head_t[:, j * NP:(j + 1) * NP], wff[:, :], start=True, stop=True)
                    mm.then_inc(s_hy, 1)

                def turn(b, head_before=last):
                    if head_before:
                        head_transposed(b - 1)
                    if not (isinstance(b, int) and b + 2 >= NBATCH):
                        aggregates(b + 2)
                    if head_before:
                        head(b - 1)
                    if not (isinstance(b, int) and b + 1 >= NBATCH):
                        outputs(b + 1)

                aggregates(0)
                aggregates(1)
                outputs(0)
                turn(0, False)
                with pe.Fori(0, NBATCH - 3) as b:
                    turn(b + 1)
                turn(NBATCH - 2)
                turn(NBATCH - 1)
                if last:
                    head_transposed(NBATCH - 1)
                    head(NBATCH - 1)

            for l in range(LAYERS):
                node_stage(l)
                edge_stage(l)
                output_stage(l)

        @block.scalar
        def _(act):
            copy = ACT.Copy

            def copied_wide(dst_ap, k, rows, width, done):
                src_ap = ps[0:rows, k:k + 2, :].rearrange("p a c -> p (a c)")[:, 0:BT * P].rearrange("p (t c) -> p t c", t=BT)
                act.activation(dst_ap, src_ap[:, :, 0:width], copy).then_inc(done, 1)

            def node_stage(l):
                if l == 0:
                    act.wait_ge(s_emb_in, 16)
                act.wait_ge(s_emb, START + NBATCH * l)
                def batch_copied(b):
                    n = l * NBATCH + b
                    act.wait_ge(s_et, START + n)
                    act.activation(current[:, :, :], emb[:, ds(b * BT, BT), :], copy).then_inc(s_cur, 1)

                def transposes_copied(b):
                    n = l * NBATCH + b
                    act.wait_ge(s_et, START + n + 1)
                    act.wait_ge(s_mask, START + n)
                    copied_wide(emb_t[:, :].rearrange("p (t c) -> p t c", t=BT), 0, P, NP, s_etc)

                def turn(b, more):
                    n = l * NBATCH + b
                    if more:
                        batch_copied(b + 1)
                    act.wait_ge(s_tk, START + n * BT)
                    act.wait_ge(s_tv, START + n * BT)
                    for k in range(2):
                        act.wait_ge(s_kt, 2 * n + k + 1)
                        act.activation(kv_t[:, k, 0:KEY_CUT], ps[:, 2 + 2 * k, 0:KEY_CUT], copy)
                        act.activation(kv_t[:, k, KEY_CUT:BN], ps[:, 3 + 2 * k, 0:BN - KEY_CUT], copy).then_inc(s_ktc, 1)
                    act.wait_ge(s_q, START + n + 1)
                    act.wait_ge(s_q_out, DMA_START + 16 * n)
                    copied_wide(query_out, 6, NP, HID, s_qc)
                    if more:
                        transposes_copied(b + 1)
                    for j in range(BT):
                        act.wait_ge(s_tk, START + n * BT + j + 1)
                        act.wait_ge(s_t_out[j], DMA_START + 16 * n)
                        act.activation(table_rows[j][:, :, 0:HID], ps[0:NP, 2:4, :].rearrange("p a (r d) -> p (a r) d", d=HID),
                                       copy).then_inc(s_tkc, 1)

                batch_copied(0)
                transposes_copied(0)
                with act.Fori(0, NBATCH - 1) as b:
                    turn(b, True)
                turn(NBATCH - 1, False)

            def exponentials(l, g, u, first):
                G = l * GROUPS + g
                act.wait_ge(s_diff, G + 1)
                act.activation(prob[u], score[u], ACT.Exp).then_inc(s_prob, 1)
                act.wait_ge(s_max, G + 1)
                if not first:
                    act.wait_ge(s_mt, START + G)
                act.activation(max_wide, row_max[u].unsqueeze(3).broadcast_to([P, ROW_TILES, HEADS, HS]), copy).then_inc(s_maxw, 1)

            def factors(l, g):
                G = l * GROUPS + g
                act.wait_ge(s_fac_in, START + G + 1)
                act.activation(factor, factor, ACT.Exp).then_inc(s_fac, 1)

            def sums_widened(l, g, u, first):
                G = l * GROUPS + g
                act.wait_ge(s_den, G + 1)
                if not first:
                    act.wait_ge(s_ut, START + G)
                act.activation(den_wide, row_den[u].unsqueeze(3).broadcast_to([P, ROW_TILES, HEADS, HS]), copy).then_inc(s_denw, 1)

            def rows_stored(l, g, half, u):
                G = l * GROUPS + g
                act.wait_ge(s_back, START + G + 1)
                act.wait_ge(s_row_out[u], DMA_START + 16 * (l * part_uses(u) + half))
                act.activation(out_rows[u][:, :, 0:HID], ps[:, 6, :].rearrange("p (t d) -> p t d", t=ROW_TILES), copy)
                act.activation(out_rows[u][:, :, HID:OUT_LINE],
                               ps[:, 7, 0:ROW_TILES * HEADS].rearrange("p (t d) -> p t d", t=ROW_TILES), copy).then_inc(s_row, 1)
                act.wait_ge(s_row, START + G + 1)
                act.dma_start(row_table.rearrange("(g t p) c -> g p t c", t=ROW_TILES, p=P)[ds(g, 1)].rearrange("o p t c -> (o p) t c"),
                              out_rows[u][:, :, :]).then_inc(s_row_out[u], 16)

            def edge_stage(l):
                exponentials(l, 0, 0, True)
                sums_widened(l, 0, 0, True)
                factors(l, 0)
                exponentials(l, 1, 1, False)
                sums_widened(l, 1, 1, False)
                rows_stored(l, 0, 0, 0)
                with act.Fori(0, PAIRS - 1) as i:
                    for g, before_half, u in ((2 + 2 * i, i, 0), (3 + 2 * i, i + 1, 1)):
                        factors(l, g - 1)
                        exponentials(l, g, u, False)
                        sums_widened(l, g, u, False)
                        rows_stored(l, g - 1, before_half, 1 - u)
                factors(l, GROUPS - 2)
                exponentials(l, GROUPS - 1, 0, False)
                sums_widened(l, GROUPS - 1, 0, False)
                rows_stored(l, GROUPS - 2, PAIRS - 1, 1)
                factors(l, GROUPS - 1)
                rows_stored(l, GROUPS - 1, PAIRS, 0)

            def output_stage(l):
                last = l == LAYERS - 1
                act.wait_ge(s_late_in, 16 * 4 * (l + 1))
                act.activation(skip_sig[:, :], skip_sig[:, :], ACT.Sigmoid).then_inc(s_skip, 1)

                def aggregates(b):
                    n = l * NBATCH + b
                    act.wait_ge(s_at, START + n + 1)
                    act.wait_ge(s_am, START + n)
                    copied_wide(emb_t[:, :].rearrange("p (t c) -> p t c", t=BT), 0, P, NP, s_atc)

                def gates(b):
                    n = l * NBATCH + b
                    act.wait_ge(s_y, n + 1)
                    act.wait_ge(s_yu, START + n)
                    act.activation(gate, ps[0:NP, 2:4, :].rearrange("p a c -> p (a c)")[:, 0:BT * HID].rearrange("p (t c) -> p t c", t=BT),
                                   ACT.Sigmoid).then_inc(s_ye, 1)

                def head_copied(b):
                    act.wait_ge(s_ht, b + 1)
                    act.wait_ge(s_hy, START + b)
                    copied_wide(head_t[:, :].rearrange("p (t c) -> p t c", t=BT), 6, P, NP, s_htc)

                def root_of_result(b):
                    act.wait_ge(s_var2, b + 1)
                    act.activation(stats[:, 3, :], stats[:, 2, :], ACT.Sqrt).then_inc(s_sd2, 1)

                def turn(b, head_before=last):
                    if head_before:
                        head_copied(b - 1)
                    gates(b)
                    if not (isinstance(b, int) and b + 2 >= NBATCH):
                        aggregates(b + 2)
                    if head_before:
                        root_of_result(b - 1)
                    act.wait_ge(s_var, l * NBATCH + b + 1)
                    act.activation(stats[:, 3, :], stats[:, 2, :], ACT.Sqrt).then_inc(s_sd, 1)

                aggregates(0)
                aggregates(1)
                turn(0, False)
                with act.Fori(0, NBATCH - 3) as b:
                    turn(b + 1)
                turn(NBATCH - 2)
                turn(NBATCH - 1)
                if last:
                    head_copied(NBATCH - 1)
                    root_of_result(NBATCH - 1)

            for l in range(LAYERS):
                node_stage(l)
                edge_stage(l)
                output_stage(l)

        @block.vector
        def _(dve):
            own = Steps(dve, s_dve)
            chained = own.chained

            def blocks4(ap):
                return ap.rearrange("p (b k) -> p b k", k=EB)

            dve.memset(zeros[:, :], 0.0).then_inc(s_zeros, 1)
            dve.memset(rel_mats[:, :, :, :], 0.0).then_inc(s_rel, 1)
            dve.wait_ge(s_dst_in, 16)
            samples = dst_i.rearrange("p (j e) -> p j e", e=CHUNK)[:, :, 0]
            own.step(dve.tensor_single_scalar(digits_i[:, 0, :], samples, P.bit_length() - 1, ALU.logical_shift_right))
            own.step(dve.tensor_single_scalar(digits_i[:, 1, :], samples, P - 1, ALU.bitwise_and))
            own.wait()
            chained(dve.tensor_copy(digits, digits_i))
            dve.wait_ge(s_const, N_CONST)
            def against(out, k, iota, n, op):
                return dve.tensor_tensor(out, iota[0:EP, :].unsqueeze(1).broadcast_to([EP, SAMPLES, n]),
                                         digits[:, k, :].unsqueeze(2).broadcast_to([EP, SAMPLES, n]), op)
            against(lo_above, 1, iota_lo, P, ALU.is_gt)
            against(hi_here, 0, iota_hi, ST, ALU.is_equal)
            against(hi_above, 0, iota_hi, ST, ALU.is_gt).then_inc(s_hot, 1)
            chunk, later, end, first_block, last_block, some, span, rows, ahead, row_start = (counts[:, k, :] for k in range(10))
            dve.wait_ge(s_pe_idx, 1)
            chained(dve.tensor_scalar(chunk, ps[:, 0, 0:ST], -1.0, 0.0, ALU.add, ALU.max))
            dve.tensor_copy(chunk_i[:, :], chunk).then_inc(s_chunk, 1)
            dve.wait_ge(s_edges_in, 32)
            dve.scalar_tensor_tensor(out=blk[:, :, 0:EB], in0=blocks4(src_i), scalar=float(RELS), in1=blocks4(ety_i),
                                     op0=ALU.mult, op1=ALU.add).then_inc(s_blocks_ready, 1)
            dve.tensor_copy(blk[:, :, EB:2 * EB], blocks4(dst_i)).then_inc(s_blocks_ready, 1)
            dve.wait_ge(s_small_in, 64)
            type_int = masked[:, :, :].rearrange("p a b -> p (a b)")[:, 0:NODES].bitcast(I32)
            chained(dve.tensor_copy(type_row[:, :], type_int))
            chained(dve.tensor_copy(type_col_f[:, :], type_col[:, :]))
            by_quad = row_out[:, 2, :].rearrange("p (q k) -> p q k", k=QUAD)

            def nodes_indexed():
                dve.wait_ge(s_chunk_in, 16 * ST)
                chained(dve.tensor_tensor(starts_later, node_iota[:, :].unsqueeze(2).broadcast_to([P, ST, CHUNK]), chunk_dst, ALU.is_gt))
                own.step(dve.memset(start_of[:, ST:ST + 1], float(EDGES)))
                chained(dve.tensor_reduce(later, starts_later, AX.X, ALU.add))
                dve.scalar_tensor_tensor(out=start_of[:, 0:ST], in0=chunk, scalar=float(CHUNK), in1=later, op0=ALU.mult, op1=ALU.add).then_inc(s_idx_vec, 1)
                dve.wait_ge(s_idx_vec, 1)
                own.step(dve.tensor_copy(counts_int[:, 0, :], start_of[:, 0:ST]))
                dve.wait_ge(s_pe_idx, 2)
                chained(dve.tensor_copy(end, ps[:, 0, 0:ST]))
                own.step(dve.tensor_scalar(counts_int[:, 1, :], end, -1.0, None, ALU.add))
                chained(dve.tensor_tensor(some, end, start_of[:, 0:ST], ALU.is_gt))
                chained(dve.tensor_single_scalar(counts_int[:, 0:2, :], counts_int[:, 0:2, :], EB.bit_length() - 1, ALU.arith_shift_right))
                chained(dve.tensor_copy(counts[:, 3:5, :], counts_int[:, 0:2, :]))
                chained(dve.tensor_tensor(span, last_block, first_block, ALU.subtract))
                chained(dve.tensor_tensor(span, span, some, ALU.mult))
                dve.tensor_scalar(rows, span, 1.0, None, ALU.add).then_inc(s_idx_vec, 1)
                dve.wait_ge(s_pe_idx, 3)
                chained(dve.tensor_copy(later, ps[:, 0, ST:2 * ST]))
                chained(dve.tensor_tensor_scan(ahead, later, later, 0.0, ALU.add, ALU.max))
                chained(dve.tensor_tensor(ahead, ahead, later, ALU.subtract))
                chained(dve.tensor_tensor(row_start, ahead, ps[:, 0, 0:ST], ALU.add))
                dve.tensor_copy(info_pack[:, :, 0], row_start).then_inc(s_info_ready, 1)
                dve.tensor_scalar(info_pack[:, :, 1], node_iota[:, :], 1.0, None, ALU.add).then_inc(s_info_ready, 1)
                dve.tensor_tensor(info_pack[:, :, 2], row_start, first_block, ALU.subtract).then_inc(s_info_ready, 1)
                dve.tensor_tensor(info_pack[:, :, 3], row_start, span, ALU.add).then_inc(s_info_ready, 1)

            def rows_indexed():
                dve.wait_ge(s_marks_in, 16)
                chained(dve.tensor_copy(mark, mark_i.rearrange("p r c -> p c r")))
                for k in range(2):
                    own.step(dve.tensor_tensor_scan(held[:, k, :], mark[:, k, :], mark[:, k, :], 0.0, ALU.max, ALU.max))
                own.wait()
                dve.tensor_copy(last_col, held[:, :, RC - 1]).then_inc(s_idx_vec, 1)
                chained(dve.memset(last_row, 0.0))
                dve.wait_ge(s_pe_idx, 4)
                chained(dve.tensor_copy(last_row[:, 1:P + 1], ps[0:2, 0, 0:P]))
                dve.tensor_tensor_scan(prior_row, last_row[:, 0:P], last_row[:, 0:P], 0.0, ALU.max, ALU.max).then_inc(s_idx_vec, 1)
                dve.wait_ge(s_pe_idx, 5)
                chained(dve.tensor_copy(prior_col, ps[:, 1, 0:2]))
                for k in range(2):
                    own.step(dve.tensor_scalar(held[:, k, :], held[:, k, :], prior_col[:, k:k + 1], None, ALU.max))
                own.wait()
                dve.tensor_scalar(row_out[:, 0, :], held[:, 0, :], -1.0, None, ALU.add).then_inc(s_rows_ready, 1)
                dve.tensor_scalar(row_out[:, 1, :], mark[:, 0, :], 0.0, RESET, ALU.is_gt, ALU.mult).then_inc(s_rows_ready, 1)
                chained(dve.tensor_tensor(row_out[:, 2, :], row_iota[:, :], held[:, 1, :], ALU.subtract))
                chained(dve.tensor_scalar(row_out[:, 2, :], row_out[:, 2, :], float(BLOCKS - 1), None, ALU.min))
                dve.tensor_copy(quad_idx[:, :], by_quad[:, :, 0]).then_inc(s_quad_idx, 1)
                dve.tensor_copy(node_int, row_out[:, 0, :]).then_inc(s_rows_ready, 1)

            def rows_tiled():
                dve.wait_ge(s_pe_idx, 6)
                dve.tensor_copy(node_of[:, :], ps[:, 0, 0:TILES]).then_inc(s_bases, 1)
                dve.tensor_scalar(tile_base[:, :], ps[:, 1, 0:TILES], part_index[:, 0:1], None, ALU.add).then_inc(s_bases, 1)

            def lines_chosen():
                own.step(dve.tensor_tensor(quad_off[:, 0, :, :], by_quad[:, :, 1:QUAD], by_quad[:, :, 0:1].broadcast_to([P, QUADS, QUAD - 1]), ALU.subtract))
                dve.wait_ge(s_quad_in, 16 * QUADS)
                own.step(dve.tensor_tensor(quad_steps, quad_in[:, :, 1:QUAD, :], quad_in[:, :, 0:QUAD - 1, :], ALU.subtract))
                own.step(dve.tensor_copy(chosen, quad_in[:, :, 0:1, :].broadcast_to([P, QUADS, QUAD, FIELDS])))
                own.wait()
                for m in range(1, QUAD):
                    n = QUAD - m
                    chained(dve.tensor_scalar(quad_off[:, 1, :, 0:n], quad_off[:, 0, :, m - 1:QUAD - 1], float(m), None, ALU.is_ge))
                    chained(dve.tensor_tensor(quad_part[:, :, 0:n, :], quad_steps[:, :, m - 1:m, :].broadcast_to([P, QUADS, n, FIELDS]),
                                              quad_off[:, 1, :, 0:n].unsqueeze(3).broadcast_to([P, QUADS, n, FIELDS]), ALU.mult))
                    last_one = dve.tensor_tensor(chosen[:, :, m:QUAD, :], chosen[:, :, m:QUAD, :], quad_part[:, :, 0:n, :], ALU.add)
                    if m < QUAD - 1:
                        chained(last_one)
                    else:
                        last_one.then_inc(s_chosen, 1)

            def lines_tiled():
                dve.wait_ge(s_pe_idx, 7)
                dve.wait_ge(s_bases, 2)
                by_slot = [t[:, :].rearrange("p (t k f) -> p k f t", k=EB // 2, f=2) for t in (codes, limit)]
                for k in range(EB // 2):
                    own.step(dve.tensor_copy(by_slot[0][:, k, :, :], ps[:, 2 + k, 0:2 * TILES].rearrange("p (f t) -> p f t", f=2)))
                    own.step(dve.tensor_tensor(by_slot[1][:, k, :, :], ps[:, 2 + EB // 2 + k, 0:2 * TILES].rearrange("p (f t) -> p f t", f=2),
                                               node_of[:, :].unsqueeze(1).broadcast_to([P, 2, TILES]), ALU.is_equal))
                own.wait()
                dve.tensor_scalar(limit[:, :], limit[:, :], 2 * OFF, -OFF, ALU.mult, ALU.add).then_inc(s_codes, 1)
                dve.wait_ge(s_codes, 1)

            def masks(b, types=range(TYPES)):
                for t in types:
                    ins = dve.scalar_tensor_tensor(out=masked[:, t, :], in0=type_row[:, ds(b * BN, BN)], scalar=float(t),
                                                   in1=emb_t[:, :], op0=ALU.is_equal, op1=ALU.mult)
                return ins

            def node_stage(l):
                dve.wait_ge(s_weights_in, 16 * NODE_LOADS * (l + 1))
                chained(dve.tensor_scalar(pri_scale[:, :], pri_scale[:, :], float(HS) ** -0.5, None, ALU.mult))
                dve.tensor_tensor(rel_mats[:, 0, :, :], rel_mats[:, 0, :, :],
                                  pri_scale[:, :].unsqueeze(2).broadcast_to([P, RELS, HID]), ALU.mult).then_inc(s_rel, 1)

                def turn(b, more):
                    n = l * NBATCH + b
                    if more:
                        dve.wait_ge(s_etc, START + n + 2)
                        dve.wait_ge(s_q, START + n + 1)
                    for j in range(BT):
                        if more and 2 * j < TYPES:
                            ins = masks(b + 1, (2 * j, 2 * j + 1))
                            if 2 * j + 2 == TYPES:
                                ins.then_inc(s_mask, 1)
                        dve.wait_ge(s_tv, START + n * BT + j + 1)
                        dve.wait_ge(s_t_out[j], DMA_START + 16 * n)
                        dve.tensor_copy(table_rows[j][:, :, HID:LINE], ps[0:NP, 4:6, :].rearrange("p a (r d) -> p (a r) d", d=HID)).then_inc(s_tvc, 1)

                dve.wait_ge(s_etc, START + l * NBATCH + 1)
                dve.wait_ge(s_q, START + l * NBATCH)
                masks(0).then_inc(s_mask, 1)
                if l == 0:
                    turn(0, True)
                    nodes_indexed()
                    turn(1, True)
                    rows_indexed()
                    turn(2, True)
                    rows_tiled()
                    turn(3, True)
                    lines_chosen()
                    turn(4, False)
                    lines_tiled()
                else:
                    with own.loop(NBATCH - 1, 0) as b:
                        turn(b, True)
                    turn(NBATCH - 1, False)

            def spreads(l, g, half, u):
                G = l * GROUPS + g
                dve.wait_ge(s_node_in[u], 16 * (l * part_uses(u) + half + 1))
                dve.wait_ge(s_rq, START + G)
                for t in range(ROW_TILES):
                    ins = dve.tensor_scalar(spread[:, t, :], row_info[u][:, 0, t * P:(t + 1) * P],
                                            tile_base[:, ds(g * ROW_TILES + t, 1)], None, ALU.is_equal)
                ins.then_inc(s_spread, 1)

            def scores(l, g, half, u):
                G = l * GROUPS + g
                keys = lines[:, u, :, 0:HID]
                dve.wait_ge(s_kv_in[u], 16 * SLOTS * (l * part_uses(u) + half + 1))
                dve.wait_ge(s_rq, START + G + 1)
                dve.tensor_tensor(keys.rearrange("p (t k) d -> p t k d", k=EB), keys.rearrange("p (t k) d -> p t k d", k=EB),
                                  ps[:, 0, :].rearrange("p (t d) -> p t d", d=HID).unsqueeze(2).broadcast_to([P, ROW_TILES, EB, HID]),
                                  ALU.mult).then_inc(s_prod, 1)
                dve.wait_ge(s_prod, START + G + 1)
                flat = score[u].rearrange("p t k h -> p (t k) h")
                dve.tensor_reduce(flat, keys.rearrange("p s (h c) -> p s h c", c=HS), AX.X, ALU.add).then_inc(s_sum, 1)
                dve.wait_ge(s_sum, G + 1)
                dve.tensor_tensor(flat, flat, limit[:, ds(g * SLOTS, SLOTS)].unsqueeze(2).broadcast_to([P, SLOTS, HEADS]),
                                  ALU.min).then_inc(s_lim, 1)
                dve.wait_ge(s_lim, G + 1)
                dve.tensor_reduce(row_max[u], score[u].rearrange("p t k h -> p t h k"), AX.X, ALU.max).then_inc(s_mx, 1)
                dve.wait_ge(s_mx, G + 1)
                dve.tensor_scalar(row_max[u], row_max[u], FLOOR, None, ALU.max).then_inc(s_max, 1)
                dve.wait_ge(s_max, G + 1)
                dve.tensor_tensor(score[u], score[u], row_max[u].unsqueeze(2).broadcast_to([P, ROW_TILES, EB, HEADS]),
                                  ALU.subtract).then_inc(s_diff, 1)

            def running_max(l, g, half, u, first):
                G = l * GROUPS + g
                peak = run_max[u]
                dve.wait_ge(s_mt, START + G + 1)
                dve.wait_ge(s_reset_in[u], 16 * (l * part_uses(u) + half + 1))
                if first:
                    dve.memset(peak[:, 0:1], 0.0).then_inc(s_run, 1)
                    dve.tensor_tensor_scan(peak[:, 1:GR + 1], row_info[u][:, 1, :], ps[:, 5, :], 0.0, ALU.add, ALU.max).then_inc(s_run, 1)
                else:
                    dve.wait_ge(s_run, 2 * G)
                    dve.tensor_copy(peak[:, 0:1], run_max[1 - u][:, GR:GR + 1]).then_inc(s_run, 1)
                    dve.tensor_tensor_scan(peak[:, 1:GR + 1], row_info[u][:, 1, :], ps[:, 5, :], run_max[1 - u][:, GR:GR + 1],
                                           ALU.add, ALU.max).then_inc(s_run, 1)
                dve.wait_ge(s_run, 2 * G + 2)
                dve.wait_ge(s_sums, START + 2 * G)
                dve.tensor_tensor(factor[:, 0, :], peak[:, 0:GR], row_info[u][:, 1, :], ALU.add).then_inc(s_grow, 1)
                dve.tensor_tensor(factor[:, 1, :], ps[:, 5, :], peak[:, 1:GR + 1], ALU.subtract)
                dve.wait_ge(s_grow, G + 1)
                dve.tensor_tensor(factor[:, 0, :], factor[:, 0, :], peak[:, 1:GR + 1], ALU.subtract).then_inc(s_fac_in, 1)

            def weighted(l, g, u):
                G = l * GROUPS + g
                dve.wait_ge(s_prob, G + 1)
                dve.tensor_reduce(row_den[u], prob[u].rearrange("p t k h -> p t h k"), AX.X, ALU.add).then_inc(s_den, 1)
                for half in range(2):
                    part = slice(half * SLOTS // 2, (half + 1) * SLOTS // 2)
                    values = lines[:, u, part, HID:LINE].rearrange("p s (h c) -> p s h c", c=HS)
                    dve.tensor_tensor(values, values, prob[u].rearrange("p t k h -> p (t k) h")[:, part, :].unsqueeze(3)
                                      .broadcast_to([P, SLOTS // 2, HEADS, HS]), ALU.mult).then_inc(s_pv, 1)

            def running_sums(l, g, u, first):
                G = l * GROUPS + g
                dve.wait_ge(s_fac, G + 1)
                dve.wait_ge(s_ut, START + G + 1)
                dve.tensor_tensor(scaled, ps[:, 1 + 2 * u:3 + 2 * u, :], factor[:, 1:2, :].broadcast_to([P, 2, GR]), ALU.mult).then_inc(s_scaled, 1)
                dve.wait_ge(s_scaled, START + G + 1)
                if not first:
                    dve.wait_ge(s_back, START + G - 1)
                    dve.wait_ge(s_sums, START + 2 * G)
                for k in range(2):
                    dve.tensor_tensor_scan(run_sum[u][:, k, :], factor[:, 0, :], scaled[:, k, :],
                                           0.0 if first else run_sum[1 - u][:, k, GR - 1:GR], ALU.mult, ALU.add).then_inc(s_sums, 1)

            def edge_stage(l):
                def turn(g, half, u):
                    spreads(l, g, half, u)
                    weighted(l, g - 1, 1 - u)
                    running_sums(l, g - 2, u, False)
                    running_max(l, g - 1, half - 1 + u, 1 - u, False)
                    scores(l, g, half, u)

                spreads(l, 0, 0, 0)
                scores(l, 0, 0, 0)
                spreads(l, 1, 0, 1)
                weighted(l, 0, 0)
                running_max(l, 0, 0, 0, True)
                scores(l, 1, 0, 1)
                spreads(l, 2, 1, 0)
                weighted(l, 1, 1)
                running_sums(l, 0, 0, True)
                running_max(l, 1, 0, 1, False)
                scores(l, 2, 1, 0)
                with dve.Fori(0, PAIRS - 1) as i:
                    turn(3 + 2 * i, i + 1, 1)
                    turn(4 + 2 * i, i + 2, 0)
                weighted(l, GROUPS - 1, 0)
                running_sums(l, GROUPS - 2, 1, False)
                running_max(l, GROUPS - 1, PAIRS, 0, False)
                running_sums(l, GROUPS - 1, 0, False)

            def mean_free(t, inv):
                def per_tile(k):
                    return stats[:, k, :].unsqueeze(2).broadcast_to([NP, BT, HID])
                chained(dve.tensor_reduce(stats[:, 0, :], t, AX.X, ALU.add))
                chained(dve.tensor_scalar(stats[:, 0, :], stats[:, 0, :], 1.0 / HID, None, ALU.mult))
                chained(dve.tensor_tensor(t, t, per_tile(0), ALU.subtract))
                chained(dve.tensor_tensor(squares, t, t, ALU.mult))
                chained(dve.tensor_reduce(stats[:, 1, :], squares, AX.X, ALU.add))
                dve.tensor_scalar(stats[:, 2, :], stats[:, 1, :], 1.0 / HID, EPS, ALU.mult, ALU.add).then_inc(inv, 1)

            def output_stage(l):
                last = l == LAYERS - 1
                dve.wait_ge(s_skip, l + 1)
                chained(dve.tensor_scalar(alpha[:, :], type_col_f[:, :], 0.0, skip_sig[0:NP, 0:1], ALU.is_equal, ALU.mult))
                for t in range(1, TYPES):
                    chained(dve.tensor_scalar(alpha_part[:, :], type_col_f[:, :], float(t), skip_sig[0:NP, t:t + 1], ALU.is_equal, ALU.mult))
                    chained(dve.tensor_tensor(alpha[:, :], alpha[:, :], alpha_part[:, :], ALU.add))

                def aggregates(b):
                    n = l * NBATCH + b
                    dve.wait_ge(s_lr_in, 16 * BT * (n + 1))
                    chained(dve.tensor_scalar(den_inv, last_rows[:, :, HID:OUT_LINE], 1e-16, None, ALU.add))
                    chained(dve.reciprocal(den_inv, den_inv))
                    dve.wait_ge(s_at, START + n)
                    for j in range(BT):
                        ins = dve.tensor_tensor(agg[:, j, :].rearrange("p (h c) -> p h c", c=HS), last_rows[:, j, 0:HID].rearrange("p (h c) -> p h c", c=HS),
                                                den_inv[:, j, :].unsqueeze(2).broadcast_to([NP, HEADS, HS]), ALU.mult)
                    ins.then_inc(s_ag, 1)

                def aggregate_masks(b):
                    n = l * NBATCH + b
                    dve.wait_ge(s_atc, START + n + 1)
                    if l > 0 or not isinstance(b, int) or b > 0:
                        dve.wait_ge(s_y, l * NBATCH + b)
                    masks(b).then_inc(s_am, 1)

                def result_of(b):
                    dve.wait_ge(s_hy, START + b + 1)
                    dve.wait_ge(s_out, DMA_START + 16 * b)
                    h_ps = ps[0:NP, 4:6, :].rearrange("p a c -> p (a c)")[:, 0:BT * HID].rearrange("p (t c) -> p t c", t=BT)
                    dve.tensor_tensor(result, h_ps, bff_row[0:NP, :].unsqueeze(1).broadcast_to([NP, BT, HID]), ALU.add).then_inc(s_hu, 1)
                    dve.wait_ge(s_hu, START + b + 1)
                    dve.wait_ge(s_xa, 16 * (b + 1))
                    chained(dve.tensor_tensor(result, result, x_again, ALU.add))
                    mean_free(result, s_var2)
                    dve.wait_ge(s_sd2, b + 1)
                    chained(dve.reciprocal(stats[:, 3, :], stats[:, 3, :]))
                    dve.tensor_tensor(result, result, stats[:, 3, :].unsqueeze(2).broadcast_to([NP, BT, HID]), ALU.mult).then_inc(s_res, 1)

                def turn(b, head_before=last):
                    n = l * NBATCH + b
                    rows_now = emb[:, ds(b * BT, BT), :]
                    dve.wait_ge(s_ye, n + 1)
                    dve.wait_ge(s_emb, START + n)
                    y_ps = ps[0:NP, 2:4, :].rearrange("p a c -> p (a c)")[:, 0:BT * HID].rearrange("p (t c) -> p t c", t=BT)
                    dve.tensor_tensor(mixed, y_ps, gate, ALU.mult).then_inc(s_yu, 1)
                    dve.wait_ge(s_yu, START + n + 1)
                    if not (isinstance(b, int) and b + 2 >= NBATCH):
                        aggregates(b + 2)
                    if not (isinstance(b, int) and b + 1 >= NBATCH):
                        aggregate_masks(b + 1)
                    if head_before:
                        result_of(b - 1)
                    chained(dve.tensor_tensor(mixed, mixed, rows_now, ALU.subtract))
                    chained(dve.tensor_tensor(mixed, mixed, alpha[:, ds(b * BT, BT)].unsqueeze(2).broadcast_to([NP, BT, HID]), ALU.mult))
                    chained(dve.tensor_tensor(mixed, mixed, rows_now, ALU.add))
                    mean_free(mixed, s_var)
                    dve.wait_ge(s_sd, n + 1)
                    chained(dve.reciprocal(stats[:, 3, :], stats[:, 3, :]))
                    chained(dve.tensor_tensor(mixed, mixed, stats[:, 3, :].unsqueeze(2).broadcast_to([NP, BT, HID]), ALU.mult))
                    dve.tensor_tensor(mixed, mixed, gain[0:NP, :].unsqueeze(1).broadcast_to([NP, BT, HID]), ALU.mult).then_inc(s_gain, 1)
                    dve.wait_ge(s_gain, n + 1)
                    if head_before:
                        dve.wait_ge(s_ht, b)
                    dve.tensor_tensor(current[:, :, :] if last else rows_now, mixed, shift[0:NP, :].unsqueeze(1).broadcast_to([NP, BT, HID]), ALU.add).then_inc(s_emb, 1)

                aggregates(0)
                aggregate_masks(0)
                aggregates(1)
                turn(0, False)
                with own.loop(NBATCH - 3, 19 if last else 12) as b:
                    turn(b + 1)
                turn(NBATCH - 2)
                turn(NBATCH - 1)
                if last:
                    result_of(NBATCH - 1)

            for l in range(LAYERS):
                node_stage(l)
                edge_stage(l)
                output_stage(l)


_INS = ["x", "src", "dst", "edge_type_8", "node_type_8", "L0_gnn_Wk", "L0_gnn_Wq", "L0_gnn_Wv", "L0_gnn_Wa", "L0_gnn_pri",
        "L0_gnn_Watt", "L0_gnn_Wmsg", "L0_gnn_skip", "L0_gnn_ln_g", "L0_gnn_ln_b", "L0_gnn_Wff", "L0_gnn_bff"]


def kernel(**inputs):
    import concourse.bacc as _bacc
    from concourse.bass_utils import run_bass_kernel_spmd as _run

    nc = _bacc.Bacc("TRN2", target_bir_lowering=False, num_devices=1)
    arrays, args = {}, []
    for name in _INS:
        a = np.ascontiguousarray(inputs[name])
        arrays[f"in_{name}"] = a
        args.append(nc.dram_tensor(f"in_{name}", a.shape, mybir.dt.from_np(a.dtype), kind="ExternalInput").ap())
    args.append(nc.dram_tensor("out_nodes", (NODES, HID), F32, kind="ExternalOutput").ap())
    build(nc, *args)
    return _run(nc, [arrays], core_ids=[0]).results[0]["out_nodes"]
```

```python
from contextlib import ExitStack, contextmanager

import numpy as np

import concourse.bass as bass
from concourse import mybir

F32 = mybir.dt.float32
BF16 = mybir.dt.bfloat16
I32 = mybir.dt.int32
ALU = mybir.AluOpType
ACT = mybir.ActivationFunctionType
AX = mybir.AxisListType
ds = bass.ds

P = 128
NODES, HID = 3125, 128
EDGES = 100000
HEADS, HS = 8, 16
TYPES, RELS, LAYERS = 8, 8, 2
EPS = 1e-5

TILES_N = (NODES + TYPES * (P - 1)) // P
BT = 4
NBATCH = TILES_N // BT
SLOTS_N = TILES_N * P
BN = BT * P
assert TILES_N % (2 * BT) == 0

NODE_LINES = RELS + 1
TABLE_NODES = NODES + SLOTS_N

EP = 125
EC = EDGES // EP
EB = 4
BLOCKS = EDGES // EB

ROW_TILES = 4
GR = ROW_TILES * P
GROUPS = -(-(BLOCKS + NODES) // GR)
ROWS = GROUPS * GR
TILES = ROWS // P
SLOTS = ROW_TILES * EB
RC = ROWS // P
HALF = TILES // 2

RUN = 5
RUNS = RC // RUN
FIELDS = 2 * EB
RUNS_EACH, RUNS_FROM = 4, 3 * BT
CHOSEN_FROM = 26
PAIRS = (GROUPS - 1) // 2
assert GROUPS % 2 == 1 and RC % RUN == 0 and 2 * TILES <= 512

CHUNK = 32
SAMPLES = EC // CHUNK
ST = -(-NODES // P)
assert EC % CHUNK == 0 and SAMPLES <= P

LINE = 2 * HID
QUERY_AT = RELS * LINE
NODE_WIDTH = QUERY_AT + HID
OUT_LINE = HID + HEADS

OFF = 1e30
FLOOR = -1e29
RESET = -1e31


class Steps:

    def __init__(self, engine, sem):
        self.engine, self.sem, self.count, self.steps = engine, sem, 0, 0

    def step(self, instruction):
        instruction.then_inc(self.sem, 1)
        self.count = self.count + 1
        self.steps += 1

    def wait(self):
        self.engine.wait_ge(self.sem, self.count)

    def chained(self, instruction):
        self.step(instruction)
        self.wait()

    @contextmanager
    def loop(self, trips, steps_each):
        start, steps = self.count, self.steps
        with self.engine.Fori(0, trips) as i:
            self.count = start + i * steps_each
            yield i
        assert self.steps - steps == steps_each, self.steps - steps
        self.count = start + trips * steps_each


START, DMA_START = 1, 16


class Arena:

    def __init__(self, whole):
        self.whole, self.used = whole, 0

    def take(self, shape, dt=F32, rows=P):
        count = int(np.prod(shape))
        words = -(-count * (2 if dt == BF16 else 4) // 64) * 16
        ap = self.whole[0:rows, self.used:self.used + words]
        self.used += words
        if dt != F32:
            ap = ap.bitcast(dt)
        ap = ap[:, 0:count]
        if len(shape) > 1:
            names = "abcd"[:len(shape)]
            ap = ap.rearrange(f"p ({' '.join(names)}) -> p {' '.join(names)}", **dict(zip(names, shape)))
        return ap


def build(nc, x, src, dst, etype, ntype, Wk, Wq, Wv, Wa, pri, Watt, Wmsg, skip, ln_g, ln_b, Wff, bff, out):
    ctx = ExitStack()
    with ctx:
        def sb(name, shape, dt=F32):
            return ctx.enter_context(nc.sbuf_tensor(name, shape, dt))

        def sem(name):
            return ctx.enter_context(nc.semaphore(name))

        def dram(name, shape, dt=F32):
            return nc.dram_tensor(name, shape, dt, kind="Internal").ap()

        block_lines = dram("block_lines", [BLOCKS + RUN, FIELDS], I32)
        x_slots = dram("x_slots", [SLOTS_N, HID + 1])
        last_table = dram("last_table", [SLOTS_N, 2], I32)
        markers = dram("markers", [ROWS, 2], I32)
        row_node = dram("row_node", [2, ROWS])
        row_lines = dram("row_lines", [ROWS, FIELDS])
        row_node_int = dram("row_node_int", [ROWS], I32)
        line_table = dram("line_table", [TABLE_NODES * NODE_LINES, LINE])
        node_lines = line_table.rearrange("(n r) c -> n (r c)", r=NODE_LINES)
        row_table = dram("row_table", [ROWS, OUT_LINE])
        out_table = dram("out_table", [TABLE_NODES, HID])

        ident = sb("ident", [P, P])
        zeros = sb("zeros", [P, P])
        primer = sb("primer", [1, 2, 16])
        before = sb("before", [P, P])
        next_one = sb("next_one", [P, P])
        wrap_one = sb("wrap_one", [P, P])
        ones = sb("ones", [P, P])
        head_pick = sb("head_pick", [P, HEADS])
        part_index = sb("part_index", [P, 1])
        ones_bf = sb("ones_bf", [P, P], BF16)
        iota_hi = sb("iota_hi", [P, ST], BF16)
        iota_lo = sb("iota_lo", [P, P], BF16)
        slot_iota = sb("slot_iota", [P, TILES_N])
        node_iota = slot_iota[:, 0:ST]
        row_iota = sb("row_iota", [P, RC])

        emb_all = sb("emb_all", [P, TILES_N, HID + 1])
        emb = emb_all[:, :, 0:HID]
        slot_node = sb("slot_node", [P, TILES_N], I32)
        slot_of = sb("slot_of", [P, ST], I32)
        last_slot = sb("last_slot", [P, TILES_N, 2], I32)
        tile_type_f = sb("tile_type_f", [P, TILES_N])
        tile_type = sb("tile_type", [1, TILES_N], I32)
        index_iota = sb("index_iota", [P, TILES_N])
        alpha_part = sb("alpha_part", [P, TILES_N])
        alpha = sb("alpha", [P, TILES_N])
        skip_sig = sb("skip_sig", [P, TYPES])
        weights = sb("weights", [P, TYPES, 4, HID])
        rel_mats = sb("rel_mats", [P, 2, RELS, HID])
        pri_scale = sb("pri_scale", [P, RELS])
        gain = sb("gain", [P, HID])
        shift = sb("shift", [P, HID])
        wff = sb("wff", [P, HID])
        bff_row = sb("bff_row", [P, HID])
        node_of = sb("node_of", [P, TILES])
        tile_base = sb("tile_base", [P, TILES])
        codes = sb("codes", [P, TILES * EB], I32)
        limit = sb("limit", [P, TILES * EB])
        first_nodes = sb("first_nodes", [1, TILES], I32)

        current = sb("current", [P, BT, HID])
        emb_t = sb("emb_t", [P, BN])
        kvq = [sb(f"kvq{u}", [P, BT, 3 * HID]) for u in range(2)]
        kv_t = [sb(f"kv_t{u}", [P, 2, BN]) for u in range(2)]

        lines = sb("lines", [P, 2, SLOTS, LINE])
        scratch = sb("scratch", [P, 1600])
        area = sb("area", [P, 12288])
        lines_arena = Arena(lines[:, :, :, :].rearrange("p a b c -> p (a b c)"))
        scratch_arena = Arena(scratch[:, :])
        area_arena = Arena(area[:, :])
        dst_i = lines_arena.take([EC], I32, EP)
        src_i = lines_arena.take([EC], I32, EP)
        ety_i = lines_arena.take([EC], I32, EP)
        blk = lines_arena.take([EC // EB, 2 * EB], I32, EP)
        digits_i = scratch_arena.take([2, SAMPLES], I32, EP)
        digits = scratch_arena.take([2, SAMPLES], BF16, EP)
        hi_here = scratch_arena.take([SAMPLES, ST], BF16, EP)
        hi_above = scratch_arena.take([SAMPLES, ST], BF16, EP)
        chunk_dst = lines_arena.take([ST, CHUNK], I32)
        starts_later = lines_arena.take([ST, CHUNK])
        x_nodes = area_arena.take([ST, HID + 1])
        area_arena.used = 0
        x_nodes_int = area_arena.take([ST, HID + 1], I32)
        lo_above = area_arena.take([SAMPLES, P], BF16, EP)
        area_arena.used = 0
        type_i = lines_arena.take([ST], I32)
        type_f = lines_arena.take([ST])
        hot = lines_arena.take([TYPES, ST])
        sums = [lines_arena.take([TYPES, ST]) for _ in range(4)]
        of_type = [lines_arena.take([TYPES]) for _ in range(4)]
        of_type_i = lines_arena.take([TYPES], I32)
        from_type = lines_arena.take([TYPES - 1, TILES_N])
        at_pad = scratch_arena.used
        pad_fill = scratch_arena.take([HID + 1])
        scratch_arena.used = at_pad
        pad_fill_int = scratch_arena.take([HID + 1], I32)
        assert lines_arena.used <= 2 * SLOTS * LINE and scratch_arena.used <= 1600
        counts = sb("counts", [P, 10, ST])
        counts_int = sb("counts_int", [P, 2, ST], I32)
        start_of = sb("start_of", [P, ST + 1])
        chunk_i = sb("chunk_i", [P, ST], I32)
        info_pack = sb("info_pack", [P, ST, 4], I32)
        lines_arena.used = 0
        mark_i = lines_arena.take([RC, 2], I32)
        mark = lines_arena.take([2, RC])
        held = lines_arena.take([2, RC])
        row_out = lines_arena.take([3, RC])
        node_int = lines_arena.take([RC], I32)
        last_col = lines_arena.take([2])
        last_row = lines_arena.take([P + 1], F32, 2)
        prior_row = lines_arena.take([P], F32, 2)
        prior_col = lines_arena.take([2])
        tile_rows = lines_arena.take([2, P], F32, HALF)
        base_row = lines_arena.take([TILES], F32, 1)
        run_idx = sb("run_idx", [P, RUNS], I32)
        run_in = lines_arena.take([RUNS, RUN, FIELDS], I32)
        chosen = lines_arena.take([RUNS, RUN, FIELDS])
        run_part = lines_arena.take([RUNS, RUN - 1, FIELDS])
        assert lines_arena.used <= 2 * SLOTS * LINE
        scratch_arena.used = 0
        run_steps = scratch_arena.take([RUNS, RUN - 1, FIELDS])
        run_off = sb("run_off", [P, 2, RUNS, RUN - 1])
        lines_arena.used = 0
        tile_lines = lines_arena.take([2, P, FIELDS], F32, HALF)
        last_idx = sb("last_idx", [P, BT], I32)
        out_idx = sb("out_idx", [P, BT], I32)
        table_rows = [area_arena.take([NODE_WIDTH]) for _ in range(BT)]
        area_arena.used = 0
        last_rows = area_arena.take([BT, OUT_LINE])
        den_inv = area_arena.take([BT, HEADS])
        agg = area_arena.take([BT, HID])
        gate = area_arena.take([BT, HID])
        mixed = area_arena.take([BT, HID])
        squares = area_arena.take([BT, HID])
        stats = area_arena.take([4, BT])
        x_again = area_arena.take([BT, HID])
        result = area_arena.take([BT, HID])
        head_t = area_arena.take([BN])
        area_arena.used = 0
        slot_idx = [sb(f"slot_idx{u}", [P, SLOTS], I32) for u in range(2)]
        window = [area_arena.take([ROW_TILES, HID]) for _ in range(2)]
        row_info = [area_arena.take([2, GR]) for _ in range(2)]
        spread = area_arena.take([ROW_TILES, P])
        score = [area_arena.take([ROW_TILES, EB, HEADS]) for _ in range(2)]
        row_max = [area_arena.take([ROW_TILES, HEADS]) for _ in range(2)]
        row_den = [area_arena.take([ROW_TILES, HEADS]) for _ in range(2)]
        prob = [area_arena.take([ROW_TILES, EB, HEADS]) for _ in range(2)]
        max_wide = area_arena.take([ROW_TILES, HEADS, HS])
        den_wide = area_arena.take([ROW_TILES, HEADS, HS])
        run_max = [area_arena.take([GR + 1]) for _ in range(2)]
        factor = area_arena.take([2, GR])
        scaled = area_arena.take([2, GR])
        run_sum = [area_arena.take([2, GR]) for _ in range(2)]
        out_rows = [sb(f"out_rows{u}", [P, ROW_TILES, OUT_LINE]) for u in range(2)]

        ps = ctx.enter_context(nc.psum_tensor("ps", [P, 8, 512], F32))

        s_const = sem("const_ready")
        s_turns = sem("gather_turns")
        s_dst_in = sem("destinations_in")
        s_edges_in = sem("sources_and_relations_in")
        s_weights_in = sem("weights_in")
        s_small_in = sem("small_in")
        s_late_in = sem("output_weights_in")
        s_emb_in = sem("emb_in")
        s_dve = sem("vector_steps")
        s_pool = sem("pool_steps")
        s_pe_idx = sem("index_products")
        s_hot = sem("sample_onehots_ready")
        s_chunk = sem("chunk_indices_ready")
        s_chunk_in = sem("chunks_in")
        s_blocks_ready = sem("block_lines_ready")
        s_blocks_out = sem("block_lines_out")
        s_info_ready = sem("node_info_ready")
        s_zeros = sem("zeros_ready")
        s_zero_out = sem("markers_zeroed")
        s_marks_out = sem("markers_out")
        s_marks_in = sem("markers_in")
        s_idx_vec = sem("index_vector")
        s_rows_ready = sem("rows_ready")
        s_rows_out = sem("rows_out")
        s_rows_in = sem("rows_in")
        s_bases = sem("rows_bases_ready")
        s_run_idx = sem("run_indices_ready")
        s_run_in = sem("runs_in")
        s_chosen = sem("row_lines_ready")
        s_lines_out = sem("row_lines_out")
        s_lines_in = sem("row_lines_in")
        s_codes = sem("codes_ready")
        s_rel = sem("relation_matrices_ready")
        s_et = sem("embedding_transposed")
        s_etc = sem("embedding_copied")
        s_kvq = sem("keys_values_queries_ready")
        s_kvqc = sem("keys_values_queries_copied")
        s_kt = sem("keys_values_transposed")
        s_kvc = sem("transposed_keys_values_copied")
        s_types_in = sem("types_in")
        s_clear = sem("types_cleared")
        s_hot_types = sem("type_onehots_ready")
        s_type_sums = sem("type_sums_ready")
        s_slot = sem("slots_ready")
        s_pads = sem("numbers_ready")
        s_x_in = sem("input_in")
        s_x_init = sem("slots_cleared")
        s_x_out = sem("input_in_slots")
        s_slot_node = sem("slot_nodes_ready")
        s_last_init = sem("last_rows_table_cleared")
        s_last_out = sem("last_rows_in_slots")
        s_last_in = sem("last_rows_table_in")
        s_copied_out = sem("output_copied")
        s_tk = sem("key_lines_ready")
        s_tv = sem("value_lines_ready")
        s_tkc = sem("key_lines_copied")
        s_tvc = sem("value_lines_copied")
        s_t_out = [sem(f"lines_out{j}") for j in range(BT)]
        s_pad_out = sem("query_padding_out")
        s_idx_in = [sem(f"slot_indices_in{u}") for u in range(2)]
        s_win_in = [sem(f"windows_in{u}") for u in range(2)]
        s_node_in = [sem(f"row_nodes_in{u}") for u in range(2)]
        s_reset_in = [sem(f"row_resets_in{u}") for u in range(2)]
        s_kv_in = [sem(f"gathered{u}") for u in range(2)]
        s_spread = sem("spread_ready")
        s_rq = sem("row_queries_ready")
        s_prod = sem("products_ready")
        s_sum = sem("score_sums_ready")
        s_lim = sem("scores_limited")
        s_mx = sem("slot_maximum_ready")
        s_max = sem("row_maximum_ready")
        s_diff = sem("score_differences_ready")
        s_prob = sem("probabilities_ready")
        s_maxw = sem("maximum_widened")
        s_den = sem("row_sums_ready")
        s_denw = sem("row_sums_widened")
        s_pv = sem("weighted_values_ready")
        s_half_used = [sem(f"values_summed{k}") for k in range(2)]
        s_mt = sem("maximum_transposed")
        s_ut = sem("row_totals_transposed")
        s_run = sem("running_maximum_ready")
        s_grow = sem("growth_started")
        s_fac_in = sem("factor_exponents_ready")
        s_fac = sem("factors_ready")
        s_scaled = sem("totals_scaled")
        s_sums = sem("running_sums_ready")
        s_back = sem("rows_transposed_back")
        s_row = sem("rows_copied")
        s_row_out = [sem(f"rows_out{u}") for u in range(2)]
        s_li = sem("last_indices_ready")
        s_oi = sem("output_indices_ready")
        s_lr_in = sem("last_rows_in")
        s_ag = sem("aggregates_ready")
        s_at = sem("aggregates_transposed")
        s_atc = sem("aggregates_copied")
        s_y = sem("outputs_ready")
        s_yu = sem("outputs_used")
        s_hu = sem("head_used")
        s_ye = sem("output_gates_ready")
        s_var = sem("variance_ready")
        s_sd = sem("deviation_ready")
        s_cur = sem("batch_copied")
        s_emb = sem("embedding_ready")
        s_skip = sem("skip_sigmoids_ready")
        s_gain = sem("gain_applied")
        s_ht = sem("head_transposed")
        s_htc = sem("head_copied")
        s_hy = sem("head_ready")
        s_xa = sem("input_again")
        s_var2 = sem("final_variance_ready")
        s_sd2 = sem("final_deviation_ready")
        s_res = sem("result_ready")
        s_out = sem("result_out")

        N_CONST = 13
        ROW_LOADS = 3
        NODE_LOADS = 3 + 3 * HEADS

        block = ctx.enter_context(nc.Block())

        def part_uses(u):
            return PAIRS + 1 if u == 0 else PAIRS

        @block.sync
        def _(sp):
            for s in (s_etc, s_tkc, s_tvc, s_tk, s_tv, s_et, s_kvq, s_kvqc, s_kvc,
                      *s_half_used, s_rq, s_fac_in, s_ut, s_scaled, s_back, s_row, s_sums, s_prod, s_mt,
                      s_y, s_res, s_ag, s_emb, s_at, s_atc, s_yu, s_hu, s_htc, s_hy):
                sp.sem_inc(s, START)
            full = NODES // P
            sp.wait_ge(s_clear, 1)
            with nc.allow_non_contiguous_dma("types of the nodes"):
                sp.dma_start(type_i[:, 0:full], ntype[0:full * P].rearrange("(t p) -> p t", p=P)).then_inc(s_types_in, 16)
                sp.dma_start(type_i[0:NODES - full * P, full:full + 1], ntype[full * P:NODES].rearrange("(p o) -> p o", o=1)).then_inc(s_types_in, 16)
            sp.dma_start(x_nodes[:, 0:full, 0:HID], x[0:full * P, :].rearrange("(t p) d -> p t d", p=P)).then_inc(s_x_in, 16)
            sp.dma_start(x_nodes[0:NODES - full * P, full, 0:HID], x[full * P:NODES, :]).then_inc(s_x_in, 16)
            sp.wait_ge(s_pads, 1)
            sp.dma_start(x_slots.rearrange("(t p) c -> p t c", p=P), pad_fill.unsqueeze(1).broadcast_to([P, TILES_N, HID + 1])).then_inc(s_x_init, 16)
            for t, a, done in ((dst_i, dst, s_dst_in), (src_i, src, s_edges_in), (ety_i, etype, s_edges_in)):
                sp.dma_start(t, a.rearrange("(p c) -> p c", p=EP)).then_inc(done, 16)
            for k, s in enumerate(s_row_out):
                sp.dma_start(primer[:, k, :], x[0:1, 0:16]).then_inc(s, DMA_START)
            for t, a in ((wff[:, :], Wff), (bff_row[:, :], bff.partition_broadcast(P))):
                sp.dma_start(t, a).then_inc(s_small_in, 16)

            def node_weights(l):
                for k, w in enumerate((Wk, Wv, Wq)):
                    sp.dma_start(weights[:, :, k, :], w[l].rearrange("t i o -> i t o")).then_inc(s_weights_in, 16)
                sp.wait_ge(s_rel, 1)
                for h in range(HEADS):
                    part = slice(h * HS, (h + 1) * HS)
                    for k, w in enumerate((Watt, Wmsg)):
                        sp.dma_start(rel_mats[part, k, :, part], w[l, h].rearrange("r i o -> i r o")).then_inc(s_weights_in, 16)
                    sp.dma_start(pri_scale[part, :], pri[l, h].partition_broadcast(HS)).then_inc(s_weights_in, 16)

            def output_weights(l):
                if l > 0:
                    sp.wait_ge(s_emb, START + NBATCH * l)
                sp.dma_start(weights[:, :, 3, :], Wa[l].rearrange("t i o -> i t o")).then_inc(s_late_in, 16)
                sp.dma_start(gain[:, :], ln_g[l].partition_broadcast(P)).then_inc(s_late_in, 16)
                sp.dma_start(shift[:, :], ln_b[l].partition_broadcast(P)).then_inc(s_late_in, 16)
                sp.dma_start(skip_sig[:, :], skip[l].partition_broadcast(P)).then_inc(s_late_in, 16)

            node_weights(0)
            output_weights(0)
            sp.wait_ge(s_zeros, 1)
            sp.dma_start(node_lines[NODES:NODES + P, QUERY_AT:NODE_WIDTH], zeros[:, :]).then_inc(s_pad_out, 16)
            sp.dma_start(node_lines[0:NODES, NODE_WIDTH:NODE_LINES * LINE].rearrange("(t p) c -> p t c", p=EP),
                         zeros[0:EP, :].unsqueeze(1).broadcast_to([EP, NODES // EP, HID])).then_inc(s_pad_out, 16)
            sp.dma_start(last_table.rearrange("(p t) c -> p (t c)", p=P), zeros[:, 0:2 * TILES_N].bitcast(I32)).then_inc(s_last_init, 16)
            sp.wait_ge(s_blocks_ready, 2)
            sp.dma_start(block_lines[0:BLOCKS, :].rearrange("(p b) c -> p b c", p=EP), blk).then_inc(s_blocks_out, 16)
            sp.dma_start(block_lines[BLOCKS:BLOCKS + RUN, :], zeros[0:RUN, 0:FIELDS].bitcast(I32)).then_inc(s_blocks_out, 16)
            sp.dma_start(markers.rearrange("(p k r) c -> p k (r c)", p=P, k=4),
                         zeros[:, 0:RC // 2].bitcast(I32).unsqueeze(1).broadcast_to([P, 4, RC // 2])).then_inc(s_zero_out, 16)

            def index_stage():
                sp.wait_ge(s_x_out, 16 * ST)
                sp.dma_start(emb_all[:, :, :], x_slots.rearrange("(t p) c -> p t c", p=P)).then_inc(s_emb_in, 16)
                sp.wait_ge(s_marks_out, 16 * ST)
                sp.wait_ge(s_blocks_out, 32)
                sp.dma_start(mark_i, markers.rearrange("(p r) c -> p r c", p=P)).then_inc(s_marks_in, 16)
                sp.wait_ge(s_rows_ready, 3)
                sp.dma_start(row_node.rearrange("k (p r) -> p k r", p=P), row_out[:, 0:2, :]).then_inc(s_rows_out, 16)
                sp.dma_start(row_node_int.rearrange("(p r) -> p r", p=P), node_int).then_inc(s_rows_out, 16)
                sp.wait_ge(s_rows_out, 32)
                sp.dma_start(tile_rows, row_node[0].rearrange("(k q p) -> q k p", k=2, p=P)).then_inc(s_rows_in, 16)
                with nc.allow_non_contiguous_dma("first rows of the tiles"):
                    sp.dma_start(base_row, row_node[0:1, :].rearrange("o (t p) -> o t p", p=P)[:, :, 0]).then_inc(s_rows_in, 16)
                    sp.dma_start(first_nodes[:, :], row_node_int.rearrange("(o t p) -> o t p", o=1, p=P)[:, :, 0]).then_inc(s_rows_in, 16)
                sp.wait_ge(s_chosen, 1)
                sp.dma_start(row_lines.rearrange("(p r) c -> p (r c)", p=P), chosen.rearrange("p q k c -> p (q k c)")).then_inc(s_lines_out, 16)
                sp.wait_ge(s_lines_out, 16)
                sp.dma_start(tile_lines, row_lines.rearrange("(k q r) c -> q k r c", k=2, r=P)).then_inc(s_lines_in, 16)

            def edge_loads(l, g, half, u, first):
                if not first:
                    sp.wait_ge(s_prod, START + l * GROUPS + g - 1)
                sp.dma_start(slot_idx[u][:, :], codes[:, ds(g * SLOTS, SLOTS)]).then_inc(s_idx_in[u], 16)
                if not first:
                    sp.wait_ge(s_rq, START + l * GROUPS + g - 1)
                nodes, resets = (row_node[k].rearrange("(g r) -> g r", r=GR)[ds(g, 1)].rearrange("o r -> (o r)").partition_broadcast(P)
                                 for k in range(2))
                sp.dma_start(row_info[u][:, 0, :], nodes).then_inc(s_node_in[u], 16)
                for t in range(ROW_TILES):
                    node = sp.value_load(first_nodes[0:1, ds(g * ROW_TILES + t, 1)], min_val=0, max_val=NODES - 1)
                    sp.dma_start(window[u][:, t, :], node_lines[ds(node, P), QUERY_AT:NODE_WIDTH]).then_inc(s_win_in[u], 16)
                if not first:
                    sp.wait_ge(s_fac_in, START + l * GROUPS + g - 1)
                sp.dma_start(row_info[u][:, 1, :], resets).then_inc(s_reset_in[u], 16)

            for l in range(LAYERS):
                if l == 0:
                    index_stage()
                sp.wait_ge(s_pad_out, 32)
                for j in range(BT):
                    sp.wait_ge(s_t_out[j], 16 * NBATCH * (l + 1))
                if l == 0:
                    sp.wait_ge(s_rows_in, 16 * ROW_LOADS)
                    sp.wait_ge(s_codes, 1)
                edge_loads(l, 0, 0, 0, True)
                if l > 0:
                    output_weights(l)
                if l + 1 < LAYERS:
                    node_weights(l + 1)
                with sp.Fori(0, PAIRS) as i:
                    edge_loads(l, 1 + 2 * i, i, 1, False)
                    edge_loads(l, 2 + 2 * i, i + 1, 0, False)
                if l == 0:
                    sp.wait_ge(s_last_out, 16 * ST)
                    sp.dma_start(last_slot[:, :, :], last_table.rearrange("(t p) c -> p t c", p=P)).then_inc(s_last_in, 16)
            with sp.Fori(0, NBATCH) as b:
                sp.wait_ge(s_res, START + b)
                sp.wait_ge(s_lr_in, 16 * BT * (NBATCH * (LAYERS - 1) + b + 1))
                sp.dma_start(x_again, x_slots.rearrange("(t p) c -> p t c", p=P)[:, ds(b * BT, BT), 0:HID]).then_inc(s_xa, 16)
            sp.wait_ge(s_out, 16 * BT * NBATCH)
            sp.dma_start(out, out_table[0:NODES, :]).then_inc(s_copied_out, 16)
            sp.wait_ge(s_copied_out, 16)

        @block.gpsimd
        def _(pool):
            own = Steps(pool, s_pool)

            def turn_counted():
                pool.sem_inc(s_turns, 1)

            def const(instruction):
                instruction.then_inc(s_const, 1)

            pool.iota(ident[:, :], [[1, P]], base=0, channel_multiplier=-1, allow_small_or_imprecise_dtypes=True).then_inc(s_pool, 1)
            pool.iota(before[:, :], [[1, P]], base=0, channel_multiplier=-1, allow_small_or_imprecise_dtypes=True).then_inc(s_pool, 1)
            pool.memset(head_pick[:, :], 0.0).then_inc(s_pool, 1)
            own.count = 3
            own.wait()
            const(pool.tensor_scalar(next_one[:, :], before[:, :], -1.0, None, ALU.is_equal))
            const(pool.tensor_scalar(wrap_one[:, :], before[:, :], float(P - 1), None, ALU.is_equal))
            pool.wait_ge(s_const, 2)
            const(pool.iota(iota_hi[:, :], [[1, ST]], base=0, channel_multiplier=0, allow_small_or_imprecise_dtypes=True))
            const(pool.iota(iota_lo[:, :], [[1, P]], base=0, channel_multiplier=0, allow_small_or_imprecise_dtypes=True))
            const(pool.tensor_scalar(ident[:, :], ident[:, :], 0.0, None, ALU.is_equal))
            const(pool.tensor_scalar(before[:, :], before[:, :], 0.0, None, ALU.is_gt))
            const(pool.affine_select(out=head_pick[:, :], in_=head_pick[:, :], compare_op=ALU.not_equal, fill=1.0,
                                     base=0, pattern=[[-HS, HEADS]], channel_multiplier=1))
            const(pool.iota(part_index[:, :], [[0, 1]], base=0, channel_multiplier=1, allow_small_or_imprecise_dtypes=True))
            const(pool.memset(ones[:, :], 1.0))
            const(pool.memset(ones_bf[:, :], 1.0))
            const(pool.iota(slot_iota[:, :], [[P, TILES_N]], base=0, channel_multiplier=1, allow_small_or_imprecise_dtypes=True))
            const(pool.iota(index_iota[:, :], [[1, TILES_N]], base=0, channel_multiplier=0, allow_small_or_imprecise_dtypes=True))
            const(pool.iota(row_iota[:, :], [[1, RC]], base=0, channel_multiplier=RC, allow_small_or_imprecise_dtypes=True))
            pool.wait_ge(s_slot, 1)
            pool.wait_ge(s_pads, 2)
            pool.wait_ge(s_x_in, 32)
            pool.wait_ge(s_x_init, 16)
            for t in range(ST):
                n = min(P, NODES - t * P)
                pool.indirect_dma_start(out=x_slots, out_offset=bass.IndirectOffsetOnAxis(ap=slot_of[0:n, t:t + 1], axis=0),
                                        in_=x_nodes[0:n, t, :], in_offset=None).then_inc(s_x_out, 16)
            pool.wait_ge(s_chunk, 1)
            for t in range(ST):
                pool.indirect_dma_start(out=chunk_dst[:, t, :], out_offset=None, in_=dst.rearrange("(c e) -> c e", e=CHUNK),
                                        in_offset=bass.IndirectOffsetOnAxis(ap=chunk_i[:, t:t + 1], axis=0)).then_inc(s_chunk_in, 16)

            def lines_stored(l, b):
                if b == 0:
                    pool.wait_ge(s_pad_out, 32)
                    pool.wait_ge(s_slot_node, 1)
                for j in range(BT):
                    pool.wait_ge(s_tkc, START + (l * NBATCH + b) * BT + j + 1)
                    pool.wait_ge(s_tvc, START + (l * NBATCH + b) * BT + j + 1)
                    pool.indirect_dma_start(out=node_lines, out_offset=bass.IndirectOffsetOnAxis(ap=slot_node[:, b * BT + j:b * BT + j + 1], axis=0),
                                            in_=table_rows[j], in_offset=None).then_inc(s_t_out[j], 16)
                    if l == 0:
                        first = (b * BT + j - RUNS_FROM) * RUNS_EACH
                        runs_gathered(max(0, first), max(0, min(first + RUNS_EACH, RUNS)))

            def markers_stored():
                pool.wait_ge(s_info_ready, 4)
                pool.wait_ge(s_zero_out, 16)
                for t in range(ST):
                    n = min(P, NODES - t * P)
                    pool.indirect_dma_start(out=markers, out_offset=bass.IndirectOffsetOnAxis(ap=info_pack[0:n, t, 0:1], axis=0),
                                            in_=info_pack[0:n, t, 1:3], in_offset=None).then_inc(s_marks_out, 16)

            def runs_gathered(first, end):
                if first < end:
                    pool.wait_ge(s_blocks_out, 32)
                    pool.wait_ge(s_run_idx, 1)
                for t in range(first, end):
                    pool.indirect_dma_start(out=run_in[:, t, :, :].rearrange("p k c -> p (k c)"), out_offset=None, in_=block_lines,
                                            in_offset=bass.IndirectOffsetOnAxis(ap=run_idx[:, t:t + 1], axis=0)).then_inc(s_run_in, 16)

            def last_rows_placed():
                pool.wait_ge(s_last_init, 16)
                for t in range(ST):
                    n = min(P, NODES - t * P)
                    pool.indirect_dma_start(out=last_table, out_offset=bass.IndirectOffsetOnAxis(ap=slot_of[0:n, t:t + 1], axis=0),
                                            in_=info_pack[0:n, t, 2:4], in_offset=None).then_inc(s_last_out, 16)

            def last_rows_gathered(l, b):
                pool.wait_ge(s_ag, START + l * NBATCH + b)
                turn_counted()
                pool.tensor_copy(last_idx[:, :], last_slot[:, ds(b * BT, BT), 1]).then_inc(s_li, 1)
                pool.wait_ge(s_li, l * NBATCH + b + 1)
                turn_counted()
                for j in range(BT):
                    pool.indirect_dma_start(out=last_rows[:, j, :], out_offset=None, in_=row_table,
                                            in_offset=bass.IndirectOffsetOnAxis(ap=last_idx[:, j:j + 1], axis=0)
                                            ).then_inc(s_lr_in, 16)

            def result_stored(b):
                pool.wait_ge(s_res, START + b + 1)
                if not isinstance(b, int) or b > 0:
                    pool.wait_ge(s_out, 16 * BT * b)
                turn_counted()
                pool.tensor_copy(out_idx[:, :], slot_node[:, ds(b * BT, BT)]).then_inc(s_oi, 1)
                pool.wait_ge(s_oi, b + 1)
                turn_counted()
                for j in range(BT):
                    pool.indirect_dma_start(out=out_table, out_offset=bass.IndirectOffsetOnAxis(ap=out_idx[:, j:j + 1], axis=0),
                                            in_=result[:, j, :], in_offset=None).then_inc(s_out, 16)

            def gathers(l, g, half, u, first):
                pool.wait_ge(s_idx_in[u], 16 * (l * part_uses(u) + half + 1))
                for k in range(SLOTS):
                    if k in (0, SLOTS // 2):
                        if not first:
                            pool.wait_ge(s_half_used[k * 2 // SLOTS], START + l * GROUPS + g - 1)
                        turn_counted()
                    pool.indirect_dma_start(out=lines[:, u, k, :], out_offset=None, in_=line_table[0:NODES * NODE_LINES, :],
                                            in_offset=bass.IndirectOffsetOnAxis(ap=slot_idx[u][:, k:k + 1], axis=0)
                                            ).then_inc(s_kv_in[u], 16)

            for l in range(LAYERS):
                for b in range(NBATCH):
                    lines_stored(l, b)
                    if l == 0 and b == 0:
                        markers_stored()
                for j in range(BT):
                    pool.wait_ge(s_t_out[j], 16 * NBATCH * (l + 1))
                gathers(l, 0, 0, 0, True)
                with pool.Fori(0, PAIRS) as i:
                    gathers(l, 1 + 2 * i, i, 1, False)
                    gathers(l, 2 + 2 * i, i + 1, 0, False)
                if l == 0:
                    last_rows_placed()
                for u in range(2):
                    pool.wait_ge(s_row_out[u], DMA_START + 16 * (l + 1) * part_uses(u))
                pool.wait_ge(s_last_in, 16)
                if l < LAYERS - 1:
                    with pool.Fori(0, NBATCH) as b:
                        last_rows_gathered(l, b)
                else:
                    for b in range(4):
                        last_rows_gathered(l, b)
                    result_stored(0)
                    last_rows_gathered(l, 4)
                    with pool.Fori(0, NBATCH - 5) as b:
                        result_stored(b + 1)
                        last_rows_gathered(l, b + 5)
                    for b in range(NBATCH - 4, NBATCH):
                        result_stored(b)

        @block.tensor
        def _(pe):
            def bank(k, rows, a, b):
                return ps[0:rows, k, a:b]

            pe.wait_ge(s_const, N_CONST)
            pe.wait_ge(s_hot_types, 1)
            every_type = hot.rearrange("p k t -> p (k t)")
            pe.matmul(bank(1, P, 0, TYPES * ST), before[:, :], every_type, start=True, stop=True)
            pe.matmul(bank(1, P, TYPES * ST, 2 * TYPES * ST), ones[:, :], every_type, start=True, stop=True).then_inc(s_type_sums, 1)
            pe.wait_ge(s_hot, 1)
            for j in range(SAMPLES):
                pe.matmul(bank(0, P, 0, ST), ones_bf[0:EP, :], hi_above[:, j, :], start=(j == 0), stop=False)
                mm = pe.matmul(bank(0, P, 0, ST), lo_above[:, j, :], hi_here[:, j, :], start=False, stop=(j == SAMPLES - 1))
            mm.then_inc(s_pe_idx, 1)

            def nodes_indexed():
                pe.wait_ge(s_idx_vec, 1)
                pe.matmul(bank(0, P, 0, ST), next_one[:, :], start_of[:, 0:ST], start=True, stop=False)
                pe.matmul(bank(0, P, 0, ST), wrap_one[:, :], start_of[:, 1:ST + 1], start=False, stop=True).then_inc(s_pe_idx, 1)
                pe.wait_ge(s_idx_vec, 2)
                pe.matmul(bank(0, P, 0, ST), before[:, :], counts[:, 7, :], start=True, stop=True)
                pe.matmul(bank(0, P, ST, 2 * ST), ones[:, :], counts[:, 7, :], start=True, stop=True).then_inc(s_pe_idx, 1)

            def markers_carried():
                pe.wait_ge(s_idx_vec, 3)
                pe.transpose(bank(0, 2, 0, P), last_col, ident[:, :]).then_inc(s_pe_idx, 1)
                pe.wait_ge(s_idx_vec, 4)
                pe.transpose(bank(1, P, 0, 2), prior_row, ident[0:2, 0:2]).then_inc(s_pe_idx, 1)

            def rows_tiled():
                pe.wait_ge(s_rows_in, 16 * ROW_LOADS)
                for h in range(2):
                    pe.transpose(bank(0, P, h * HALF, (h + 1) * HALF), tile_rows[:, h, :], ident[0:HALF, 0:HALF])
                pe.matmul(bank(1, P, 0, TILES), ones[0:1, :], base_row, start=True, stop=True).then_inc(s_pe_idx, 1)

            def lines_tiled():
                pe.wait_ge(s_lines_in, 16)
                pe.wait_ge(s_tkc, START + TILES_N)
                pe.wait_ge(s_tvc, START + TILES_N)
                for f in range(FIELDS):
                    for h in range(2):
                        mm = pe.transpose(bank(2 + f // 2, P, f % 2 * TILES + h * HALF, f % 2 * TILES + (h + 1) * HALF),
                                          tile_lines[:, h, :, f], ident[0:HALF, 0:HALF])
                mm.then_inc(s_pe_idx, 1)

            def transposed(source, ready, k=0):
                for j in range(BT):
                    mm = pe.transpose(bank(k, P, j * P, (j + 1) * P), source[:, j, :], ident[:, :])
                mm.then_inc(ready, 1)

            def type_of(b, j):
                return pe.value_load(tile_type[0:1, ds(b * BT + j, 1)], min_val=0, max_val=TYPES - 1)

            def node_stage(l):
                pe.wait_ge(s_rel, l + 2)
                pe.wait_ge(s_weights_in, 16 * NODE_LOADS * (l + 1))
                if l == 0:
                    pe.wait_ge(s_chunk, 1)
                    pe.wait_ge(s_slot, 1)
                    pe.wait_ge(s_slot_node, 1)

                def batch_transposed(b, free=None):
                    n = l * NBATCH + b
                    if free:
                        pe.wait_ge(*free)
                    pe.wait_ge(s_cur, n + 1)
                    pe.wait_ge(s_kvc, START + n)
                    transposed(current, s_et)

                def typed(b, u):
                    n = l * NBATCH + b
                    pe.wait_ge(s_etc, START + n + 1)
                    pe.wait_ge(s_kvqc, START + n)
                    for j in range(BT):
                        mm = pe.matmul(bank(j, P, 0, 3 * HID), emb_t[:, j * P:(j + 1) * P],
                                       weights[:, ds(type_of(b, j), 1), 0:3, :].rearrange("p o k d -> p (o k d)"), start=True, stop=True)
                    mm.then_inc(s_kvq, 1)

                def flipped(b, u):
                    pe.wait_ge(s_kvqc, START + l * NBATCH + b + 1)
                    for k in range(2):
                        for j in range(BT):
                            mm = pe.transpose(bank(k, P, j * P, (j + 1) * P), kvq[u][:, j, k * HID:(k + 1) * HID], ident[:, :])
                    mm.then_inc(s_kt, 1)

                def related(b, u, j):
                    n = l * NBATCH + b
                    if j == 0:
                        pe.wait_ge(s_kvc, START + n + 1)
                    for k, (ready, copied) in enumerate(((s_tk, s_tkc), (s_tv, s_tvc))):
                        pe.wait_ge(copied, START + n * BT + j)
                        for half in range(2):
                            mm = pe.matmul(bank(4 + 2 * k + half, P, 0, 512), kv_t[u][:, k, j * P:(j + 1) * P],
                                           rel_mats[:, k, half * 4:half * 4 + 4, :].rearrange("p r d -> p (r d)"), start=True, stop=True)
                        mm.then_inc(ready, 1)

                def turn(b, u, more=True, free=None):
                    if more:
                        batch_transposed(b + 1, free)
                    related(b, u, 0)
                    if more:
                        typed(b + 1, 1 - u)
                    related(b, u, 1)
                    related(b, u, 2)
                    if more:
                        flipped(b + 1, 1 - u)
                    related(b, u, 3)

                batch_transposed(0)
                typed(0, 0)
                flipped(0, 0)
                if l == 0:
                    for b in range(NBATCH):
                        turn(b, b % 2, b + 1 < NBATCH, {1: (s_info_ready, 4), 3: (s_rows_ready, 3), 4: (s_bases, 2)}.get(b))
                        if b in (0, 2, 3):
                            pe.wait_ge(s_kvc, START + b + 2)
                        if b == 0:
                            nodes_indexed()
                        if b == 2:
                            markers_carried()
                        if b == 3:
                            rows_tiled()
                    lines_tiled()
                else:
                    with pe.Fori(0, NBATCH // 2 - 1) as i:
                        for u in range(2):
                            turn(2 * i + u, u)
                    turn(NBATCH - 2, 0)
                    turn(NBATCH - 1, 1, False)

            def row_queries(l, g, half, u):
                pe.wait_ge(s_win_in[u], 16 * ROW_TILES * (l * part_uses(u) + half + 1))
                pe.wait_ge(s_spread, l * GROUPS + g + 1)
                pe.wait_ge(s_prod, START + l * GROUPS + g)
                for t in range(ROW_TILES):
                    mm = pe.matmul(bank(0, P, t * P, (t + 1) * P), spread[:, t, :], window[u][:, t, :], start=True, stop=True)
                mm.then_inc(s_rq, 1)

            def transposes(l, g, u, first):
                G = l * GROUPS + g
                pe.wait_ge(s_maxw, G + 1)
                if not first:
                    pe.wait_ge(s_fac_in, START + G)
                for t in range(ROW_TILES):
                    mm = pe.transpose(bank(5, P, t * P, (t + 1) * P), max_wide[:, t, :, :].rearrange("p h c -> p (h c)"), ident[:, :])
                mm.then_inc(s_mt, 1)
                if not first:
                    pe.wait_ge(s_scaled, START + G - 1)
                for half in range(2):
                    pe.wait_ge(s_pv, 2 * G + half + 1)
                    for t in range(half * ROW_TILES // 2, (half + 1) * ROW_TILES // 2):
                        for k in range(EB):
                            mm = pe.matmul(bank(1 + 2 * u, P, t * P, (t + 1) * P), lines[:, u, t * EB + k, HID:LINE], ident[:, :],
                                           start=(k == 0), stop=(k == EB - 1))
                    mm.then_inc(s_half_used[half], 1)
                pe.wait_ge(s_denw, G + 1)
                for t in range(ROW_TILES):
                    mm = pe.transpose(bank(2 + 2 * u, P, t * P, (t + 1) * P), den_wide[:, t, :, :].rearrange("p h c -> p (h c)"), ident[:, :])
                mm.then_inc(s_ut, 1)

            def back(l, g, u, first):
                G = l * GROUPS + g
                pe.wait_ge(s_sums, START + 2 * G + 2)
                if not first:
                    pe.wait_ge(s_row, START + G)
                for t in range(ROW_TILES):
                    pe.transpose(bank(6, P, t * P, (t + 1) * P), run_sum[u][:, 0, t * P:(t + 1) * P], ident[:, :])
                for t in range(ROW_TILES):
                    mm = pe.matmul(bank(7, P, t * HEADS, (t + 1) * HEADS), run_sum[u][:, 1, t * P:(t + 1) * P], head_pick[:, :], start=True, stop=True)
                mm.then_inc(s_back, 1)

            def edge_stage(l):
                pe.wait_ge(s_tkc, START + TILES_N * (l + 1))
                pe.wait_ge(s_tvc, START + TILES_N * (l + 1))
                pe.wait_ge(s_codes, 1)
                row_queries(l, 0, 0, 0)
                row_queries(l, 1, 0, 1)
                transposes(l, 0, 0, True)
                with pe.Fori(0, PAIRS - 1) as i:
                    for g, half, u in ((2 + 2 * i, i + 1, 0), (3 + 2 * i, i + 1, 1)):
                        row_queries(l, g, half, u)
                        transposes(l, g - 1, 1 - u, False)
                        back(l, g - 2, u, False)
                row_queries(l, GROUPS - 1, PAIRS, 0)
                transposes(l, GROUPS - 2, 1, False)
                back(l, GROUPS - 3, 0, False)
                transposes(l, GROUPS - 1, 0, False)
                back(l, GROUPS - 2, 1, False)
                back(l, GROUPS - 1, 0, False)

            def output_stage(l):
                last = l == LAYERS - 1
                pe.wait_ge(s_row, START + GROUPS * (l + 1))
                pe.wait_ge(s_late_in, 16 * 4 * (l + 1))
                def aggregates(b):
                    n = l * NBATCH + b
                    pe.wait_ge(s_ag, START + n + 1)
                    pe.wait_ge(s_atc, START + n)
                    transposed(agg, s_at)

                def outputs(b):
                    n = l * NBATCH + b
                    pe.wait_ge(s_atc, START + n + 1)
                    pe.wait_ge(s_yu, START + n)
                    for j in range(BT):
                        mm = pe.matmul(bank(2, P, j * HID, (j + 1) * HID), emb_t[:, j * P:(j + 1) * P],
                                       weights[:, ds(type_of(b, j), 1), 3, :].rearrange("p o d -> p (o d)"), start=True, stop=True)
                    mm.then_inc(s_y, 1)

                def head_transposed(b):
                    pe.wait_ge(s_emb, START + l * NBATCH + b + 1)
                    pe.wait_ge(s_htc, START + b)
                    transposed(current, s_ht, 6)

                def head(b):
                    pe.wait_ge(s_htc, START + b + 1)
                    pe.wait_ge(s_hu, START + b)
                    for j in range(BT):
                        mm = pe.matmul(bank(4, P, j * HID, (j + 1) * HID), head_t[:, j * P:(j + 1) * P], wff[:, :], start=True, stop=True)
                    mm.then_inc(s_hy, 1)

                def turn(b, head_before=last):
                    if head_before:
                        head_transposed(b - 1)
                    if not (isinstance(b, int) and b + 2 >= NBATCH):
                        aggregates(b + 2)
                    if head_before:
                        head(b - 1)
                    if not (isinstance(b, int) and b + 1 >= NBATCH):
                        outputs(b + 1)

                aggregates(0)
                aggregates(1)
                outputs(0)
                turn(0, False)
                with pe.Fori(0, NBATCH - 3) as b:
                    turn(b + 1)
                turn(NBATCH - 2)
                turn(NBATCH - 1)
                if last:
                    head_transposed(NBATCH - 1)
                    head(NBATCH - 1)

            for l in range(LAYERS):
                node_stage(l)
                edge_stage(l)
                output_stage(l)

        @block.scalar
        def _(act):
            copy = ACT.Copy

            def copied(dst_ap, k, done):
                act.activation(dst_ap, ps[:, k, 0:BN], copy).then_inc(done, 1)

            def node_stage(l):
                if l == 0:
                    act.wait_ge(s_emb_in, 16)
                act.wait_ge(s_emb, START + NBATCH * l)

                def batch_copied(b):
                    n = l * NBATCH + b
                    act.wait_ge(s_et, START + n)
                    act.activation(current[:, :, :], emb[:, ds(b * BT, BT), :], copy).then_inc(s_cur, 1)

                def transposes_copied(b):
                    n = l * NBATCH + b
                    act.wait_ge(s_et, START + n + 1)
                    act.wait_ge(s_kvq, START + n)
                    copied(emb_t[:, :], 0, s_etc)

                def typed_copied(b, u):
                    n = l * NBATCH + b
                    act.wait_ge(s_kvq, START + n + 1)
                    if l > 0 or b > 0:
                        act.wait_ge(s_tvc, START + (n - 1) * BT)
                    act.activation(kvq[u][:, :, :], ps[:, 0:BT, 0:3 * HID], copy).then_inc(s_kvqc, 1)

                def flipped_copied(b, u):
                    n = l * NBATCH + b
                    act.wait_ge(s_kt, n + 1)
                    if l > 0 or b > 0:
                        act.wait_ge(s_tv, START + (n - 1) * BT)
                    act.activation(kv_t[u][:, :, :], ps[:, 0:2, :], copy).then_inc(s_kvc, 1)

                def keys_copied(b, j):
                    n = l * NBATCH + b
                    act.wait_ge(s_tk, START + n * BT + j + 1)
                    if l > 0 or b > 0:
                        act.wait_ge(s_t_out[j], 16 * n)
                    lines_of = table_rows[j][:, 0:QUERY_AT].rearrange("p (r d) -> p r d", d=LINE)
                    act.activation(lines_of[:, :, 0:HID], ps[:, 4:6, :].rearrange("p a (r d) -> p (a r) d", d=HID), copy).then_inc(s_tkc, 1)

                def turn(b, u, more=True, more_after=True):
                    if more:
                        transposes_copied(b + 1)
                    if more_after:
                        batch_copied(b + 2)
                    keys_copied(b, 0)
                    if more:
                        typed_copied(b + 1, 1 - u)
                    keys_copied(b, 1)
                    keys_copied(b, 2)
                    if more:
                        flipped_copied(b + 1, 1 - u)
                    keys_copied(b, 3)

                batch_copied(0)
                transposes_copied(0)
                batch_copied(1)
                typed_copied(0, 0)
                flipped_copied(0, 0)
                if l == 0:
                    for b in range(NBATCH):
                        turn(b, b % 2, b + 1 < NBATCH, b + 2 < NBATCH)
                else:
                    with act.Fori(0, NBATCH // 2 - 1) as i:
                        for u in range(2):
                            turn(2 * i + u, u)
                    turn(NBATCH - 2, 0, True, False)
                    turn(NBATCH - 1, 1, False, False)

            def exponentials(l, g, u, first):
                G = l * GROUPS + g
                act.wait_ge(s_diff, G + 1)
                act.activation(prob[u], score[u], ACT.Exp).then_inc(s_prob, 1)
                act.wait_ge(s_max, G + 1)
                if not first:
                    act.wait_ge(s_mt, START + G)
                act.activation(max_wide, row_max[u].unsqueeze(3).broadcast_to([P, ROW_TILES, HEADS, HS]), copy).then_inc(s_maxw, 1)

            def factors(l, g):
                G = l * GROUPS + g
                act.wait_ge(s_fac_in, START + G + 1)
                act.activation(factor, factor, ACT.Exp).then_inc(s_fac, 1)

            def sums_widened(l, g, u, first):
                G = l * GROUPS + g
                act.wait_ge(s_den, G + 1)
                if not first:
                    act.wait_ge(s_ut, START + G)
                act.activation(den_wide, row_den[u].unsqueeze(3).broadcast_to([P, ROW_TILES, HEADS, HS]), copy).then_inc(s_denw, 1)

            def rows_stored(l, g, half, u):
                G = l * GROUPS + g
                act.wait_ge(s_back, START + G + 1)
                act.wait_ge(s_row_out[u], DMA_START + 16 * (l * part_uses(u) + half))
                act.activation(out_rows[u][:, :, 0:HID], ps[:, 6, :].rearrange("p (t d) -> p t d", t=ROW_TILES), copy)
                act.activation(out_rows[u][:, :, HID:OUT_LINE],
                               ps[:, 7, 0:ROW_TILES * HEADS].rearrange("p (t d) -> p t d", t=ROW_TILES), copy).then_inc(s_row, 1)
                act.wait_ge(s_row, START + G + 1)
                act.dma_start(row_table.rearrange("(g t p) c -> g p t c", t=ROW_TILES, p=P)[ds(g, 1)].rearrange("o p t c -> (o p) t c"),
                              out_rows[u][:, :, :]).then_inc(s_row_out[u], 16)

            def edge_stage(l):
                exponentials(l, 0, 0, True)
                sums_widened(l, 0, 0, True)
                factors(l, 0)
                exponentials(l, 1, 1, False)
                sums_widened(l, 1, 1, False)
                rows_stored(l, 0, 0, 0)
                with act.Fori(0, PAIRS - 1) as i:
                    for g, before_half, u in ((2 + 2 * i, i, 0), (3 + 2 * i, i + 1, 1)):
                        factors(l, g - 1)
                        exponentials(l, g, u, False)
                        sums_widened(l, g, u, False)
                        rows_stored(l, g - 1, before_half, 1 - u)
                factors(l, GROUPS - 2)
                exponentials(l, GROUPS - 1, 0, False)
                sums_widened(l, GROUPS - 1, 0, False)
                rows_stored(l, GROUPS - 2, PAIRS - 1, 1)
                factors(l, GROUPS - 1)
                rows_stored(l, GROUPS - 1, PAIRS, 0)

            def output_stage(l):
                last = l == LAYERS - 1
                act.wait_ge(s_late_in, 16 * 4 * (l + 1))
                act.activation(skip_sig[:, :], skip_sig[:, :], ACT.Sigmoid).then_inc(s_skip, 1)

                def aggregates(b):
                    n = l * NBATCH + b
                    act.wait_ge(s_at, START + n + 1)
                    act.wait_ge(s_y, START + n)
                    copied(emb_t[:, :], 0, s_atc)

                def gates(b):
                    n = l * NBATCH + b
                    act.wait_ge(s_y, START + n + 1)
                    act.wait_ge(s_yu, START + n)
                    act.activation(gate.rearrange("p t c -> p (t c)"), ps[:, 2, 0:BN], ACT.Sigmoid).then_inc(s_ye, 1)

                def head_copied(b):
                    act.wait_ge(s_ht, b + 1)
                    act.wait_ge(s_hy, START + b)
                    copied(head_t, 6, s_htc)

                def root_of_result(b):
                    act.wait_ge(s_var2, b + 1)
                    act.activation(stats[:, 3, :], stats[:, 2, :], ACT.Sqrt).then_inc(s_sd2, 1)

                def turn(b, head_before=last):
                    if head_before:
                        head_copied(b - 1)
                    gates(b)
                    if not (isinstance(b, int) and b + 2 >= NBATCH):
                        aggregates(b + 2)
                    if head_before:
                        root_of_result(b - 1)
                    act.wait_ge(s_var, l * NBATCH + b + 1)
                    act.activation(stats[:, 3, :], stats[:, 2, :], ACT.Sqrt).then_inc(s_sd, 1)

                aggregates(0)
                aggregates(1)
                turn(0, False)
                with act.Fori(0, NBATCH - 3) as b:
                    turn(b + 1)
                turn(NBATCH - 2)
                turn(NBATCH - 1)
                if last:
                    head_copied(NBATCH - 1)
                    root_of_result(NBATCH - 1)

            for l in range(LAYERS):
                node_stage(l)
                edge_stage(l)
                output_stage(l)

        @block.vector
        def _(dve):
            own = Steps(dve, s_dve)
            chained = own.chained

            def blocks4(ap):
                return ap.rearrange("p (b k) -> p b k", k=EB)

            dve.memset(type_i, -1.0).then_inc(s_clear, 1)
            chained(dve.memset(pad_fill, 0.0))
            dve.memset(pad_fill_int[:, HID:HID + 1], NODES).then_inc(s_pads, 1)
            dve.memset(zeros[:, :], 0.0).then_inc(s_zeros, 1)
            dve.memset(rel_mats[:, :, :, :], 0.0).then_inc(s_rel, 1)
            dve.wait_ge(s_types_in, 32)
            chained(dve.tensor_copy(type_f, type_i))
            dve.wait_ge(s_const, N_CONST)
            dve.tensor_tensor(hot, type_f.unsqueeze(1).broadcast_to([P, TYPES, ST]), index_iota[:, 0:TYPES].unsqueeze(2).broadcast_to([P, TYPES, ST]),
                              ALU.is_equal).then_inc(s_hot_types, 1)
            dve.tensor_copy(x_nodes_int[:, :, HID], node_iota[:, :]).then_inc(s_pads, 1)
            in_tile, in_tiles, ahead_of, running = sums
            of_all, tiles_of, first_tile, base = of_type
            flat = [v.rearrange("p k t -> p (k t)") for v in (in_tiles, running)]
            dve.wait_ge(s_type_sums, 1)
            chained(dve.tensor_copy(in_tiles, ps[:, 1, TYPES * ST:2 * TYPES * ST].rearrange("p (k t) -> p k t", t=ST)))
            chained(dve.tensor_tensor_scan(flat[1], flat[0], flat[0], 0.0, ALU.add, ALU.max))
            chained(dve.tensor_tensor(ahead_of, running, in_tiles, ALU.subtract))
            chained(dve.tensor_tensor(of_all, running[:, :, ST - 1], ahead_of[:, :, 0], ALU.subtract))
            chained(dve.tensor_scalar(of_type_i, of_all, float(P - 1), None, ALU.add))
            chained(dve.tensor_single_scalar(of_type_i, of_type_i, P.bit_length() - 1, ALU.arith_shift_right))
            chained(dve.tensor_copy(tiles_of, of_type_i))
            chained(dve.tensor_tensor_scan(first_tile, tiles_of, tiles_of, 0.0, ALU.add, ALU.max))
            chained(dve.tensor_tensor(first_tile, first_tile, tiles_of, ALU.subtract))
            own.step(dve.scalar_tensor_tensor(out=base, in0=first_tile, scalar=float(P), in1=ahead_of[:, :, 0], op0=ALU.mult, op1=ALU.subtract))
            chained(dve.tensor_tensor(in_tile, ahead_of, ps[:, 1, 0:TYPES * ST].rearrange("p (k t) -> p k t", t=ST), ALU.add))
            chained(dve.tensor_tensor(in_tile, in_tile, base.unsqueeze(2).broadcast_to([P, TYPES, ST]), ALU.add))
            chained(dve.tensor_tensor(in_tile, in_tile, hot, ALU.mult))
            chained(dve.tensor_reduce(type_f, in_tile.rearrange("p k t -> p t k"), AX.X, ALU.add))
            dve.tensor_copy(slot_of[:, :], type_f).then_inc(s_slot, 1)
            chained(dve.tensor_tensor(from_type, index_iota[:, :].unsqueeze(1).broadcast_to([P, TYPES - 1, TILES_N]),
                                      first_tile[:, 1:TYPES].unsqueeze(2).broadcast_to([P, TYPES - 1, TILES_N]), ALU.is_ge))
            chained(dve.tensor_reduce(tile_type_f[:, :], from_type.rearrange("p k t -> p t k"), AX.X, ALU.add))
            own.step(dve.tensor_copy(tile_type[:, :], tile_type_f[0:1, :]))
            dve.wait_ge(s_dst_in, 16)
            samples = dst_i.rearrange("p (j e) -> p j e", e=CHUNK)[:, :, 0]
            own.step(dve.tensor_single_scalar(digits_i[:, 0, :], samples, P.bit_length() - 1, ALU.logical_shift_right))
            own.step(dve.tensor_single_scalar(digits_i[:, 1, :], samples, P - 1, ALU.bitwise_and))
            own.wait()
            chained(dve.tensor_copy(digits, digits_i))
            dve.wait_ge(s_const, N_CONST)
            def against(out, k, iota, n, op):
                return dve.tensor_tensor(out, iota[0:EP, :].unsqueeze(1).broadcast_to([EP, SAMPLES, n]),
                                         digits[:, k, :].unsqueeze(2).broadcast_to([EP, SAMPLES, n]), op)
            against(lo_above, 1, iota_lo, P, ALU.is_gt)
            against(hi_here, 0, iota_hi, ST, ALU.is_equal)
            against(hi_above, 0, iota_hi, ST, ALU.is_gt).then_inc(s_hot, 1)
            chunk, later, end, first_block, last_block, some, span, rows, ahead, row_start = (counts[:, k, :] for k in range(10))
            dve.wait_ge(s_pe_idx, 1)
            chained(dve.tensor_scalar(chunk, ps[:, 0, 0:ST], -1.0, 0.0, ALU.add, ALU.max))
            dve.tensor_copy(chunk_i[:, :], chunk).then_inc(s_chunk, 1)
            dve.wait_ge(s_edges_in, 32)
            dve.scalar_tensor_tensor(out=blk[:, :, 0:EB], in0=blocks4(src_i), scalar=float(NODE_LINES), in1=blocks4(ety_i),
                                     op0=ALU.mult, op1=ALU.add).then_inc(s_blocks_ready, 1)
            dve.tensor_copy(blk[:, :, EB:2 * EB], blocks4(dst_i)).then_inc(s_blocks_ready, 1)
            by_run = row_out[:, 2, :].rearrange("p (q k) -> p q k", k=RUN)

            def nodes_indexed():
                dve.wait_ge(s_chunk_in, 16 * ST)
                chained(dve.tensor_tensor(starts_later, node_iota[:, :].unsqueeze(2).broadcast_to([P, ST, CHUNK]), chunk_dst, ALU.is_gt))
                own.step(dve.memset(start_of[:, ST:ST + 1], float(EDGES)))
                chained(dve.tensor_reduce(later, starts_later, AX.X, ALU.add))
                dve.scalar_tensor_tensor(out=start_of[:, 0:ST], in0=chunk, scalar=float(CHUNK), in1=later, op0=ALU.mult, op1=ALU.add).then_inc(s_idx_vec, 1)
                dve.wait_ge(s_idx_vec, 1)
                own.step(dve.tensor_copy(counts_int[:, 0, :], start_of[:, 0:ST]))
                dve.wait_ge(s_pe_idx, 2)
                chained(dve.tensor_copy(end, ps[:, 0, 0:ST]))
                own.step(dve.tensor_scalar(counts_int[:, 1, :], end, -1.0, None, ALU.add))
                chained(dve.tensor_tensor(some, end, start_of[:, 0:ST], ALU.is_gt))
                chained(dve.tensor_single_scalar(counts_int[:, 0:2, :], counts_int[:, 0:2, :], EB.bit_length() - 1, ALU.arith_shift_right))
                chained(dve.tensor_copy(counts[:, 3:5, :], counts_int[:, 0:2, :]))
                chained(dve.tensor_tensor(span, last_block, first_block, ALU.subtract))
                chained(dve.tensor_tensor(span, span, some, ALU.mult))
                dve.tensor_scalar(rows, span, 1.0, None, ALU.add).then_inc(s_idx_vec, 1)
                dve.wait_ge(s_pe_idx, 3)
                chained(dve.tensor_copy(later, ps[:, 0, ST:2 * ST]))
                chained(dve.tensor_tensor_scan(ahead, later, later, 0.0, ALU.add, ALU.max))
                chained(dve.tensor_tensor(ahead, ahead, later, ALU.subtract))
                chained(dve.tensor_tensor(row_start, ahead, ps[:, 0, 0:ST], ALU.add))
                dve.tensor_copy(info_pack[:, :, 0], row_start).then_inc(s_info_ready, 1)
                dve.tensor_scalar(info_pack[:, :, 1], node_iota[:, :], 1.0, None, ALU.add).then_inc(s_info_ready, 1)
                dve.tensor_tensor(info_pack[:, :, 2], row_start, first_block, ALU.subtract).then_inc(s_info_ready, 1)
                dve.tensor_tensor(info_pack[:, :, 3], row_start, span, ALU.add).then_inc(s_info_ready, 1)

            def rows_indexed():
                dve.wait_ge(s_marks_in, 16)
                chained(dve.tensor_copy(mark, mark_i.rearrange("p r c -> p c r")))
                for k in range(2):
                    own.step(dve.tensor_tensor_scan(held[:, k, :], mark[:, k, :], mark[:, k, :], 0.0, ALU.max, ALU.max))
                own.wait()
                dve.tensor_copy(last_col, held[:, :, RC - 1]).then_inc(s_idx_vec, 1)
                chained(dve.memset(last_row, 0.0))
                dve.wait_ge(s_pe_idx, 4)
                chained(dve.tensor_copy(last_row[:, 1:P + 1], ps[0:2, 0, 0:P]))
                dve.tensor_tensor_scan(prior_row, last_row[:, 0:P], last_row[:, 0:P], 0.0, ALU.max, ALU.max).then_inc(s_idx_vec, 1)
                dve.wait_ge(s_pe_idx, 5)
                chained(dve.tensor_copy(prior_col, ps[:, 1, 0:2]))
                for k in range(2):
                    own.step(dve.tensor_scalar(held[:, k, :], held[:, k, :], prior_col[:, k:k + 1], None, ALU.max))
                own.wait()
                dve.tensor_scalar(row_out[:, 0, :], held[:, 0, :], -1.0, None, ALU.add).then_inc(s_rows_ready, 1)
                dve.tensor_scalar(row_out[:, 1, :], mark[:, 0, :], 0.0, RESET, ALU.is_gt, ALU.mult).then_inc(s_rows_ready, 1)
                chained(dve.tensor_tensor(row_out[:, 2, :], row_iota[:, :], held[:, 1, :], ALU.subtract))
                chained(dve.tensor_scalar(row_out[:, 2, :], row_out[:, 2, :], float(BLOCKS - 1), None, ALU.min))
                dve.tensor_copy(run_idx[:, :], by_run[:, :, 0]).then_inc(s_run_idx, 1)
                dve.tensor_copy(node_int, row_out[:, 0, :]).then_inc(s_rows_ready, 1)

            def rows_tiled():
                dve.wait_ge(s_pe_idx, 6)
                dve.tensor_copy(node_of[:, :], ps[:, 0, 0:TILES]).then_inc(s_bases, 1)
                dve.tensor_scalar(tile_base[:, :], ps[:, 1, 0:TILES], part_index[:, 0:1], None, ALU.add).then_inc(s_bases, 1)

            def lines_chosen(m):
                if m == 0:
                    own.step(dve.tensor_tensor(run_off[:, 0, :, :], by_run[:, :, 1:RUN], by_run[:, :, 0:1].broadcast_to([P, RUNS, RUN - 1]), ALU.subtract))
                    dve.wait_ge(s_run_in, 16 * RUNS)
                    own.step(dve.tensor_tensor(run_steps, run_in[:, :, 1:RUN, :], run_in[:, :, 0:RUN - 1, :], ALU.subtract))
                    own.step(dve.tensor_copy(chosen, run_in[:, :, 0:1, :].broadcast_to([P, RUNS, RUN, FIELDS])))
                    own.wait()
                    return
                n = RUN - m
                chained(dve.tensor_scalar(run_off[:, 1, :, 0:n], run_off[:, 0, :, m - 1:RUN - 1], float(m), None, ALU.is_ge))
                chained(dve.tensor_tensor(run_part[:, :, 0:n, :], run_steps[:, :, m - 1:m, :].broadcast_to([P, RUNS, n, FIELDS]),
                                          run_off[:, 1, :, 0:n].unsqueeze(3).broadcast_to([P, RUNS, n, FIELDS]), ALU.mult))
                own_block = dve.tensor_tensor(chosen[:, :, m:RUN, :], chosen[:, :, m:RUN, :], run_part[:, :, 0:n, :], ALU.add)
                if m < RUN - 1:
                    chained(own_block)
                else:
                    own_block.then_inc(s_chosen, 1)

            def lines_tiled():
                dve.wait_ge(s_pe_idx, 7)
                dve.wait_ge(s_bases, 2)
                by_slot = [t[:, :].rearrange("p (t k f) -> p k f t", k=EB // 2, f=2) for t in (codes, limit)]
                for k in range(EB // 2):
                    own.step(dve.tensor_copy(by_slot[0][:, k, :, :], ps[:, 2 + k, 0:2 * TILES].rearrange("p (f t) -> p f t", f=2)))
                    own.step(dve.tensor_tensor(by_slot[1][:, k, :, :], ps[:, 2 + EB // 2 + k, 0:2 * TILES].rearrange("p (f t) -> p f t", f=2),
                                               node_of[:, :].unsqueeze(1).broadcast_to([P, 2, TILES]), ALU.is_equal))
                own.wait()
                dve.tensor_scalar(limit[:, :], limit[:, :], 2 * OFF, -OFF, ALU.mult, ALU.add).then_inc(s_codes, 1)
                dve.wait_ge(s_codes, 1)

            def node_stage(l):
                dve.wait_ge(s_weights_in, 16 * NODE_LOADS * (l + 1))
                chained(dve.tensor_scalar(pri_scale[:, :], pri_scale[:, :], float(HS) ** -0.5, None, ALU.mult))
                dve.tensor_tensor(rel_mats[:, 0, :, :], rel_mats[:, 0, :, :],
                                  pri_scale[:, :].unsqueeze(2).broadcast_to([P, RELS, HID]), ALU.mult).then_inc(s_rel, 1)

                def turn(b, u):
                    n = l * NBATCH + b
                    for j in range(BT):
                        if j == 0:
                            dve.wait_ge(s_kvqc, START + n + 1)
                        if l > 0 or b > 0:
                            dve.wait_ge(s_t_out[j], 16 * n)
                        dve.tensor_copy(table_rows[j][:, QUERY_AT:NODE_WIDTH], kvq[u][:, j, 2 * HID:3 * HID])
                        dve.wait_ge(s_tv, START + n * BT + j + 1)
                        lines_of = table_rows[j][:, 0:QUERY_AT].rearrange("p (r d) -> p r d", d=LINE)
                        dve.tensor_copy(lines_of[:, :, HID:LINE], ps[:, 6:8, :].rearrange("p a (r d) -> p (a r) d", d=HID)).then_inc(s_tvc, 1)
                        if l == 0 and 0 <= b * BT + j - CHOSEN_FROM < RUN:
                            lines_chosen(b * BT + j - CHOSEN_FROM)

                if l == 0:
                    dve.wait_ge(s_emb_in, 16)
                    numbers = emb_all[:, :, HID].bitcast(I32)
                    chained(dve.tensor_scalar(alpha_part[:, :], numbers, float(NODES), None, ALU.is_ge))
                    chained(dve.tensor_tensor(alpha_part[:, :], alpha_part[:, :], slot_iota[:, :], ALU.mult))
                    dve.tensor_tensor(slot_node[:, :], alpha_part[:, :], numbers, ALU.add).then_inc(s_slot_node, 1)
                    for b in range(NBATCH):
                        turn(b, b % 2)
                        if b == 0:
                            nodes_indexed()
                        if b == 2:
                            rows_indexed()
                        if b == 3:
                            rows_tiled()
                    lines_tiled()
                else:
                    with dve.Fori(0, NBATCH // 2) as i:
                        for u in range(2):
                            turn(2 * i + u, u)

            def spreads(l, g, half, u):
                G = l * GROUPS + g
                dve.wait_ge(s_node_in[u], 16 * (l * part_uses(u) + half + 1))
                dve.wait_ge(s_rq, START + G)
                for t in range(ROW_TILES):
                    ins = dve.tensor_scalar(spread[:, t, :], row_info[u][:, 0, t * P:(t + 1) * P],
                                            tile_base[:, ds(g * ROW_TILES + t, 1)], None, ALU.is_equal)
                ins.then_inc(s_spread, 1)

            def scores(l, g, half, u):
                G = l * GROUPS + g
                keys = lines[:, u, :, 0:HID]
                dve.wait_ge(s_kv_in[u], 16 * SLOTS * (l * part_uses(u) + half + 1))
                dve.wait_ge(s_rq, START + G + 1)
                dve.tensor_tensor(keys.rearrange("p (t k) d -> p t k d", k=EB), keys.rearrange("p (t k) d -> p t k d", k=EB),
                                  ps[:, 0, :].rearrange("p (t d) -> p t d", d=HID).unsqueeze(2).broadcast_to([P, ROW_TILES, EB, HID]),
                                  ALU.mult).then_inc(s_prod, 1)
                dve.wait_ge(s_prod, START + G + 1)
                flat = score[u].rearrange("p t k h -> p (t k) h")
                dve.tensor_reduce(flat, keys.rearrange("p s (h c) -> p s h c", c=HS), AX.X, ALU.add).then_inc(s_sum, 1)
                dve.wait_ge(s_sum, G + 1)
                dve.tensor_tensor(flat, flat, limit[:, ds(g * SLOTS, SLOTS)].unsqueeze(2).broadcast_to([P, SLOTS, HEADS]),
                                  ALU.min).then_inc(s_lim, 1)
                dve.wait_ge(s_lim, G + 1)
                dve.tensor_reduce(row_max[u], score[u].rearrange("p t k h -> p t h k"), AX.X, ALU.max).then_inc(s_mx, 1)
                dve.wait_ge(s_mx, G + 1)
                dve.tensor_scalar(row_max[u], row_max[u], FLOOR, None, ALU.max).then_inc(s_max, 1)
                dve.wait_ge(s_max, G + 1)
                dve.tensor_tensor(score[u], score[u], row_max[u].unsqueeze(2).broadcast_to([P, ROW_TILES, EB, HEADS]),
                                  ALU.subtract).then_inc(s_diff, 1)

            def running_max(l, g, half, u, first):
                G = l * GROUPS + g
                peak = run_max[u]
                dve.wait_ge(s_mt, START + G + 1)
                dve.wait_ge(s_reset_in[u], 16 * (l * part_uses(u) + half + 1))
                if first:
                    dve.memset(peak[:, 0:1], 0.0).then_inc(s_run, 1)
                    dve.tensor_tensor_scan(peak[:, 1:GR + 1], row_info[u][:, 1, :], ps[:, 5, :], 0.0, ALU.add, ALU.max).then_inc(s_run, 1)
                else:
                    dve.wait_ge(s_run, 2 * G)
                    dve.tensor_copy(peak[:, 0:1], run_max[1 - u][:, GR:GR + 1]).then_inc(s_run, 1)
                    dve.tensor_tensor_scan(peak[:, 1:GR + 1], row_info[u][:, 1, :], ps[:, 5, :], run_max[1 - u][:, GR:GR + 1],
                                           ALU.add, ALU.max).then_inc(s_run, 1)
                dve.wait_ge(s_run, 2 * G + 2)
                dve.wait_ge(s_sums, START + 2 * G)
                dve.tensor_tensor(factor[:, 0, :], peak[:, 0:GR], row_info[u][:, 1, :], ALU.add).then_inc(s_grow, 1)
                dve.tensor_tensor(factor[:, 1, :], ps[:, 5, :], peak[:, 1:GR + 1], ALU.subtract)
                dve.wait_ge(s_grow, G + 1)
                dve.tensor_tensor(factor[:, 0, :], factor[:, 0, :], peak[:, 1:GR + 1], ALU.subtract).then_inc(s_fac_in, 1)

            def weighted(l, g, u):
                G = l * GROUPS + g
                dve.wait_ge(s_prob, G + 1)
                dve.tensor_reduce(row_den[u], prob[u].rearrange("p t k h -> p t h k"), AX.X, ALU.add).then_inc(s_den, 1)
                for half in range(2):
                    part = slice(half * SLOTS // 2, (half + 1) * SLOTS // 2)
                    values = lines[:, u, part, HID:LINE].rearrange("p s (h c) -> p s h c", c=HS)
                    dve.tensor_tensor(values, values, prob[u].rearrange("p t k h -> p (t k) h")[:, part, :].unsqueeze(3)
                                      .broadcast_to([P, SLOTS // 2, HEADS, HS]), ALU.mult).then_inc(s_pv, 1)

            def running_sums(l, g, u, first):
                G = l * GROUPS + g
                dve.wait_ge(s_fac, G + 1)
                dve.wait_ge(s_ut, START + G + 1)
                dve.tensor_tensor(scaled, ps[:, 1 + 2 * u:3 + 2 * u, :], factor[:, 1:2, :].broadcast_to([P, 2, GR]), ALU.mult).then_inc(s_scaled, 1)
                dve.wait_ge(s_scaled, START + G + 1)
                if not first:
                    dve.wait_ge(s_back, START + G - 1)
                    dve.wait_ge(s_sums, START + 2 * G)
                for k in range(2):
                    dve.tensor_tensor_scan(run_sum[u][:, k, :], factor[:, 0, :], scaled[:, k, :],
                                           0.0 if first else run_sum[1 - u][:, k, GR - 1:GR], ALU.mult, ALU.add).then_inc(s_sums, 1)

            def edge_stage(l):
                def turn(g, half, u):
                    spreads(l, g, half, u)
                    weighted(l, g - 1, 1 - u)
                    running_sums(l, g - 2, u, False)
                    running_max(l, g - 1, half - 1 + u, 1 - u, False)
                    scores(l, g, half, u)

                spreads(l, 0, 0, 0)
                scores(l, 0, 0, 0)
                spreads(l, 1, 0, 1)
                weighted(l, 0, 0)
                running_max(l, 0, 0, 0, True)
                scores(l, 1, 0, 1)
                spreads(l, 2, 1, 0)
                weighted(l, 1, 1)
                running_sums(l, 0, 0, True)
                running_max(l, 1, 0, 1, False)
                scores(l, 2, 1, 0)
                with dve.Fori(0, PAIRS - 1) as i:
                    turn(3 + 2 * i, i + 1, 1)
                    turn(4 + 2 * i, i + 2, 0)
                weighted(l, GROUPS - 1, 0)
                running_sums(l, GROUPS - 2, 1, False)
                running_max(l, GROUPS - 1, PAIRS, 0, False)
                running_sums(l, GROUPS - 1, 0, False)

            def mean_free(t, inv):
                def per_tile(k):
                    return stats[:, k, :].unsqueeze(2).broadcast_to([P, BT, HID])
                chained(dve.tensor_reduce(stats[:, 0, :], t, AX.X, ALU.add))
                chained(dve.tensor_scalar(stats[:, 0, :], stats[:, 0, :], 1.0 / HID, None, ALU.mult))
                chained(dve.tensor_tensor(t, t, per_tile(0), ALU.subtract))
                chained(dve.tensor_tensor(squares, t, t, ALU.mult))
                chained(dve.tensor_reduce(stats[:, 1, :], squares, AX.X, ALU.add))
                dve.tensor_scalar(stats[:, 2, :], stats[:, 1, :], 1.0 / HID, EPS, ALU.mult, ALU.add).then_inc(inv, 1)

            def output_stage(l):
                last = l == LAYERS - 1
                dve.wait_ge(s_skip, l + 1)
                dve.wait_ge(s_small_in, 32)
                chained(dve.tensor_scalar(alpha[:, :], tile_type_f[:, :], 0.0, skip_sig[:, 0:1], ALU.is_equal, ALU.mult))
                for t in range(1, TYPES):
                    chained(dve.tensor_scalar(alpha_part[:, :], tile_type_f[:, :], float(t), skip_sig[:, t:t + 1], ALU.is_equal, ALU.mult))
                    chained(dve.tensor_tensor(alpha[:, :], alpha[:, :], alpha_part[:, :], ALU.add))

                def aggregates(b):
                    n = l * NBATCH + b
                    dve.wait_ge(s_lr_in, 16 * BT * (n + 1))
                    chained(dve.tensor_scalar(den_inv, last_rows[:, :, HID:OUT_LINE], 1e-16, None, ALU.add))
                    chained(dve.reciprocal(den_inv, den_inv))
                    dve.wait_ge(s_at, START + n)
                    for j in range(BT):
                        ins = dve.tensor_tensor(agg[:, j, :].rearrange("p (h c) -> p h c", c=HS), last_rows[:, j, 0:HID].rearrange("p (h c) -> p h c", c=HS),
                                                den_inv[:, j, :].unsqueeze(2).broadcast_to([P, HEADS, HS]), ALU.mult)
                    ins.then_inc(s_ag, 1)

                def result_of(b):
                    dve.wait_ge(s_hy, START + b + 1)
                    if not isinstance(b, int) or b > 0:
                        dve.wait_ge(s_out, 16 * BT * b)
                    h_ps = ps[:, 4, 0:BN].rearrange("p (t c) -> p t c", t=BT)
                    dve.tensor_tensor(result, h_ps, bff_row[:, :].unsqueeze(1).broadcast_to([P, BT, HID]), ALU.add).then_inc(s_hu, 1)
                    dve.wait_ge(s_hu, START + b + 1)
                    dve.wait_ge(s_xa, 16 * (b + 1))
                    chained(dve.tensor_tensor(result, result, x_again, ALU.add))
                    mean_free(result, s_var2)
                    dve.wait_ge(s_sd2, b + 1)
                    chained(dve.reciprocal(stats[:, 3, :], stats[:, 3, :]))
                    dve.tensor_tensor(result, result, stats[:, 3, :].unsqueeze(2).broadcast_to([P, BT, HID]), ALU.mult).then_inc(s_res, 1)

                def turn(b, head_before=last):
                    n = l * NBATCH + b
                    rows_now = emb[:, ds(b * BT, BT), :]
                    dve.wait_ge(s_ye, n + 1)
                    dve.wait_ge(s_emb, START + n)
                    y_ps = ps[:, 2, 0:BN].rearrange("p (t c) -> p t c", t=BT)
                    dve.tensor_tensor(mixed, y_ps, gate, ALU.mult).then_inc(s_yu, 1)
                    dve.wait_ge(s_yu, START + n + 1)
                    if not (isinstance(b, int) and b + 2 >= NBATCH):
                        aggregates(b + 2)
                    if head_before:
                        result_of(b - 1)
                    chained(dve.tensor_tensor(mixed, mixed, rows_now, ALU.subtract))
                    chained(dve.tensor_tensor(mixed, mixed, alpha[:, ds(b * BT, BT)].unsqueeze(2).broadcast_to([P, BT, HID]), ALU.mult))
                    chained(dve.tensor_tensor(mixed, mixed, rows_now, ALU.add))
                    mean_free(mixed, s_var)
                    dve.wait_ge(s_sd, n + 1)
                    chained(dve.reciprocal(stats[:, 3, :], stats[:, 3, :]))
                    chained(dve.tensor_tensor(mixed, mixed, stats[:, 3, :].unsqueeze(2).broadcast_to([P, BT, HID]), ALU.mult))
                    dve.tensor_tensor(mixed, mixed, gain[:, :].unsqueeze(1).broadcast_to([P, BT, HID]), ALU.mult).then_inc(s_gain, 1)
                    dve.wait_ge(s_gain, n + 1)
                    if head_before:
                        dve.wait_ge(s_ht, b)
                    dve.tensor_tensor(current[:, :, :] if last else rows_now, mixed, shift[:, :].unsqueeze(1).broadcast_to([P, BT, HID]), ALU.add).then_inc(s_emb, 1)

                aggregates(0)
                aggregates(1)
                turn(0, False)
                turn(1)
                with own.loop(NBATCH - 4, 19 if last else 12) as b:
                    turn(b + 2)
                turn(NBATCH - 2)
                turn(NBATCH - 1)
                if last:
                    result_of(NBATCH - 1)

            for l in range(LAYERS):
                node_stage(l)
                edge_stage(l)
                output_stage(l)


_INS = ["x", "src", "dst", "edge_type_8", "node_type_8", "L0_gnn_Wk", "L0_gnn_Wq", "L0_gnn_Wv", "L0_gnn_Wa", "L0_gnn_pri",
        "L0_gnn_Watt", "L0_gnn_Wmsg", "L0_gnn_skip", "L0_gnn_ln_g", "L0_gnn_ln_b", "L0_gnn_Wff", "L0_gnn_bff"]


def kernel(**inputs):
    import concourse.bacc as _bacc
    from concourse.bass_utils import run_bass_kernel_spmd as _run

    nc = _bacc.Bacc("TRN2", target_bir_lowering=False, num_devices=1)
    arrays, args = {}, []
    for name in _INS:
        a = np.ascontiguousarray(inputs[name])
        arrays[f"in_{name}"] = a
        args.append(nc.dram_tensor(f"in_{name}", a.shape, mybir.dt.from_np(a.dtype), kind="ExternalInput").ap())
    args.append(nc.dram_tensor("out_nodes", (NODES, HID), F32, kind="ExternalOutput").ap())
    build(nc, *args)
    return _run(nc, [arrays], core_ids=[0]).results[0]["out_nodes"]
```
